# Optimizing a Trainium2 kernel written in Bass

```python
import numpy as np
import jax
import jax.numpy as jnp

def _softmax(x, axis=-1):
    return jax.nn.softmax(x, axis=axis)

def _gelu(x):
    return jax.nn.gelu(x, approximate=True)

def _silu(x):
    return jax.nn.silu(x)

def _sigmoid(x):
    return jax.nn.sigmoid(x)

def _layernorm(x, axis=-1, eps=1e-05):
    m = jnp.mean(x, axis=axis, keepdims=True)
    v = jnp.var(x, axis=axis, keepdims=True)
    return (x - m) / jnp.sqrt(v + eps)

def _scatter_add(tgt, idx, src, axis=0):
    return tgt.at[idx].add(src)

def _segment_sum(src, seg, n):
    return jax.ops.segment_sum(src, seg, n)
kernel_name = 'mk_cond_seq_d4_seqx_r8_79cba3'

def setup_inputs(seed: int=0):
    np.random.seed(seed)
    _w = jnp.asarray

    def _rec_inputs():
        import jax
        import jax.numpy as jnp
        _rk = jax.random.key(seed)
        x = -0.0003482 + 1 * jax.random.normal(jax.random.fold_in(_rk, 1), (32, 128, 144), jnp.float32)
        _lenS = 128 - jax.random.randint(jax.random.fold_in(_rk, 7), (32,), 0, max(1, 128 // 4) + 1, jnp.int32)
        _lenS2 = 128 - jax.random.randint(jax.random.fold_in(_rk, 8), (32,), 0, max(1, 128 // 4) + 1, jnp.int32)
        cond_1152 = 0.00257642 + 1.0011 * jax.random.normal(jax.random.fold_in(_rk, 11), (32, 144), jnp.float32)
        return (x, cond_1152)
    x, cond_1152 = _rec_inputs()

    def _L0_cond_setup():
        import jax, jax.numpy as jnp
        import numpy as np
        from jax.scipy.linalg import expm
        N, D, COND_DIM = (144, 64, 144)
        B, T = (16, 128)

        def _rotation(cond, W, b):
            v = jax.nn.silu(cond) @ W.T + b
            iu, ju = jnp.triu_indices(D, k=1)
            A = jnp.zeros((cond.shape[0], D, D), dtype=v.dtype)
            A = A.at[:, iu, ju].set(v).at[:, ju, iu].set(-v)
            return expm(A)
        key = jax.random.key(seed)
        k1, k2, k3, k4, k5 = jax.random.split(key, 5)
        x = jax.random.normal(k1, (B, T, N), dtype=jnp.float32)
        cond = jax.random.normal(k2, (B, COND_DIM), dtype=jnp.float32)
        P = jax.random.normal(k3, (N, D), dtype=jnp.float32)
        n_skew = D * (D - 1) // 2
        bound = 1.0 / np.sqrt(COND_DIM)
        W = jax.random.uniform(k4, (n_skew, COND_DIM), minval=-bound, maxval=bound, dtype=jnp.float32)
        b = jax.random.uniform(k5, (n_skew,), minval=-bound, maxval=bound, dtype=jnp.float32)
        return {'x': x, 'cond': cond, 'P': P, 'W': W, 'b': b}
    _L0_cond_all = _L0_cond_setup()
    _L0_cond_in = {k: v for k, v in _L0_cond_all.items() if k in ('P', 'W', 'b')}
    del _L0_cond_all

    def _L1_cond_setup():
        import jax, jax.numpy as jnp
        import numpy as np
        N, T, D, H = (32, 128, 144, 16)
        DH = D // H
        MLP = int(D * 4.0)
        EPS = 1e-06

        def _layernorm(x):
            m = jnp.mean(x, axis=-1, keepdims=True)
            v = jnp.var(x, axis=-1, keepdims=True)
            return (x - m) * jax.lax.rsqrt(v + EPS)

        def _modulate(x, shift, scale):
            return x * (1.0 + scale[:, None, :]) + shift[:, None, :]

        def _attention(x, qkv_w, qkv_b, proj_w, proj_b):
            n, t, d = x.shape
            scale = DH ** (-0.5)
            qkv = x @ qkv_w + qkv_b
            qkv = qkv.reshape(n, t, 3, H, DH)
            q, k, v = (qkv[:, :, 0], qkv[:, :, 1], qkv[:, :, 2])
            attn = jnp.einsum('nthd,ntkd->nthk', q * scale, k)
            attn = jax.nn.softmax(attn, axis=-1)
            out = jnp.einsum('nthk,ntkd->nthd', attn, v)
            out = out.transpose(0, 2, 1, 3).reshape(n, t, d)
            return out @ proj_w + proj_b

        def _mlp(x, fc1_w, fc1_b, fc2_w, fc2_b):
            h = jax.nn.gelu(x @ fc1_w + fc1_b, approximate=False)
            return h @ fc2_w + fc2_b
        key = jax.random.key(seed)
        ks = jax.random.split(key, 14)
        s = 0.02
        return {'x': jax.random.normal(ks[0], (N, T, D), jnp.float32), 'c': jax.random.normal(ks[1], (N, D), jnp.float32), 'qkv_w': jax.random.normal(ks[2], (D, 3 * D), jnp.float32) * s, 'qkv_b': jax.random.normal(ks[3], (3 * D,), jnp.float32) * s, 'proj_w': jax.random.normal(ks[4], (D, D), jnp.float32) * s, 'proj_b': jax.random.normal(ks[5], (D,), jnp.float32) * s, 'fc1_w': jax.random.normal(ks[6], (D, MLP), jnp.float32) * s, 'fc1_b': jax.random.normal(ks[7], (MLP,), jnp.float32) * s, 'fc2_w': jax.random.normal(ks[8], (MLP, D), jnp.float32) * s, 'fc2_b': jax.random.normal(ks[9], (D,), jnp.float32) * s, 'ada_w': jax.random.normal(ks[10], (D, 6 * D), jnp.float32) * s, 'ada_b': jax.random.normal(ks[11], (6 * D,), jnp.float32) * s}
    _L1_cond_all = _L1_cond_setup()
    _L1_cond_in = {k: v for k, v in _L1_cond_all.items() if k in ('qkv_w', 'qkv_b', 'proj_w', 'proj_b', 'fc1_w', 'fc1_b', 'fc2_w', 'fc2_b', 'ada_w', 'ada_b')}
    del _L1_cond_all

    def _L2_cond_setup():
        import jax, jax.numpy as jnp
        import numpy as np
        DIM = 144
        HEADS = 16
        HEAD_DIM = DIM // HEADS
        HIDDEN = int(DIM * 4.0)
        EPS = 1e-12

        def rmsnorm(x, g, d):
            n = jnp.linalg.norm(x, axis=-1, keepdims=True)
            return x / jnp.maximum(n, EPS) * d ** 0.5 * g

        def modulate(x, scale, shift):
            return x * (1.0 + scale[:, None, :]) + shift[:, None, :]
        key = jax.random.key(seed)
        ks = jax.random.split(key, 12)
        B, N = (8, 128)
        s = 0.02
        return {'x': jax.random.normal(ks[0], (B, N, DIM), jnp.float32), 'c': jax.random.normal(ks[1], (B, DIM), jnp.float32), 'g1': jnp.ones((1,), jnp.float32), 'g2': jnp.ones((1,), jnp.float32), 'qkv_w': jax.random.normal(ks[2], (3 * DIM, DIM), jnp.float32) * s, 'qkv_b': jnp.zeros((3 * DIM,), jnp.float32), 'qg': jnp.ones((1,), jnp.float32), 'kg': jnp.ones((1,), jnp.float32), 'proj_w': jax.random.normal(ks[3], (DIM, DIM), jnp.float32) * s, 'proj_b': jnp.zeros((DIM,), jnp.float32), 'fc1_w': jax.random.normal(ks[4], (HIDDEN, DIM), jnp.float32) * s, 'fc1_b': jnp.zeros((HIDDEN,), jnp.float32), 'fc2_w': jax.random.normal(ks[5], (DIM, HIDDEN), jnp.float32) * s, 'fc2_b': jnp.zeros((DIM,), jnp.float32), 'ada_w': jax.random.normal(ks[6], (6 * DIM, DIM), jnp.float32) * s, 'ada_b': jnp.zeros((6 * DIM,), jnp.float32)}
    _L2_cond_all = _L2_cond_setup()
    _L2_cond_in = {k: v for k, v in _L2_cond_all.items() if k in ('g1', 'g2', 'qkv_w', 'qkv_b', 'qg', 'kg', 'proj_w', 'proj_b', 'fc1_w', 'fc1_b', 'fc2_w', 'fc2_b', 'ada_w', 'ada_b')}
    del _L2_cond_all

    def _L3_cond_setup():
        import jax, jax.numpy as jnp
        import numpy as np
        NUM_HEADS = 16
        NUM_EXPERTS = 4
        TOP_K = 2
        LN_EPS = 1e-06

        def _ln(h):
            mu = jnp.mean(h, axis=-1, keepdims=True)
            var = jnp.var(h, axis=-1, keepdims=True)
            return (h - mu) * jax.lax.rsqrt(var + LN_EPS)

        def _modulate(h, shift, scale):
            return h * (1.0 + scale[:, None, :]) + shift[:, None, :]
        key = jax.random.key(seed)
        ks = jax.random.split(key, 12)
        B, N, C = (8, 128, 144)
        H = 4 * C
        E = NUM_EXPERTS
        s = 0.02
        return {'x': jax.random.normal(ks[0], (B, N, C), jnp.float32), 'c': jax.random.normal(ks[1], (B, C), jnp.float32), 'w_adaln': jax.random.normal(ks[2], (C, 6 * C), jnp.float32) * s, 'b_adaln': jnp.zeros((6 * C,), jnp.float32), 'w_qkv': jax.random.normal(ks[3], (C, 3 * C), jnp.float32) * s, 'b_qkv': jnp.zeros((3 * C,), jnp.float32), 'w_proj': jax.random.normal(ks[4], (C, C), jnp.float32) * s, 'b_proj': jnp.zeros((C,), jnp.float32), 'w_gate': jax.random.normal(ks[5], (C, E), jnp.float32) * s, 'w1': jax.random.normal(ks[6], (E, C, H), jnp.float32) * s, 'b1': jnp.zeros((E, H), jnp.float32), 'w2': jax.random.normal(ks[7], (E, H, C), jnp.float32) * s, 'b2': jnp.zeros((E, C), jnp.float32)}
    _L3_cond_all = _L3_cond_setup()
    _L3_cond_in = {k: v for k, v in _L3_cond_all.items() if k in ('w_adaln', 'b_adaln', 'w_qkv', 'b_qkv', 'w_proj', 'b_proj', 'w_gate', 'w1', 'b1', 'w2', 'b2')}
    del _L3_cond_all
    return {'x': x, 'cond_1152': cond_1152, 'L0_cond_P': _L0_cond_in['P'], 'L0_cond_W': _L0_cond_in['W'], 'L0_cond_b': _L0_cond_in['b'], 'L1_cond_qkv_w': _L1_cond_in['qkv_w'], 'L1_cond_qkv_b': _L1_cond_in['qkv_b'], 'L1_cond_proj_w': _L1_cond_in['proj_w'], 'L1_cond_proj_b': _L1_cond_in['proj_b'], 'L1_cond_fc1_w': _L1_cond_in['fc1_w'], 'L1_cond_fc1_b': _L1_cond_in['fc1_b'], 'L1_cond_fc2_w': _L1_cond_in['fc2_w'], 'L1_cond_fc2_b': _L1_cond_in['fc2_b'], 'L1_cond_ada_w': _L1_cond_in['ada_w'], 'L1_cond_ada_b': _L1_cond_in['ada_b'], 'L2_cond_g1': _L2_cond_in['g1'], 'L2_cond_g2': _L2_cond_in['g2'], 'L2_cond_qkv_w': _L2_cond_in['qkv_w'], 'L2_cond_qkv_b': _L2_cond_in['qkv_b'], 'L2_cond_qg': _L2_cond_in['qg'], 'L2_cond_kg': _L2_cond_in['kg'], 'L2_cond_proj_w': _L2_cond_in['proj_w'], 'L2_cond_proj_b': _L2_cond_in['proj_b'], 'L2_cond_fc1_w': _L2_cond_in['fc1_w'], 'L2_cond_fc1_b': _L2_cond_in['fc1_b'], 'L2_cond_fc2_w': _L2_cond_in['fc2_w'], 'L2_cond_fc2_b': _L2_cond_in['fc2_b'], 'L2_cond_ada_w': _L2_cond_in['ada_w'], 'L2_cond_ada_b': _L2_cond_in['ada_b'], 'L3_cond_w_adaln': _L3_cond_in['w_adaln'], 'L3_cond_b_adaln': _L3_cond_in['b_adaln'], 'L3_cond_w_qkv': _L3_cond_in['w_qkv'], 'L3_cond_b_qkv': _L3_cond_in['b_qkv'], 'L3_cond_w_proj': _L3_cond_in['w_proj'], 'L3_cond_b_proj': _L3_cond_in['b_proj'], 'L3_cond_w_gate': _L3_cond_in['w_gate'], 'L3_cond_w1': _L3_cond_in['w1'], 'L3_cond_b1': _L3_cond_in['b1'], 'L3_cond_w2': _L3_cond_in['w2'], 'L3_cond_b2': _L3_cond_in['b2']}

def reference(x, cond_1152, L0_cond_P, L0_cond_W, L0_cond_b, L1_cond_qkv_w, L1_cond_qkv_b, L1_cond_proj_w, L1_cond_proj_b, L1_cond_fc1_w, L1_cond_fc1_b, L1_cond_fc2_w, L1_cond_fc2_b, L1_cond_ada_w, L1_cond_ada_b, L2_cond_g1, L2_cond_g2, L2_cond_qkv_w, L2_cond_qkv_b, L2_cond_qg, L2_cond_kg, L2_cond_proj_w, L2_cond_proj_b, L2_cond_fc1_w, L2_cond_fc1_b, L2_cond_fc2_w, L2_cond_fc2_b, L2_cond_ada_w, L2_cond_ada_b, L3_cond_w_adaln, L3_cond_b_adaln, L3_cond_w_qkv, L3_cond_b_qkv, L3_cond_w_proj, L3_cond_b_proj, L3_cond_w_gate, L3_cond_w1, L3_cond_b1, L3_cond_w2, L3_cond_b2):
    import jax
    import jax.numpy as jnp

    def _L0_cond_ref(x, cond, P, W, b):
        import jax, jax.numpy as jnp
        import numpy as np
        from jax.scipy.linalg import expm
        N, D, COND_DIM = (144, 64, 144)
        B, T = (16, 128)

        def _rotation(cond, W, b):
            v = jax.nn.silu(cond) @ W.T + b
            iu, ju = jnp.triu_indices(D, k=1)
            A = jnp.zeros((cond.shape[0], D, D), dtype=v.dtype)
            A = A.at[:, iu, ju].set(v).at[:, ju, iu].set(-v)
            return expm(A)
        U, _ = jnp.linalg.qr(P)
        R = _rotation(cond, W, b)
        z = jnp.einsum('btn,nd->btd', x, U)
        z_rot = jnp.einsum('btd,bde->bte', z, R)
        x_rot = x + jnp.einsum('btd,nd->btn', z_rot - z, U)
        return x_rot

    def _L1_cond_ref(x, c, qkv_w, qkv_b, proj_w, proj_b, fc1_w, fc1_b, fc2_w, fc2_b, ada_w, ada_b):
        import jax, jax.numpy as jnp
        import numpy as np
        N, T, D, H = (32, 128, 144, 16)
        DH = D // H
        MLP = int(D * 4.0)
        EPS = 1e-06

        def _layernorm(x):
            m = jnp.mean(x, axis=-1, keepdims=True)
            v = jnp.var(x, axis=-1, keepdims=True)
            return (x - m) * jax.lax.rsqrt(v + EPS)

        def _modulate(x, shift, scale):
            return x * (1.0 + scale[:, None, :]) + shift[:, None, :]

        def _attention(x, qkv_w, qkv_b, proj_w, proj_b):
            n, t, d = x.shape
            scale = DH ** (-0.5)
            qkv = x @ qkv_w + qkv_b
            qkv = qkv.reshape(n, t, 3, H, DH)
            q, k, v = (qkv[:, :, 0], qkv[:, :, 1], qkv[:, :, 2])
            attn = jnp.einsum('nthd,ntkd->nthk', q * scale, k)
            attn = jax.nn.softmax(attn, axis=-1)
            out = jnp.einsum('nthk,ntkd->nthd', attn, v)
            out = out.transpose(0, 2, 1, 3).reshape(n, t, d)
            return out @ proj_w + proj_b

        def _mlp(x, fc1_w, fc1_b, fc2_w, fc2_b):
            h = jax.nn.gelu(x @ fc1_w + fc1_b, approximate=False)
            return h @ fc2_w + fc2_b
        ada = jax.nn.silu(c) @ ada_w + ada_b
        shift_msa, scale_msa, gate_msa, shift_mlp, scale_mlp, gate_mlp = jnp.split(ada, 6, axis=1)
        x = x + gate_msa[:, None, :] * _attention(_modulate(_layernorm(x), shift_msa, scale_msa), qkv_w, qkv_b, proj_w, proj_b)
        x = x + gate_mlp[:, None, :] * _mlp(_modulate(_layernorm(x), shift_mlp, scale_mlp), fc1_w, fc1_b, fc2_w, fc2_b)
        return x

    def _L2_cond_ref(x, c, g1, g2, qkv_w, qkv_b, qg, kg, proj_w, proj_b, fc1_w, fc1_b, fc2_w, fc2_b, ada_w, ada_b):
        import jax, jax.numpy as jnp
        import numpy as np
        DIM = 144
        HEADS = 16
        HEAD_DIM = DIM // HEADS
        HIDDEN = int(DIM * 4.0)
        EPS = 1e-12

        def rmsnorm(x, g, d):
            n = jnp.linalg.norm(x, axis=-1, keepdims=True)
            return x / jnp.maximum(n, EPS) * d ** 0.5 * g

        def modulate(x, scale, shift):
            return x * (1.0 + scale[:, None, :]) + shift[:, None, :]
        B, N, D = x.shape
        mod = jax.nn.silu(c) @ ada_w.T + ada_b
        shift_msa, scale_msa, gate_msa, shift_mlp, scale_mlp, gate_mlp = jnp.split(mod, 6, axis=-1)
        gate_msa = jnp.tanh(gate_msa)
        gate_mlp = jnp.tanh(gate_mlp)
        h = modulate(rmsnorm(x, g1, D), scale_msa, shift_msa)
        qkv = h @ qkv_w.T + qkv_b
        qkv = qkv.reshape(B, N, 3, HEADS, HEAD_DIM).transpose(2, 0, 3, 1, 4)
        q, k, v = (qkv[0], qkv[1], qkv[2])
        q = rmsnorm(q, qg, HEAD_DIM)
        k = rmsnorm(k, kg, HEAD_DIM)
        q = q * HEAD_DIM ** (-0.5)
        attn = jax.nn.softmax(jnp.einsum('bhqd,bhkd->bhqk', q, k), axis=-1)
        o = jnp.einsum('bhqk,bhkd->bhqd', attn, v)
        o = o.transpose(0, 2, 1, 3).reshape(B, N, D)
        o = o @ proj_w.T + proj_b
        x = x + gate_msa[:, None, :] * o
        h2 = modulate(rmsnorm(x, g2, D), scale_mlp, shift_mlp)
        m = jax.nn.gelu(h2 @ fc1_w.T + fc1_b, approximate=True) @ fc2_w.T + fc2_b
        x = x + gate_mlp[:, None, :] * m
        return x

    def _L3_cond_ref(x, c, w_adaln, b_adaln, w_qkv, b_qkv, w_proj, b_proj, w_gate, w1, b1, w2, b2):
        import jax, jax.numpy as jnp
        import numpy as np
        NUM_HEADS = 16
        NUM_EXPERTS = 4
        TOP_K = 2
        LN_EPS = 1e-06

        def _ln(h):
            mu = jnp.mean(h, axis=-1, keepdims=True)
            var = jnp.var(h, axis=-1, keepdims=True)
            return (h - mu) * jax.lax.rsqrt(var + LN_EPS)

        def _modulate(h, shift, scale):
            return h * (1.0 + scale[:, None, :]) + shift[:, None, :]
        B, N, C = x.shape
        nh = NUM_HEADS
        hd = C // nh
        mod = jax.nn.silu(c) @ w_adaln + b_adaln
        sh_msa, sc_msa, g_msa, sh_mlp, sc_mlp, g_mlp = jnp.split(mod, 6, axis=-1)
        h = _modulate(_ln(x), sh_msa, sc_msa)
        qkv = (h @ w_qkv + b_qkv).reshape(B, N, 3, nh, hd).transpose(2, 0, 3, 1, 4)
        q, k, v = (qkv[0], qkv[1], qkv[2])
        attn = jax.nn.softmax(jnp.einsum('bhqd,bhkd->bhqk', q, k) * hd ** (-0.5), axis=-1)
        o = jnp.einsum('bhqk,bhkd->bhqd', attn, v).transpose(0, 2, 1, 3).reshape(B, N, C)
        o = o @ w_proj + b_proj
        x = x + g_msa[:, None, :] * o
        xn = _modulate(_ln(x), sh_mlp, sc_mlp)
        xf = xn.reshape(-1, C)
        gate_logits = xf @ w_gate
        topk_logits, topk_idx = jax.lax.top_k(gate_logits, TOP_K)
        gates = jax.nn.softmax(topk_logits, axis=-1)
        cw = jnp.sum(jax.nn.one_hot(topk_idx, NUM_EXPERTS, dtype=xf.dtype) * gates[..., None], axis=1)
        hmid = jax.nn.gelu(jnp.einsum('tc,ech->eth', xf, w1) + b1[:, None, :], approximate=True)
        eo = jnp.einsum('eth,ehc->etc', hmid, w2) + b2[:, None, :]
        moe = jnp.einsum('te,etc->tc', cw, eo).reshape(B, N, C)
        return x + g_mlp[:, None, :] * moe
    x = _L0_cond_ref(x, cond_1152, L0_cond_P, L0_cond_W, L0_cond_b)
    x = _L1_cond_ref(x, cond_1152, L1_cond_qkv_w, L1_cond_qkv_b, L1_cond_proj_w, L1_cond_proj_b, L1_cond_fc1_w, L1_cond_fc1_b, L1_cond_fc2_w, L1_cond_fc2_b, L1_cond_ada_w, L1_cond_ada_b)
    x = _L2_cond_ref(x, cond_1152, L2_cond_g1, L2_cond_g2, L2_cond_qkv_w, L2_cond_qkv_b, L2_cond_qg, L2_cond_kg, L2_cond_proj_w, L2_cond_proj_b, L2_cond_fc1_w, L2_cond_fc1_b, L2_cond_fc2_w, L2_cond_fc2_b, L2_cond_ada_w, L2_cond_ada_b)
    x = _L3_cond_ref(x, cond_1152, L3_cond_w_adaln, L3_cond_b_adaln, L3_cond_w_qkv, L3_cond_b_qkv, L3_cond_w_proj, L3_cond_b_proj, L3_cond_w_gate, L3_cond_w1, L3_cond_b1, L3_cond_w2, L3_cond_b2)
    return x

_drawn_inputs = setup_inputs


def setup_inputs(seed=0):
    import zlib

    import numpy as np

    out = dict(_drawn_inputs(seed))
    spreads = {'L2_cond_qkv_b': (0.0, 0.8),
     'L2_cond_proj_b': (0.0, 0.479),
     'L2_cond_fc1_b': (0.0, 0.8),
     'L2_cond_fc2_b': (0.0, 0.523),
     'L2_cond_ada_b': (0.0, 0.549),
     'L3_cond_b_adaln': (0.0, 0.523),
     'L3_cond_b_qkv': (0.0, 0.8),
     'L3_cond_b_proj': (0.0, 0.413),
     'L3_cond_b1': (0.0, 0.8),
     'L3_cond_b2': (0.0, 0.597)}
    factors = {'L1_cond_qkv_w': 8.0,
     'L1_cond_qkv_b': 8.0,
     'L1_cond_proj_w': 8.0,
     'L1_cond_proj_b': 8.0,
     'L1_cond_fc1_w': 6.646,
     'L1_cond_fc1_b': 8.0,
     'L1_cond_fc2_w': 6.543,
     'L1_cond_fc2_b': 8.0,
     'L1_cond_ada_w': 5.771,
     'L1_cond_ada_b': 8.0,
     'L2_cond_qkv_w': 8.0,
     'L2_cond_proj_w': 8.0,
     'L2_cond_fc1_w': 5.198,
     'L2_cond_fc2_w': 4.813,
     'L3_cond_w_adaln': 2.799,
     'L3_cond_w_qkv': 8.0,
     'L3_cond_w_proj': 8.0,
     'L3_cond_w_gate': 5.2,
     'L3_cond_w1': 7.087,
     'L3_cond_w2': 6.493}
    for name, (base, spread) in spreads.items():
        noise = np.random.default_rng([zlib.crc32(name.encode()), seed]).standard_normal(out[name].shape)
        drawn = base * np.exp(spread * noise) if base else spread * noise
        out[name] = jnp.asarray(drawn.astype(out[name].dtype))
    for name, factor in factors.items():
        out[name] = (out[name] * factor).astype(out[name].dtype)
    return out
```

```python
from contextlib import ExitStack

import numpy as np
import concourse.bass as bass
from concourse import mybir

F32 = mybir.dt.float32
BF16 = mybir.dt.bfloat16
ACT = mybir.ActivationFunctionType
ALU = mybir.AluOpType
AX = mybir.AxisListType

P = 128
B = 32
T = 128
D = 144
DT = D - P
H = 16
DH = D // H
HID = 4 * D
MT = 5
HL = HID - 4 * P
R = 64
E = 4
L = 3
G = 4
PAIRS = B // 2
SLOT = 64
PIECES = 6
DOUBLINGS = 10
SM = DH ** -0.5

MAIN_W = [3 * D + D + HID + 4 * D, 3 * D + D + HID + 4 * D, 3 * D + D + E + E * HID + E * 4 * D]
TAIL_W = [3 * D + D + HID, 3 * D + D + HID, 3 * D + D + E + E * HID]
LAST_W = [D, D, E * D]


def program(nc, t):
    ctx = ExitStack()
    with ctx:
        def sb(name, shape, dt=F32):
            return ctx.enter_context(nc.sbuf_tensor(name, shape, dt))

        def sem(name):
            return ctx.enter_context(nc.semaphore(name))

        bank = [ctx.enter_context(nc.psum_tensor(f"bank{i}", [P, 512], F32)) for i in range(8)]

        x_all = sb("x_all", [P, B, D])
        gate_all = sb("gate_all", [P, 2, B, D])
        ident = sb("ident", [P, P])
        identb = sb("identb", [P, P], BF16)
        w_main = [sb(f"w_main{l}", [P, MAIN_W[l]]) for l in range(L)]
        w_tail = [sb(f"w_tail{l}", [DT + 1, TAIL_W[l]]) for l in range(L)]
        w_last = [sb(f"w_last{l}", [HL + 1, LAST_W[l]]) for l in range(L)]
        mod = sb("mod", [P, L, 4, B])
        modt = sb("modt", [DT, L, 4, B])
        mean_all = sb("mean_all", [P, B])
        rstd_all = sb("rstd_all", [P, B])
        var_all = sb("var_all", [P, B])
        stats = sb("stats", [P, 2, 6])
        aggr = sb("aggr", [P, 2, 2])
        mhalf = sb("mhalf", [P, 1])
        phalf = sb("phalf", [P, 1])
        zero = sb("zero", [P, 1])
        gain = sb("gain", [P, 4])

        consts_in = sem("consts_in")
        w_in = [sem(f"w_in{l}") for l in range(L)]
        ones_ready = sem("ones_ready")
        gates_in = sem("gates_in")
        gates_out = sem("gates_out")
        scratch = nc.dram_tensor("gates_dram", [L * 2, B, D], F32, kind="Internal").ap()
        araw_dram = nc.dram_tensor("araw_dram", [B, R, R], F32, kind="Internal").ap()

        def load_gates(eng, phase):
            src = bass.AP(tensor=scratch.tensor, offset=phase * B * D, ap=[[0, P], [1, B * D]])
            eng.dma_start(gate_all[:, phase % 2].rearrange("p b d -> p (b d)"), src).then_inc(gates_in, 16)
            eng.wait_ge(gates_in, 16 * (phase + 1))

        adapter = ExitStack()
        with adapter:
            def asb(name, shape, dt=F32):
                return adapter.enter_context(nc.sbuf_tensor(name, shape, dt))

            qt = asb("qt", [P, D])
            u0 = asb("u0", [P, R])
            u1 = asb("u1", [DT, R])
            ex = asb("ex", [P, PAIRS, R])
            ey = asb("ey", [P, PAIRS, R])

            with ExitStack() as c:
                def tsb(name, shape, dt=F32):
                    return c.enter_context(nc.sbuf_tensor(name, shape, dt))

                def tsem(name):
                    return c.enter_context(nc.semaphore(name))

                cond = tsb("cond", [B, D])
                th = tsb("th", [B, D])
                sil = tsb("sil", [B, D])
                sc0 = tsb("sc0", [P, B])
                sc1 = tsb("sc1", [DT + 1, B])
                ada0 = tsb("ada0", [P, L, 6 * D])
                ada1 = tsb("ada1", [DT + 1, L, 6 * D])
                sk0 = tsb("sk0", [P, R * R])
                sk1 = tsb("sk1", [DT + 1, R * R])
                araw = tsb("araw", [B, R * R])
                gates = tsb("gates", [B, L * 2, D])
                sign = tsb("sign", [P, R])
                cond_in = tsem("cond_in")
                ada_in = tsem("ada_in")
                skew_in = tsem("skew_in")
                th_done = tsem("th_done")
                sil_done = tsem("sil_done")
                sct_done = tsem("sct_done")
                sc_done = tsem("sc_done")
                ones_set = ones_ready
                ada_done = tsem("ada_done")
                gate_mm = tsem("gate_mm")
                gate_ev = tsem("gate_ev")
                mod_ev = tsem("mod_ev")
                raw_mm = tsem("raw_mm")
                raw_ev_act = tsem("raw_ev_act")
                raw_ev_dve = tsem("raw_ev_dve")
                raw_out = tsem("raw_out")
                raw_back = tsem("raw_back")

                with nc.Block() as block:
                    @block.sync
                    def _(sp):
                        sp.dma_start(ident[:, :], t["ident"]).then_inc(consts_in, 16)
                        sp.dma_start(cond[:, :], t["cond"]).then_inc(cond_in, 16)
                        sp.dma_start(sign[:, :], t["sign"]).then_inc(consts_in, 16)
                        sp.dma_start(qt[0:R, :], t["pt"]).then_inc(consts_in, 16)
                        for j in range(4):
                            sp.dma_start(gain[:, j:j + 1], bass.AP(tensor=t["gains"].tensor, offset=j, ap=[[0, P], [1, 1]])).then_inc(consts_in, 16)
                        sp.dma_start(ada0[:, :, :], t["ada"][:, 0:P].rearrange("l k n -> k l n")).then_inc(ada_in, 16)
                        sp.dma_start(ada1[:, :, :], t["ada"][:, P:].rearrange("l k n -> k l n")).then_inc(ada_in, 16)
                        sp.dma_start(x_all[:, :, :], t["x"].rearrange("b t d -> t b d")).then_inc(consts_in, 16)
                        sp.wait_ge(raw_ev_act, 4)
                        sp.wait_ge(raw_ev_dve, 4)
                        sp.dma_start(araw_dram.rearrange("b i j -> b (i j)"), araw[:, :]).then_inc(raw_out, 16)
                        sp.wait_ge(raw_out, 16)
                        halves = araw_dram.rearrange("(q h) i j -> h i q j", h=2)
                        for half in range(2):
                            sp.dma_start(ex[half * R:(half + 1) * R, :, :], halves[half]).then_inc(raw_back, 16)
                        sp.wait_ge(gate_ev, L * 2)
                        sp.dma_start(scratch.rearrange("g b d -> b g d"), gates[:, :, :]).then_inc(gates_out, 16)
                        sp.wait_ge(gates_out, 16)
                        load_gates(sp, 0)
                        load_gates(sp, 1)

                    @block.scalar
                    def _(act):
                        act.dma_start(sk0[:, :], t["skew"][0:P]).then_inc(skew_in, 16)
                        act.dma_start(sk1[:, :], t["skew"][P:]).then_inc(skew_in, 16)
                        act.wait_ge(cond_in, 16)
                        nc.scalar.activation(th[:, :], cond[:, :], ACT.Tanh, scale=0.5).then_inc(th_done, 1)
                        for l in range(L):
                            act.dma_start(w_main[l][:, :], t[f"main{l}"]).then_inc(w_in[l], 16)
                            act.dma_start(w_tail[l][:, :], t[f"tail{l}"]).then_inc(w_in[l], 16)
                            act.dma_start(w_last[l][:, :], t[f"last{l}"]).then_inc(w_in[l], 16)
                        for g in range(L * 2):
                            act.wait_ge(gate_mm, g + 1)
                            f = ACT.Tanh if g // 2 == 1 else ACT.Copy
                            nc.scalar.activation(gates[:, g, :], bank[2 + g // 3][0:B, (g % 3) * D:(g % 3 + 1) * D], f).then_inc(gate_ev, 1)
                        for n in range(0, 8, 2):
                            act.wait_ge(raw_mm, n + 1)
                            nc.scalar.copy(araw[:, n * 512:(n + 1) * 512], bank[4 + n % 4][0:B, :]).then_inc(raw_ev_act, 1)

                    @block.vector
                    def _(dve):
                        nc.vector.memset(mhalf[:, :], -0.5).then_inc(ones_set, 1)
                        nc.vector.memset(phalf[:, :], 0.5).then_inc(ones_set, 1)
                        nc.vector.memset(zero[:, :], 0.0).then_inc(ones_set, 1)
                        nc.vector.memset(sc1[:, :], 1.0).then_inc(ones_set, 1)
                        dve.wait_ge(consts_in, 16 * 8)
                        nc.vector.tensor_copy(identb[:, :], ident[:, :]).then_inc(ones_set, 1)
                        dve.wait_ge(th_done, 1)
                        nc.vector.scalar_tensor_tensor(out=sil[:, :], in0=th[:, :], scalar=1.0, in1=cond[:, :], op0=ALU.add, op1=ALU.mult).then_inc(sil_done, 1)
                        dve.wait_ge(sct_done, 1)
                        dve.wait_ge(ones_set, 5)
                        nc.vector.tensor_scalar(sc0[:, :], bank[0][:, 0:B], 0.5, None, ALU.mult).then_inc(sc_done, 1)
                        nc.vector.tensor_scalar(sc1[0:DT, :], bank[0][0:DT, B:2 * B], 0.5, None, ALU.mult).then_inc(sc_done, 1)
                        for which in range(4):
                            dve.wait_ge(ada_done, 1)
                            one = float(which % 2)
                            nc.vector.tensor_scalar(mod[:, :, which, :], bank[0][:, 0:L * 4 * B].rearrange("p (l w b) -> p l w b", l=L, w=4)[:, :, which, :], one, None, ALU.add).then_inc(mod_ev, 1)
                            nc.vector.tensor_scalar(modt[:, :, which, :], bank[1][0:DT, 0:L * 4 * B].rearrange("p (l w b) -> p l w b", l=L, w=4)[:, :, which, :], one, None, ALU.add).then_inc(mod_ev, 1)
                        for n in range(1, 8, 2):
                            dve.wait_ge(raw_mm, n + 1)
                            nc.vector.tensor_copy(araw[:, n * 512:(n + 1) * 512], bank[4 + n % 4][0:B, :]).then_inc(raw_ev_dve, 1)
                        dve.wait_ge(raw_back, 32)
                        nc.vector.scalar_tensor_tensor(out=ex[:, :, :], in0=ex[:, :, :], scalar=2.0 ** -DOUBLINGS,
                                                       in1=sign[:, :].unsqueeze(1).to_broadcast([P, PAIRS, R]), op0=ALU.mult, op1=ALU.mult).then_inc(mod_ev, 1)
                        dve.wait_ge(mod_ev, 9)
                        dve.wait_ge(gates_in, 32)

                    @block.tensor
                    def _(pe):
                        pe.wait_ge(sil_done, 1)
                        nc.tensor.transpose(bank[0][:, 0:B], sil[:, 0:P], ident[0:B, 0:B])
                        nc.tensor.transpose(bank[0][0:DT, B:2 * B], sil[:, P:D], ident[0:B, 0:B]).then_inc(sct_done, 1)
                        pe.wait_ge(sc_done, 2)
                        pe.wait_ge(ada_in, 32)
                        for l in range(L):
                            for w, col in enumerate((0, 1, 3, 4)):
                                o = (l * 4 + w) * B
                                nc.tensor.matmul(bank[0][:, o:o + B], ada0[:, l, col * D:col * D + P], sc0[:, :], start=True, stop=False)
                                nc.tensor.matmul(bank[0][:, o:o + B], ada1[:, l, col * D:col * D + P], sc1[:, :], start=False, stop=True)
                                nc.tensor.matmul(bank[1][0:DT, o:o + B], ada0[:, l, col * D + P:(col + 1) * D], sc0[:, :], start=True, stop=False)
                                last = nc.tensor.matmul(bank[1][0:DT, o:o + B], ada1[:, l, col * D + P:(col + 1) * D], sc1[:, :], start=False, stop=True)
                        last.then_inc(ada_done, 1)
                        for g in range(L * 2):
                            col = 2 + 3 * (g % 2)
                            o = (g % 3) * D
                            if g == 3:
                                pass
                            nc.tensor.matmul(bank[2 + g // 3][0:B, o:o + D], sc0[:, :], ada0[:, g // 2, col * D:(col + 1) * D], start=True, stop=False)
                            last = nc.tensor.matmul(bank[2 + g // 3][0:B, o:o + D], sc1[:, :], ada1[:, g // 2, col * D:(col + 1) * D], start=False, stop=True)
                            if g % 3 == 2:
                                last.then_inc(gate_mm, 3)
                        pe.wait_ge(skew_in, 32)
                        for n in range(8):
                            if n >= 4:
                                pe.wait_ge(raw_ev_dve if n % 2 else raw_ev_act, (n - 4) // 2 + 1)
                            nc.tensor.matmul(bank[4 + n % 4][0:B, :], sc0[:, :], sk0[:, n * 512:(n + 1) * 512], start=True, stop=False)
                            nc.tensor.matmul(bank[4 + n % 4][0:B, :], sc1[:, :], sk1[:, n * 512:(n + 1) * 512], start=False, stop=True).then_inc(raw_mm, 1)
            with ExitStack() as c:
                def tsb(name, shape, dt=F32):
                    return c.enter_context(nc.sbuf_tensor(name, shape, dt))

                def tsem(name):
                    return c.enter_context(nc.semaphore(name))

                vs = tsb("vs", [R, R, D])
                inv_t = tsb("inv_t", [R, R])
                junk = tsb("junk", [R, D])
                junk2 = tsb("junk2", [R, D])
                acc = tsb("acc", [R, 16])
                nrm2, dot, half_sign, signed, w, tt, coef, nrm = (acc[:, j:j + 1] for j in range(8))
                qa = tsb("qa", [R, D])
                reduced = tsem("reduced")
                row_done = tsem("row_done")
                chain = tsem("chain")
                nrm2_done = tsem("nrm2_done")
                nrm_done = tsem("nrm_done")
                setup_qr = tsem("setup_qr")
                back = tsem("back")
                ut_mm = tsem("ut_mm")
                STEPS = 9

                with nc.Block() as block:
                    @block.gpsimd
                    def _(pool):
                        for k in range(R):
                            pool.wait_ge(nrm2_done, k + 1)
                            pool.wait_ge(ones_ready, 1)
                            nc.gpsimd.tensor_tensor(nrm, nrm2, phalf[0:R, :], ALU.pow).then_inc(nrm_done, 1)

                    @block.tensor
                    def _(pe):
                        for k in range(R):
                            pe.wait_ge(reduced, k + 1)
                            nc.tensor.matmul(bank[k % 2][0:R, 0:D], ident[0:R, k:k + 1].to_broadcast([R, R]), qa[:, :], start=True, stop=True).then_inc(row_done, 1)
                        pe.wait_ge(back, 2 * R + 3)
                        nc.tensor.transpose(bank[0][:, 0:R], qt[0:R, 0:P], ident[0:R, 0:R])
                        nc.tensor.transpose(bank[0][0:DT, R:2 * R], qt[0:R, P:D], ident[0:R, 0:R]).then_inc(ut_mm, 1)

                    @block.vector
                    def _(dve):
                        nc.vector.tensor_copy(qa[:, :], qt[0:R, :]).then_inc(reduced, 1)
                        for k in range(R):
                            done = k * STEPS
                            v = vs[:, k, :]
                            dve.wait_ge(row_done, k + 1)
                            nc.vector.tensor_copy(v, bank[k % 2][0:R, 0:D]).then_inc(chain, 1)
                            dve.wait_ge(chain, done + 1)
                            nc.vector.tensor_tensor(junk[:, :], v, v, ALU.mult).then_inc(chain, 1)
                            nc.vector.tensor_tensor(junk2[:, :], v, qa[:, :], ALU.mult).then_inc(chain, 1)
                            dve.wait_ge(chain, done + 2)
                            nc.vector.tensor_reduce(nrm2, junk[:, :], AX.X, ALU.add).then_inc(nrm2_done, 1)
                            dve.wait_ge(chain, done + 3)
                            nc.vector.tensor_reduce(dot, junk2[:, :], AX.X, ALU.add).then_inc(chain, 1)
                            nc.vector.tensor_scalar(half_sign, vs[:, k, k:k + 1], 0.0, 0.5, ALU.is_ge, ALU.subtract).then_inc(chain, 1)
                            dve.wait_ge(chain, done + 5)
                            dve.wait_ge(nrm_done, k + 1)
                            nc.vector.scalar_tensor_tensor(out=signed, in0=nrm, scalar=2.0, in1=half_sign, op0=ALU.mult, op1=ALU.mult).then_inc(chain, 1)
                            dve.wait_ge(chain, done + 6)
                            nc.vector.tensor_tensor(vs[:, k, k:k + 1], vs[:, k, k:k + 1], signed, ALU.add).then_inc(chain, 1)
                            nc.vector.scalar_tensor_tensor(out=w, in0=qa[:, k:k + 1], scalar=signed, in1=dot, op0=ALU.mult, op1=ALU.add)
                            dve.wait_ge(chain, done + 7)
                            nc.vector.tensor_tensor(tt, vs[:, k, k:k + 1], signed, ALU.mult).then_inc(chain, 1)
                            dve.wait_ge(chain, done + 8)
                            nc.vector.reciprocal(inv_t[:, k:k + 1], tt).then_inc(chain, 1)
                            dve.wait_ge(chain, done + 9)
                            nc.vector.scalar_tensor_tensor(out=coef, in0=w, scalar=-1.0, in1=inv_t[:, k:k + 1], op0=ALU.mult, op1=ALU.mult).then_inc(back, 1)
                            dve.wait_ge(back, k + 1)
                            nc.vector.scalar_tensor_tensor(out=qa[:, :], in0=v, scalar=coef, in1=qa[:, :], op0=ALU.mult, op1=ALU.add).then_inc(setup_qr, 1)
                            dve.wait_ge(setup_qr, k + 1)
                            nc.vector.memset(qa[:, k:k + 1], 0.0).then_inc(reduced, 1)
                        nc.vector.memset(qt[:, :], 0.0).then_inc(back, 1)
                        dve.wait_ge(back, R + 1)
                        nc.vector.tensor_copy(qt[0:R, 0:R], ident[0:R, 0:R]).then_inc(back, 1)
                        for i in range(R):
                            k = R - 1 - i
                            dve.wait_ge(back, R + 2 + i)
                            nc.vector.tensor_tensor(junk[:, :], vs[:, k, :], qt[0:R, :], ALU.mult).then_inc(chain, 1)
                            dve.wait_ge(chain, i * 3 + (R * STEPS + 1))
                            nc.vector.tensor_reduce(dot, junk[:, :], AX.X, ALU.add).then_inc(chain, 1)
                            dve.wait_ge(chain, i * 3 + (R * STEPS + 2))
                            nc.vector.scalar_tensor_tensor(out=coef, in0=dot, scalar=-1.0, in1=inv_t[:, k:k + 1], op0=ALU.mult, op1=ALU.mult).then_inc(chain, 1)
                            dve.wait_ge(chain, i * 3 + (R * STEPS + 3))
                            nc.vector.scalar_tensor_tensor(out=qt[0:R, :], in0=vs[:, k, :], scalar=coef, in1=qt[0:R, :], op0=ALU.mult, op1=ALU.add).then_inc(back, 1)
                        dve.wait_ge(back, 2 * R + 2)
                        nc.vector.tensor_copy(qt[R:P, :], qt[0:R, :]).then_inc(back, 1)
                        dve.wait_ge(ut_mm, 1)
                        nc.vector.tensor_copy(u0[:, :], bank[0][:, 0:R]).then_inc(ut_mm, 1)
                        nc.vector.tensor_copy(u1[:, :], bank[0][0:DT, R:2 * R]).then_inc(ut_mm, 1)
                        dve.wait_ge(ut_mm, 3)
            with ExitStack() as c:
                def tsb(name, shape, dt=F32):
                    return c.enter_context(nc.sbuf_tensor(name, shape, dt))

                def tsem(name):
                    return c.enter_context(nc.semaphore(name))

                a2, a4, a6, poly = (tsb(n, [P, PAIRS, R]) for n in ("a2", "a4", "a6", "poly"))
                prod_done = tsem("prod_done")
                evac_done = tsem("evac_done")
                term = tsem("term")
                HALF = PAIRS // 2

                def halves(m, h):
                    return m[:, h * HALF:(h + 1) * HALF, :].rearrange("p q j -> p (q j)")

                with nc.Block() as block:
                    @block.tensor
                    def _(pe):
                        def product(lhs, rhs, h, dst):
                            for q in range(HALF):
                                for half in range(2):
                                    rows = slice(half * R, (half + 1) * R)
                                    last = nc.tensor.matmul(bank[dst][rows, q * R:(q + 1) * R], lhs[rows, h * HALF + q, :], rhs[rows, h * HALF + q, :],
                                                            start=True, stop=True)
                            last.then_inc(prod_done, 1)

                        for n, (lhs, rhs) in enumerate(((ex, ex), (a2, a2), (a4, a2), (ex, poly))):
                            for h in range(2):
                                if n:
                                    pe.wait_ge(evac_done, 2 * n - 1 + h)
                                if n == 3:
                                    pe.wait_ge(term, 2)
                                product(lhs, rhs, h, 2 * (n % 2) + h)
                        for s in range(DOUBLINGS):
                            pe.wait_ge(term, 6)
                            for h in range(2):
                                pe.wait_ge(evac_done, 10 + (4 * (s - 1) + 2 * h + 2 if s else 0))
                                product(ey, ex, h, 4 * (s % 2) + 2 * h)
                                product(ex, ey, h, 4 * (s % 2) + 2 * h + 1)

                    @block.vector
                    def _(dve):
                        for h in range(2):
                            dve.wait_ge(prod_done, 1 + h)
                            nc.vector.tensor_scalar(halves(a2, h), bank[h][:, :], -1.0, None, ALU.mult).then_inc(evac_done, 1)
                        for h in range(2):
                            dve.wait_ge(prod_done, 3 + h)
                            nc.vector.tensor_copy(halves(a4, h), bank[2 + h][:, :]).then_inc(evac_done, 1)
                        for h in range(2):
                            dve.wait_ge(prod_done, 5 + h)
                            nc.vector.tensor_copy(halves(a6, h), bank[h][:, :]).then_inc(evac_done, 1)
                        dve.wait_ge(evac_done, 6)
                        nc.vector.tensor_scalar(poly[:, :, :], a2[:, :, :], 1 / 6, None, ALU.mult).then_inc(term, 1)
                        dve.wait_ge(term, 1)
                        nc.vector.scalar_tensor_tensor(out=poly[:, :, :], in0=a4[:, :, :], scalar=1 / 120, in1=poly[:, :, :], op0=ALU.mult, op1=ALU.add).then_inc(evac_done, 1)
                        dve.wait_ge(evac_done, 7)
                        nc.vector.scalar_tensor_tensor(out=poly[:, :, :], in0=a6[:, :, :], scalar=1 / 5040, in1=poly[:, :, :], op0=ALU.mult, op1=ALU.add).then_inc(term, 1)
                        nc.vector.tensor_scalar(a2[:, :, :], a2[:, :, :], 0.5, None, ALU.mult).then_inc(term, 1)
                        dve.wait_ge(term, 3)
                        nc.vector.scalar_tensor_tensor(out=a2[:, :, :], in0=a4[:, :, :], scalar=1 / 24, in1=a2[:, :, :], op0=ALU.mult, op1=ALU.add).then_inc(term, 1)
                        dve.wait_ge(term, 4)
                        nc.vector.scalar_tensor_tensor(out=a2[:, :, :], in0=a6[:, :, :], scalar=1 / 720, in1=a2[:, :, :], op0=ALU.mult, op1=ALU.add).then_inc(term, 1)
                        for h in range(2):
                            dve.wait_ge(prod_done, 7 + h)
                            dve.wait_ge(term, 5)
                            nc.vector.tensor_tensor(halves(a4, h), halves(ex, h), bank[2 + h][:, :], ALU.subtract).then_inc(evac_done, 1)
                        dve.wait_ge(evac_done, 9)
                        nc.vector.tensor_tensor(ex[:, :, :], a2[:, :, :], a4[:, :, :], ALU.add).then_inc(evac_done, 1)
                        nc.vector.tensor_tensor(ey[:, :, :], a2[:, :, :], a4[:, :, :], ALU.subtract).then_inc(term, 1)
                        dve.wait_ge(term, 6)
                        for s in range(DOUBLINGS):
                            for h in range(2):
                                dve.wait_ge(prod_done, 8 + 4 * s + 2 * h + 2)
                                for m, b in ((ex, 0), (ey, 1)):
                                    if s == 0 and h == 0 and b == 0:
                                        dve.wait_ge(evac_done, 10)
                                    elif s:
                                        dve.wait_ge(evac_done, 10 + 4 * s - 4 + 2 * h + 1 + b)
                                    nc.vector.scalar_tensor_tensor(out=halves(m, h), in0=halves(m, h), scalar=2.0, in1=bank[4 * (s % 2) + 2 * h + b][:, :],
                                                                   op0=ALU.mult, op1=ALU.add).then_inc(evac_done, 1)
                        dve.wait_ge(evac_done, 10 + 4 * DOUBLINGS)
            with ExitStack() as c:
                def tsb(name, shape, dt=F32):
                    return c.enter_context(nc.sbuf_tensor(name, shape, dt))

                def tsem(name):
                    return c.enter_context(nc.semaphore(name))

                xc = tsb("xc", [P, 2, 2, D])
                yc = tsb("yc", [P, 2, R])
                xt0 = tsb("xt0", [P, 2, 2 * T])
                xt1 = tsb("xt1", [DT, 2, 2 * T])
                zt = tsb("zt", [P, 2, T])
                bm = tsb("bm", [P, 2, D])
                staged = tsem("staged")
                xt_mm = tsem("xt_mm")
                xt_done = tsem("xt_done")
                z_mm = tsem("z_mm")
                z_done = tsem("z_done")
                rot_mm = tsem("rot_mm")
                x_done = tsem("x_done")
                st_done = tsem("st_done")
                var_done = tsem("var_done")
                rs_done = tsem("rs_done")

                with nc.Block() as block:
                    @block.gpsimd
                    def _(pool):
                        def stage(q, u):
                            nc.gpsimd.tensor_copy(xc[:, u, :, :], x_all[:, bass.ds(q * 2, 2), :]).then_inc(staged, 1)
                            nc.gpsimd.tensor_copy(yc[:, u, :], ey[:, q, :]).then_inc(staged, 1)

                        stage(0, 0)
                        stage(1, 1)
                        with nc.gpsimd.Fori(1, PAIRS // 2) as i:
                            for u in range(2):
                                pool.wait_ge(ones_ready, 1)
                                pool.wait_ge(x_done, i * 2 - 1 + u)
                                stage(i * 2 + u, u)

                    @block.tensor
                    def _(pe):
                        with nc.tensor.Fori(0, PAIRS // 2) as i:
                            for u in range(2):
                                n = i * 2 + u
                                pe.wait_ge(staged, n * 2 + 2)
                                for s in range(2):
                                    nc.tensor.transpose(bank[0][:, s * T:(s + 1) * T], xc[:, u, s, 0:P], ident[:, :])
                                for s in range(2):
                                    last = nc.tensor.transpose(bank[1][0:DT, s * T:(s + 1) * T], xc[:, u, s, P:D], ident[:, :])
                                last.then_inc(xt_mm, 1)
                                for s in range(2):
                                    h = slice(s * R, (s + 1) * R)
                                    nc.tensor.matmul(bank[3][h, 0:D], yc[h, u, :], qt[h, :], start=True, stop=True)
                                pe.wait_ge(ones_ready, 1)
                                pe.wait_ge(xt_done, n + 1)
                                for s in range(2):
                                    h = slice(s * R, (s + 1) * R)
                                    nc.tensor.matmul(bank[2][h, 0:T], u0[:, :], xt0[:, u, s * T:(s + 1) * T], start=True, stop=False)
                                    last = nc.tensor.matmul(bank[2][h, 0:T], u1[:, :], xt1[:, u, s * T:(s + 1) * T], start=False, stop=True)
                                last.then_inc(z_mm, 1)
                                pe.wait_ge(z_done, n + 1)
                                for s in range(2):
                                    h = slice(s * R, (s + 1) * R)
                                    last = nc.tensor.matmul(bank[4 + s][:, 0:D], zt[h, u, :], bm[h, u, :], start=True, stop=True)
                                last.then_inc(rot_mm, 1)

                    @block.scalar
                    def _(act):
                        with nc.scalar.Fori(0, PAIRS // 2) as i:
                            for u in range(2):
                                n = i * 2 + u
                                act.wait_ge(z_mm, n + 1)
                                nc.scalar.copy(zt[:, u, :], bank[2][:, 0:T])
                                nc.scalar.copy(bm[:, u, :], bank[3][:, 0:D]).then_inc(z_done, 1)

                    @block.vector
                    def _(dve):
                        with nc.vector.Fori(0, PAIRS // 2) as i:
                            for u in range(2):
                                n = i * 2 + u
                                dve.wait_ge(xt_mm, n + 1)
                                nc.vector.tensor_copy(xt0[:, u, :], bank[0][:, 0:2 * T])
                                nc.vector.tensor_copy(xt1[:, u, :], bank[1][0:DT, 0:2 * T]).then_inc(xt_done, 1)
                                dve.wait_ge(rot_mm, n + 1)
                                for s in range(2):
                                    seq = n * 2 + s
                                    last = nc.vector.tensor_tensor(x_all[:, seq, :], xc[:, u, s, :], bank[4 + s][:, 0:D], ALU.add)
                                last.then_inc(x_done, 1)
                                dve.wait_ge(ones_ready, 1)
                                dve.wait_ge(x_done, n + 1)
                                nc.vector.bn_stats(stats[:, 0, :], x_all[:, n * 2, :])
                                nc.vector.bn_stats(stats[:, 1, :], x_all[:, n * 2 + 1, :]).then_inc(st_done, 1)
                                dve.wait_ge(ones_ready, 1)
                                dve.wait_ge(st_done, n + 1)
                                nc.vector.bn_aggr(aggr[:, 0, :], stats[:, 0, :])
                                nc.vector.bn_aggr(aggr[:, 1, :], stats[:, 1, :]).then_inc(var_done, 1)
                                dve.wait_ge(var_done, n + 1)
                                nc.vector.tensor_copy(mean_all[:, bass.ds(n * 2, 2)], aggr[:, :, 0])
                                nc.vector.tensor_scalar(var_all[:, bass.ds(n * 2, 2)], aggr[:, :, 1], 1e-6, None, ALU.add).then_inc(rs_done, 1)
                        dve.wait_ge(rs_done, PAIRS)
                with nc.Block() as block:
                    @block.gpsimd
                    def _(pool):
                        nc.gpsimd.tensor_tensor(rstd_all[:, :], var_all[:, :], mhalf[:, :].to_broadcast([P, B]), ALU.pow).then_inc(rs_done, 1)
                        pool.wait_ge(rs_done, PAIRS + 1)
        def variance(dve, rms, both, b, done, ms, count):
            if rms:
                nc.vector.scalar_tensor_tensor(out=both[:, 1:2], in0=both[:, 0:1], scalar=both[:, 0:1], in1=both[:, 1:2], op0=ALU.mult, op1=ALU.add).then_inc(ms, 1)
                dve.wait_ge(ms, count + 1)
                nc.vector.tensor_scalar(var_all[:, bass.ds(b, 1)], both[:, 1:2], 1e-24 / D, None, ALU.max).then_inc(done, 1)
            else:
                nc.vector.tensor_copy(mean_all[:, bass.ds(b, 1)], both[:, 0:1])
                nc.vector.tensor_scalar(var_all[:, bass.ds(b, 1)], both[:, 1:2], 1e-6, None, ALU.add).then_inc(done, 1)

        with ExitStack() as c:
            def tsb(name, shape, dt=F32):
                return c.enter_context(nc.sbuf_tensor(name, shape, dt))

            turned = nc.dram_tensor("turned", [B, H, T, DH], F32, kind="Internal").ap()
            hn = tsb("h_hn", [P, 2, D])
            ht0 = tsb("h_ht0", [P, 2, T])
            ht1 = tsb("h_ht1", [DT + 1, 2, T])
            qkv = tsb("h_qkv", [P, 2, 3 * D])
            qk_prod = tsb("h_qk_prod", [P, H, H, DH])
            score = tsb("h_score", [P, 2, H, H])
            top = tsb("h_top", [P, H])
            prob = tsb("h_prob", [P, 2, H, H])
            rsum = tsb("h_rsum", [P, 2, H])
            pv_prod = tsb("h_pv_prod", [P, 2, H, H, DH])
            out_h = tsb("h_out", [P, 2, D])
            y = tsb("h_y", [P, 2, D])
            at0 = tsb("h_at0", [P, 2, T])
            at1 = tsb("h_at1", [DT + 1, 2, T])
            upd = tsb("h_upd", [P, 2, D])
            names = ("set hn_done ht_mm ht_done qkv_mm qkv_done qk_done score_done max_done sub_done exp_done sum_done rsum_done pv_done "
                     "pvsum_mm out_done turn_out turn_in y_mm y_done proj_mm upd_done x_new stat_done aggr_done var_new rstd_new").split()
            S = {k: sem("h_" + k) for k in names}
            b_tp, b_mm, b_sum, b_ty, b_pj = bank[0:5]

            def drive(eng, step):
                step(-1, 1, middle=False, sums=False, last=False)
                step(0, 0, sums=False, last=False)
                step(1, 1, last=False)
                step(2, 0)
                step(3, 1)
                with eng.Fori(0, (B - 6) // 2) as i:
                    step(i * 2 + 4, 0)
                    step(i * 2 + 5, 1)
                step(B - 2, 0)
                step(B - 1, 1, front=False)
                step(B, 0, front=False, middle=False)
                step(B + 1, 1, front=False, middle=False, sums=False)

            with nc.Block() as block:
                @block.tensor
                def _(pe):
                    def step(b, u, front=True, middle=True, sums=True, last=True):
                        w = 1 - u
                        if front:
                            pe.wait_ge(S["hn_done"], b + 2)
                            nc.tensor.transpose(b_tp[:, 0:T], hn[:, w, 0:P], ident[:, :])
                            nc.tensor.transpose(b_tp[0:DT, T:2 * T], hn[:, w, P:D], ident[:, :]).then_inc(S["ht_mm"], 1)
                        if sums:
                            pe.wait_ge(S["pv_done"], b)
                            if last:
                                pe.wait_ge(S["out_done"], b - 1)
                            for k in range(H):
                                mm = nc.tensor.matmul(b_sum[:, 0:D], ident[:, :], pv_prod[:, w, k, :, :].rearrange("p h d -> p (h d)"), start=(k == 0), stop=(k == H - 1))
                            mm.then_inc(S["pvsum_mm"], 1)
                        if last:
                            pe.wait_ge(S["turn_in"], (b - 1) * 16)
                            nc.tensor.transpose(b_ty[:, 0:T], y[:, u, 0:P], ident[:, :])
                            nc.tensor.transpose(b_ty[0:DT, T:2 * T], y[:, u, P:D], ident[:, :]).then_inc(S["y_mm"], 1)
                        if front:
                            pe.wait_ge(S["set"], 2)
                            pe.wait_ge(S["ht_done"], b * 2 + 4)
                            if middle:
                                pe.wait_ge(S["qkv_done"], b + 1)
                            nc.tensor.matmul(b_mm[:, 0:3 * D], ht0[:, w, :], w_main[0][:, 0:3 * D], start=True, stop=False)
                            nc.tensor.matmul(b_mm[:, 0:3 * D], ht1[:, w, :], w_tail[0][:, 0:3 * D], start=False, stop=True).then_inc(S["qkv_mm"], 1)
                        if last:
                            pe.wait_ge(S["y_done"], b * 2 - 2)
                            if not isinstance(b, int) or b > 2:
                                pe.wait_ge(S["upd_done"], b - 2)
                            nc.tensor.matmul(b_pj[:, 0:D], at0[:, u, :], w_main[0][:, 3 * D:4 * D], start=True, stop=False)
                            nc.tensor.matmul(b_pj[:, 0:D], at1[:, u, :], w_tail[0][:, 3 * D:4 * D], start=False, stop=True).then_inc(S["proj_mm"], 1)

                    pe.wait_ge(w_in[0], 48)
                    drive(nc.tensor, step)

                @block.scalar
                def _(act):
                    def step(b, u, front=True, middle=True, sums=True, last=True):
                        w = 1 - u
                        if middle:
                            act.wait_ge(S["sub_done"], b + 1)
                            nc.scalar.activation(prob[:, u, :, :], score[:, u, :, :], ACT.Exp, scale=SM).then_inc(S["exp_done"], 1)
                        if front:
                            act.wait_ge(S["qkv_mm"], b + 2)
                            nc.scalar.copy(qkv[:, w, :], b_mm[:, 0:3 * D]).then_inc(S["qkv_done"], 1)
                        if last:
                            act.wait_ge(S["y_mm"], b - 1)
                            nc.scalar.copy(at0[:, u, :], b_ty[:, 0:T]).then_inc(S["y_done"], 1)
                            nc.scalar.copy(at1[0:DT, u, :], b_ty[0:DT, T:2 * T]).then_inc(S["y_done"], 1)

                    drive(nc.scalar, step)

                @block.gpsimd
                def _(pool):
                    def step(b, u, front=True, middle=True, sums=True, last=True):
                        w = 1 - u
                        if middle:
                            pool.wait_ge(S["exp_done"], b + 1)
                            if sums and last:
                                pool.wait_ge(S["pvsum_mm"], b - 1)
                            nc.gpsimd.tensor_tensor(pv_prod[:, u, :, :, :], prob[:, u, :, :].rearrange("p h k -> p k h").unsqueeze(3).to_broadcast([P, H, H, DH]),
                                                    qkv[:, u, 2 * D:3 * D].rearrange("p (k d) -> p k d", d=DH).unsqueeze(2).to_broadcast([P, H, H, DH]), ALU.mult).then_inc(S["pv_done"], 1)
                        if last:
                            pool.wait_ge(S["var_new"], b - 1)
                            nc.gpsimd.tensor_tensor(rstd_all[:, bass.ds(b - 2, 1)], var_all[:, bass.ds(b - 2, 1)], mhalf[:, :], ALU.pow).then_inc(S["rstd_new"], 1)

                    drive(nc.gpsimd, step)
                    pool.wait_ge(S["rstd_new"], B)

                @block.sync
                def _(sp):
                    def step(b, u, front=True, middle=True, sums=True, last=True):
                        if not sums:
                            return
                        w = 1 - u
                        sp.wait_ge(S["out_done"], b)
                        sp.dma_start(turned[b - 1].rearrange("h t d -> t h d"), out_h[:, w, :].rearrange("p (h d) -> p h d", d=DH)).then_inc(S["turn_out"], 16)
                        sp.wait_ge(S["turn_out"], b * 16)
                        sp.dma_start(y[:, w, :], turned[b - 1].rearrange("h t d -> (h t d)").rearrange("(p q) -> p q", q=D)).then_inc(S["turn_in"], 16)

                    drive(nc.sync, step)

                @block.vector
                def _(dve):
                    def step(b, u, front=True, middle=True, sums=True, last=True):
                        w = 1 - u
                        nb = b + 1
                        if front:
                            nc.vector.tensor_scalar(hn[:, w, :], x_all[:, nb, :], mean_all[:, bass.ds(nb, 1)], rstd_all[:, bass.ds(nb, 1)], ALU.subtract, ALU.mult).then_inc(S["hn_done"], 1)
                        if middle:
                            dve.wait_ge(S["qkv_done"], b + 1)
                            heads = qkv[:, u, :].rearrange("p (s h d) -> p s h d", s=3, d=DH)
                            nc.vector.tensor_tensor(qk_prod[:, :, :, :], heads[:, 0].unsqueeze(2).to_broadcast([P, H, H, DH]),
                                                    heads[:, 1].unsqueeze(1).to_broadcast([P, H, H, DH]), ALU.mult).then_inc(S["qk_done"], 1)
                        if front:
                            dve.wait_ge(S["ht_mm"], b + 2)
                            nc.vector.tensor_scalar(ht0[:, w, :], b_tp[:, 0:T], mod[:, 0, 1, bass.ds(nb, 1)], mod[:, 0, 0, bass.ds(nb, 1)], ALU.mult, ALU.add).then_inc(S["ht_done"], 1)
                            nc.vector.tensor_scalar(ht1[0:DT, w, :], b_tp[0:DT, T:2 * T], modt[:, 0, 1, bass.ds(nb, 1)], modt[:, 0, 0, bass.ds(nb, 1)], ALU.mult, ALU.add).then_inc(S["ht_done"], 1)
                        if middle:
                            dve.wait_ge(S["qk_done"], b + 1)
                            nc.vector.tensor_reduce(score[:, u, :, :], qk_prod[:, :, :, :], AX.X, ALU.add).then_inc(S["score_done"], 1)
                            dve.wait_ge(S["score_done"], b + 1)
                            nc.vector.tensor_reduce(top[:, :], score[:, u, :, :], AX.X, ALU.max).then_inc(S["max_done"], 1)
                            dve.wait_ge(S["max_done"], b + 1)
                            nc.vector.tensor_tensor(score[:, u, :, :], score[:, u, :, :], top[:, :].unsqueeze(2).to_broadcast([P, H, H]), ALU.subtract).then_inc(S["sub_done"], 1)
                        if sums:
                            dve.wait_ge(S["rsum_done"], b)
                            dve.wait_ge(S["pvsum_mm"], b)
                            if last:
                                dve.wait_ge(S["turn_out"], (b - 1) * 16)
                            nc.vector.tensor_tensor(out_h[:, w, :].rearrange("p (h d) -> p h d", d=DH), b_sum[:, 0:D].rearrange("p (h d) -> p h d", d=DH),
                                                    rsum[:, w, :].unsqueeze(2).to_broadcast([P, H, DH]), ALU.mult).then_inc(S["out_done"], 1)
                        if last:
                            pb = b - 2
                            dve.wait_ge(S["proj_mm"], b - 1)
                            nc.vector.tensor_tensor(upd[:, u, :], b_pj[:, 0:D], gate_all[:, 0, pb, :], ALU.mult).then_inc(S["upd_done"], 1)
                            dve.wait_ge(S["upd_done"], b - 1)
                            nc.vector.tensor_tensor(x_all[:, pb, :], x_all[:, pb, :], upd[:, u, :], ALU.add).then_inc(S["x_new"], 1)
                            dve.wait_ge(ones_ready, 1)
                            dve.wait_ge(S["x_new"], b - 1)
                            nc.vector.bn_stats(stats[:, u, :], x_all[:, pb, :]).then_inc(S["stat_done"], 1)
                            dve.wait_ge(ones_ready, 1)
                            dve.wait_ge(S["stat_done"], b - 1)
                            nc.vector.bn_aggr(aggr[:, u, :], stats[:, u, :]).then_inc(S["aggr_done"], 1)
                            dve.wait_ge(S["aggr_done"], b - 1)
                            variance(dve, False, aggr[:, u], pb, S["var_new"], None, b - 2)
                        if middle:
                            dve.wait_ge(S["exp_done"], b + 1)
                            nc.vector.tensor_reduce(rsum[:, u, :], prob[:, u, :, :], AX.X, ALU.add).then_inc(S["sum_done"], 1)
                            dve.wait_ge(S["sum_done"], b + 1)
                            nc.vector.reciprocal(rsum[:, u, :], rsum[:, u, :]).then_inc(S["rsum_done"], 1)

                    nc.vector.memset(ht1[:, :, :], 1.0).then_inc(S["set"], 1)
                    nc.vector.memset(at1[:, :, :], 1.0).then_inc(S["set"], 1)
                    dve.wait_ge(S["set"], 2)
                    drive(nc.vector, step)
                    dve.wait_ge(S["var_new"], B)
                    dve.wait_ge(S["rsum_done"], B)
        hn = sb("hn", [P, 2, D])
        ht0 = sb("ht0", [P, 2, T])
        ht1 = sb("ht1", [DT + 1, 2, T])
        sq = sb("sq", [P, 2 * D])
        ssum = sb("ssum", [P, 2 * H])
        qk = sb("qk", [P, 2 * D])
        rest = sb("rest", [P, 2 * D])
        stack = sb("stack", [P, 2, 2, H, SLOT], BF16)
        qs = sb("qs", [P, 2, H // 2, T], BF16)
        ks = sb("ks", [P, 2, H // 2, T], BF16)
        va = sb("va", [P, 2, H, 32])
        rmax = sb("rmax", [P, H])
        pt = sb("pt", [P, 2, H, T])
        ot = sb("ot", [P, 2, 4 * T])
        rsum = sb("rsum", [P, H])
        at = sb("at", [P, 2, D])
        at0 = sb("at0", [P, 2, T])
        at1 = sb("at1", [DT + 1, 2, T])
        upd = sb("upd", [P, 2, D])

        names = ("hn_done ht_mm ht_done qkv_mm square_done ssum_done rq_done qkn_done high_done v_done rest_done "
                 "midp_done low_done qs_mm qs_done ks_mm ks_done s_mm max_done neg_done q2_mm q2_done st_mm exp_done "
                 "pv_mm ot_done back_mm rsum_done at_done at_mm at_ev proj_mm upd_done x_new stat_done aggr_done var_new rstd_new gain_step ms_done").split()
        S = {k: sem("a_" + k) for k in names}

        set_done = sem("set_done")
        bank_hs = [bank[0:2], bank[2:4]]
        b_tp, b_mm, b_tq, b_ov = bank[4], bank[5], bank[6], bank[7]
        tp16 = b_tp[:, :].bitcast(BF16).rearrange("p (c t) -> p c t", t=T)
        tq16 = b_tq[:, :].bitcast(BF16).rearrange("p (c t) -> p c t", t=T)

        with nc.Block() as block:
            @block.vector
            def _(dve):
                nc.vector.memset(ht1[:, :, :], 1.0).then_inc(set_done, 1)
                nc.vector.memset(at1[:, :, :], 1.0).then_inc(set_done, 1)
                nc.vector.memset(va[:, :, :, :], 0.0).then_inc(set_done, 1)
                nc.vector.memset(stack[:, :, :, :, :], 0.0).then_inc(set_done, 1)
                dve.wait_ge(set_done, 4)
                nc.vector.memset(va[:, :, :, DH:DH + 1], 1.0).then_inc(set_done, 1)
                nc.vector.memset(stack[:, :, 1, :, PIECES * DH:PIECES * DH + 2], 1.0).then_inc(set_done, 1)
                dve.wait_ge(set_done, 6)
                for l in range(L):
                    dve.wait_ge(w_in[l], 48)

        def attention(l):
            base = (l - 1) * B
            wq0, wq1 = w_main[l][:, 0:3 * D], w_tail[l][:, 0:3 * D]
            wp0, wp1 = w_main[l][:, 3 * D:4 * D], w_tail[l][:, 3 * D:4 * D]
            rms = l == 1

            def drive(eng, step):
                step(-1, 1, middle=False, tail=False)
                step(0, 0, tail=False)
                step(1, 1)
                with eng.Fori(0, (B - 4) // 2) as i:
                    step(i * 2 + 2, 0)
                    step(i * 2 + 3, 1)
                step(B - 2, 0)
                step(B - 1, 1, front=False)
                step(B, 0, front=False, middle=False)

            with nc.Block() as block:
                @block.sync
                def _(sp):
                    load_gates(sp, 2 * l + 1)

                @block.tensor
                def _(pe):
                    def step(b, u, front=True, middle=True, tail=True):
                        n = b + base
                        w = 1 - u
                        if middle:
                            pe.wait_ge(S["qs_done"], n + 1)
                            pe.wait_ge(S["ks_done"], n + 1)
                            for half in range(2):
                                if front and tail or not isinstance(b, int) or b or base:
                                    pe.wait_ge(S["exp_done"], n * 4 - 2 + 2 * half)
                                for h in range(8 * half, 8 * half + 8):
                                    r = slice(SLOT * (h % 2), SLOT * (h % 2) + PIECES * DH)
                                    last = nc.tensor.matmul(bank_hs[half][h % 2][:, (h % 8) // 2 * T:((h % 8) // 2 + 1) * T], qs[r, u, h // 2, :], ks[r, u, h // 2, :],
                                                            start=True, stop=True)
                                last.then_inc(S["s_mm"], 1)
                        if tail:
                            pe.wait_ge(S["ot_done"], n)
                            for g in range(4):
                                last = nc.tensor.transpose(b_ov[:, g * T:(g + 1) * T], ot[:, w, g * T:(g + 1) * T], ident[:, :])
                            last.then_inc(S["back_mm"], 1)
                        if front:
                            pe.wait_ge(S["hn_done"], n + 2)
                            if middle:
                                pe.wait_ge(S["ks_done"], n + 1)
                            nc.tensor.transpose(b_tp[:, 0:T], hn[:, w, 0:P], ident[:, :])
                            nc.tensor.transpose(b_tp[0:DT, T:2 * T], hn[:, w, P:D], ident[:, :]).then_inc(S["ht_mm"], 1)
                        if middle:
                            pe.wait_ge(S["neg_done"], 2 * n + 2)
                            for c in range(8):
                                last = nc.tensor.transpose(tq16[:, c, :], stack[:, u, 0, 2 * c:2 * c + 2, :].rearrange("p h s -> p (h s)"), identb[:, :])
                            last.then_inc(S["q2_mm"], 1)
                        if tail:
                            pe.wait_ge(S["at_done"], n)
                            if front:
                                pe.wait_ge(S["ht_done"], 2 * n + 4)
                            nc.tensor.transpose(b_tp[:, 0:T], at[:, w, 0:P], ident[:, :])
                            nc.tensor.transpose(b_tp[0:DT, T:2 * T], at[:, w, P:D], ident[:, :]).then_inc(S["at_mm"], 1)
                        if front:
                            pe.wait_ge(S["ht_done"], 2 * n + 4)
                            if tail:
                                pe.wait_ge(S["rest_done"], n + 1)
                                if not (isinstance(n, int) and n <= 1):
                                    pe.wait_ge(S["upd_done"], n - 1)
                            nc.tensor.matmul(b_mm[:, 0:3 * D], ht0[:, w, :], wq0, start=True, stop=False)
                            nc.tensor.matmul(b_mm[:, 0:3 * D], ht1[:, w, :], wq1, start=False, stop=True).then_inc(S["qkv_mm"], 1)
                        if middle:
                            pe.wait_ge(S["q2_done"], n + 1)
                            for half in range(2):
                                pe.wait_ge(S["max_done"], 2 * n + 1 + half)
                                for h in range(8 * half, 8 * half + 8):
                                    r = slice(SLOT * (h % 2), SLOT * (h % 2) + PIECES * DH + 2)
                                    last = nc.tensor.matmul(bank_hs[half][h % 2][:, (h % 8) // 2 * T:((h % 8) // 2 + 1) * T], ks[r, u, h // 2, :], qs[r, u, h // 2, :],
                                                            start=True, stop=True)
                                last.then_inc(S["st_mm"], 1)
                        if tail:
                            pe.wait_ge(S["at_ev"], 2 * n)
                            if front:
                                pe.wait_ge(S["rest_done"], n + 2)
                                pe.wait_ge(S["v_done"], n + 2)
                            nc.tensor.matmul(b_mm[:, 0:D], at0[:, w, :], wp0, start=True, stop=False)
                            nc.tensor.matmul(b_mm[:, 0:D], at1[:, w, :], wp1, start=False, stop=True).then_inc(S["proj_mm"], 1)
                        if front:
                            pe.wait_ge(S["low_done"], 2 * n + 4)
                            if middle:
                                pe.wait_ge(S["q2_done"], n + 1)
                            for c in range(8):
                                last = nc.tensor.transpose(tq16[:, c, :], stack[:, w, 0, 2 * c:2 * c + 2, :].rearrange("p h s -> p (h s)"), identb[:, :])
                            last.then_inc(S["qs_mm"], 1)
                            pe.wait_ge(S["ht_done"], 2 * n + 4)
                            if tail:
                                pe.wait_ge(S["at_ev"], 2 * n)
                            for c in range(8):
                                last = nc.tensor.transpose(tp16[:, c, :], stack[:, w, 1, 2 * c:2 * c + 2, :].rearrange("p h s -> p (h s)"), identb[:, :])
                            last.then_inc(S["ks_mm"], 1)
                        if middle:
                            if tail:
                                pe.wait_ge(S["at_done"], n)
                            for h in range(H):
                                if h % 8 == 0:
                                    pe.wait_ge(S["exp_done"], n * 4 + 2 + h // 4)
                                r = 32 * (h % 4)
                                last = nc.tensor.matmul(b_ov[r:r + 32, (h // 4) * T:(h // 4 + 1) * T], va[:, u, h, :], pt[:, u, h, :], start=True, stop=True)
                            last.then_inc(S["pv_mm"], 1)

                    drive(nc.tensor, step)

                @block.scalar
                def _(act):
                    def step(b, u, front=True, middle=True, tail=True):
                        n = b + base
                        w = 1 - u
                        if tail:
                            act.wait_ge(S["pv_mm"], n)
                            nc.scalar.copy(ot[:, w, :], b_ov[:, :]).then_inc(S["ot_done"], 1)
                            act.wait_ge(S["at_mm"], n)
                            nc.scalar.copy(at0[:, w, :], b_tp[:, 0:T]).then_inc(S["at_ev"], 1)
                            nc.scalar.copy(at1[0:DT, w, :], b_tp[0:DT, T:2 * T]).then_inc(S["at_ev"], 1)
                        if front:
                            act.wait_ge(S["qkv_mm"], n + 2)
                            nc.scalar.copy(va[:, w, :, 0:DH], b_mm[:, 2 * D:3 * D].rearrange("p (h d) -> p h d", d=DH)).then_inc(S["v_done"], 1)
                            src = b_mm[:, 0:2 * D]
                            if rms:
                                act.wait_ge(S["v_done"], n + 2)
                                nc.scalar.activation(sq[:, :], src, ACT.Square).then_inc(S["square_done"], 1)
                                act.wait_ge(S["qkn_done"], n + 2 - base)
                                src = qk[:, :]
                            src = src.rearrange("p (s h d) -> p s h d", s=2, d=DH)
                            for s, first, by in ((0, 1, 2), (1, 0, 1)):
                                dst = stack[:, w, s, :, 0:PIECES * DH].rearrange("p h (c d) -> p h c d", d=DH)
                                dst = dst[:, :, first::2, :] if by == 2 else dst[:, :, 0:3, :]
                                nc.scalar.copy(dst, src[:, s].unsqueeze(2).to_broadcast([P, H, 3, DH])).then_inc(S["high_done"], 1)
                            act.wait_ge(S["rest_done"], n + 2)
                            less = rest[:, :].rearrange("p (s h d) -> p s h d", s=2, d=DH)
                            for s in range(2):
                                dst = stack[:, w, s, :, 0:PIECES * DH].rearrange("p h (c d) -> p h c d", d=DH)
                                dst = dst[:, :, 2::2, :] if s == 0 else dst[:, :, 3:5, :]
                                nc.scalar.copy(dst, less[:, s].unsqueeze(2).to_broadcast([P, H, 2, DH])).then_inc(S["midp_done"], 1)
                        if middle:
                            for c in range(4):
                                act.wait_ge(S["st_mm"], 2 * n + 1 + c // 2)
                                nc.scalar.activation(pt[:, u, 8 * (c // 2) + c % 2:8 * (c // 2) + 8:2, :], bank[c][:, :].rearrange("p (h t) -> p h t", t=T), ACT.Exp, scale=SM).then_inc(S["exp_done"], 1)
                        if front:
                            act.wait_ge(S["ks_mm"], n + 2)
                            nc.scalar.copy(ks[:, w, :, :], tp16).then_inc(S["ks_done"], 1)

                    drive(nc.scalar, step)

                @block.gpsimd
                def _(pool):
                    def step(b, u, front=True, middle=True, tail=True):
                        n = b + base
                        w = 1 - u
                        if front and rms:
                            pool.wait_ge(S["ssum_done"], n + 2 - base)
                            nc.gpsimd.tensor_tensor(ssum[:, :], ssum[:, :], mhalf[:, :].to_broadcast([P, 2 * H]), ALU.pow).then_inc(S["rq_done"], 1)
                        if tail:
                            pool.wait_ge(S["var_new"], n)
                            nc.gpsimd.tensor_tensor(rstd_all[:, bass.ds(b - 1, 1)], var_all[:, bass.ds(b - 1, 1)], mhalf[:, :], ALU.pow).then_inc(S["rstd_new"], 1)

                    drive(nc.gpsimd, step)
                    pool.wait_ge(S["rstd_new"], base + B)

                @block.vector
                def _(dve):
                    def step(b, u, front=True, middle=True, tail=True):
                        n = b + base
                        w = 1 - u
                        if front:
                            nb = b + 1
                            if rms:
                                nc.vector.tensor_scalar(hn[:, w, :], x_all[:, nb, :], rstd_all[:, bass.ds(nb, 1)], gain[:, 0:1], ALU.mult, ALU.mult).then_inc(S["hn_done"], 1)
                            else:
                                nc.vector.tensor_scalar(hn[:, w, :], x_all[:, nb, :], mean_all[:, bass.ds(nb, 1)], rstd_all[:, bass.ds(nb, 1)], ALU.subtract, ALU.mult).then_inc(S["hn_done"], 1)
                        if middle:
                            for half in range(2):
                                dve.wait_ge(S["s_mm"], 2 * n + 1 + half)
                                for c in range(2):
                                    last = nc.vector.tensor_reduce(rmax[:, 8 * half + c:8 * half + 8:2], bank_hs[half][c][:, :].rearrange("p (h t) -> p h t", t=T), AX.X, ALU.max)
                                last.then_inc(S["max_done"], 1)
                            dve.wait_ge(S["max_done"], 2 * n + 2)
                            c0 = PIECES * DH
                            nc.vector.tensor_scalar(stack[:, u, 0, :, c0], rmax[:, :], -1.0, None, ALU.mult).then_inc(S["neg_done"], 1)
                            dve.wait_ge(S["neg_done"], 2 * n + 1)
                            nc.vector.scalar_tensor_tensor(out=stack[:, u, 0, :, c0 + 1], in0=rmax[:, :], scalar=-1.0, in1=stack[:, u, 0, :, c0], op0=ALU.mult, op1=ALU.subtract).then_inc(S["neg_done"], 1)
                        if tail:
                            dve.wait_ge(S["back_mm"], n)
                            heads = b_ov[:, :].rearrange("p (h s) -> p h s", s=32)
                            nc.vector.reciprocal(rsum[:, :], heads[:, :, DH]).then_inc(S["rsum_done"], 1)
                            dve.wait_ge(S["rsum_done"], n)
                            nc.vector.tensor_tensor(at[:, w, :].rearrange("p (h d) -> p h d", d=DH), heads[:, :, 0:DH], rsum[:, :].unsqueeze(2).to_broadcast([P, H, DH]), ALU.mult).then_inc(S["at_done"], 1)
                        if front:
                            dve.wait_ge(S["ht_mm"], n + 2)
                            nc.vector.tensor_scalar(ht0[:, w, :], b_tp[:, 0:T], mod[:, l, 1, bass.ds(nb, 1)], mod[:, l, 0, bass.ds(nb, 1)], ALU.mult, ALU.add).then_inc(S["ht_done"], 1)
                            nc.vector.tensor_scalar(ht1[0:DT, w, :], b_tp[0:DT, T:2 * T], modt[:, l, 1, bass.ds(nb, 1)], modt[:, l, 0, bass.ds(nb, 1)], ALU.mult, ALU.add).then_inc(S["ht_done"], 1)
                        if middle:
                            dve.wait_ge(S["q2_mm"], n + 1)
                            nc.vector.tensor_copy(qs[:, u, :, :], tq16).then_inc(S["q2_done"], 1)
                        if front:
                            if rms:
                                m = n + 2 - base
                                dve.wait_ge(S["square_done"], m)
                                nc.vector.tensor_reduce(ssum[:, :], sq[:, :].rearrange("p (g d) -> p g d", d=DH), AX.X, ALU.add).then_inc(S["gain_step"], 1)
                                dve.wait_ge(S["gain_step"], m * 3 - 2)
                                nc.vector.tensor_scalar(ssum[:, :], ssum[:, :], 1e-24, None, ALU.max).then_inc(S["ssum_done"], 1)
                                dve.wait_ge(S["rq_done"], m)
                                for s in range(2):
                                    nc.vector.tensor_scalar(ssum[:, s * H:(s + 1) * H], ssum[:, s * H:(s + 1) * H], gain[:, 2 + s:3 + s], DH ** 0.5, ALU.mult, ALU.mult).then_inc(S["gain_step"], 1)
                                dve.wait_ge(S["gain_step"], m * 3)
                                nc.vector.tensor_tensor(qk[:, :].rearrange("p (g d) -> p g d", d=DH), b_mm[:, 0:2 * D].rearrange("p (g d) -> p g d", d=DH),
                                                        ssum[:, :].unsqueeze(2).to_broadcast([P, 2 * H, DH]), ALU.mult).then_inc(S["qkn_done"], 1)
                            dve.wait_ge(S["high_done"], 2 * n + 4)
                            src = qk[:, :] if rms else b_mm[:, 0:2 * D]
                            pieces = stack[:, w, :, :, 0:PIECES * DH].rearrange("p s h (c d) -> p s h c d", d=DH)
                            r4 = rest[:, :].rearrange("p (s h d) -> p s h d", s=2, d=DH)
                            nc.vector.tensor_tensor(r4, src.rearrange("p (s h d) -> p s h d", s=2, d=DH), pieces[:, :, :, 1, :], ALU.subtract).then_inc(S["rest_done"], 1)
                            dve.wait_ge(S["midp_done"], 2 * n + 4)
                            for s in range(2):
                                nc.vector.tensor_tensor(pieces[:, s, :, 5 * s, :], r4[:, s], pieces[:, s, :, 4, :], ALU.subtract).then_inc(S["low_done"], 1)
                        if tail:
                            pb = b - 1
                            dve.wait_ge(S["proj_mm"], n)
                            nc.vector.tensor_tensor(upd[:, w, :], b_mm[:, 0:D], gate_all[:, 0, pb, :], ALU.mult).then_inc(S["upd_done"], 1)
                            dve.wait_ge(S["upd_done"], n)
                            nc.vector.tensor_tensor(x_all[:, pb, :], x_all[:, pb, :], upd[:, w, :], ALU.add).then_inc(S["x_new"], 1)
                            dve.wait_ge(ones_ready, 1)
                            dve.wait_ge(S["x_new"], n)
                            nc.vector.bn_stats(stats[:, w, :], x_all[:, pb, :]).then_inc(S["stat_done"], 1)
                        if front:
                            dve.wait_ge(S["qs_mm"], n + 2)
                            nc.vector.tensor_copy(qs[:, w, :, :], tq16).then_inc(S["qs_done"], 1)
                        if tail:
                            dve.wait_ge(ones_ready, 1)
                            dve.wait_ge(S["stat_done"], n)
                            nc.vector.bn_aggr(aggr[:, w, :], stats[:, w, :]).then_inc(S["aggr_done"], 1)
                            dve.wait_ge(S["aggr_done"], n)
                            variance(dve, l == 1, aggr[:, w], pb, S["var_new"], S["ms_done"], b - 1)
                    drive(nc.vector, step)
                    dve.wait_ge(S["var_new"], base + B)


        def mlp(l):
            experts = E if l == 2 else 1
            phase = 2 * l + 1
            rms = l == 1
            gelu = ACT.Gelu if l == 0 else ACT.Gelu_apprx_tanh
            off = 3 * D + D + (E if l == 2 else 0)
            off2 = off + experts * HID
            groups = B // G
            with ExitStack() as c:
                def tsb(name, shape, dt=F32):
                    return c.enter_context(nc.sbuf_tensor(f"m{l}_{name}", shape, dt))

                hn = tsb("hn", [P, G, D])
                h0 = tsb("h0", [P, 2, G * T])
                h1 = tsb("h1", [DT + 1, 2, G * T])
                hid = tsb("hid", [P, 2, MT, G * T])
                upd = tsb("upd", [P, G, D])
                st = tsb("st", [P, G, 6])
                ag = tsb("ag", [P, G, 2])
                lg = tsb("lg", [P, G, E])
                cmp = tsb("cmp", [P, G, E, E])
                cmp2 = tsb("cmp2", [P, G, E, E])
                sel = tsb("sel", [P, G, E])
                wts = tsb("wts", [P, 2, G, E])
                tops = tsb("tops", [P, G])
                below = tsb("below", [P, E, E])
                names = "set hn_done h_mm h_done fc1_mm gelu_done fc2_mm upd_done x_new ".split()
                names += ("stat_done aggr_done var_new rstd_new" + " ms_done" * (l == 0) if l < 2 else
                          "lg_mm lg_done route exp_done sel_done wts_done gated stored").split()
                S = {k: sem(f"m{l}_" + k) for k in names}
                b_h0, b_h1, b_lg = bank[0], bank[1], bank[1]
                b_fc1 = [bank[2], bank[3], bank[4], bank[5]]
                b_fc2 = [bank[6], bank[7]]

                def drive(eng, step):
                    step(-1, 1, products=False)
                    step(0, 0)
                    with eng.Fori(0, (groups - 2) // 2) as i:
                        step(i * 2 + 1, 1)
                        step(i * 2 + 2, 0)
                    step(groups - 1, 1, front=False)

                def width(m):
                    return P if m < MT - 1 else HL

                with nc.Block() as block:
                    @block.tensor
                    def _(pe):
                        def step(g, u, front=True, products=True):
                            w = 1 - u

                            def fc1(e):
                                for m in range(MT):
                                    t_done = (g * experts + e) * MT + m
                                    if not isinstance(g, int) or t_done >= 4:
                                        pe.wait_ge(S["set"], 2)
                                        pe.wait_ge(S["gelu_done"], t_done - 3)
                                    o = off + e * HID + m * P
                                    dst = b_fc1_of(t_done_mod(g, u, e, m))[0:width(m), :]
                                    nc.tensor.matmul(dst, w_main[l][:, o:o + width(m)], h0[:, u, :], start=True, stop=False)
                                    nc.tensor.matmul(dst, w_tail[l][:, o:o + width(m)], h1[:, u, :], start=False, stop=True).then_inc(S["fc1_mm"], 1)

                            def fc2(e):
                                pe.wait_ge(S["gelu_done"], (g * experts + e + 1) * MT)
                                if not isinstance(g, int) or g or e:
                                    pe.wait_ge(S["upd_done"], (g * experts + e) * 2)
                                for s in range(G):
                                    for m in range(MT):
                                        k = P if m < MT - 1 else HL + 1
                                        wt = w_main[l][:, off2 + (e * 4 + m) * D:off2 + (e * 4 + m + 1) * D] if m < MT - 1 else w_last[l][:, e * D:(e + 1) * D]
                                        mm = nc.tensor.matmul(b_fc2[s // 2][:, (s % 2) * D:(s % 2 + 1) * D], hid[0:k, e % 2 if experts > 1 else u, m, s * T:(s + 1) * T], wt,
                                                              start=(m == 0), stop=(m == MT - 1))
                                    if s % 2:
                                        mm.then_inc(S["fc2_mm"], 1)

                            if products:
                                pe.wait_ge(S["h_done"], g * 2 * G + 2 * G)
                                fc1(0)
                                for e in range(1, experts):
                                    fc1(e)
                                    fc2(e - 1)
                            if front:
                                pe.wait_ge(S["hn_done"], g * G + 2 * G)
                                for s in range(G):
                                    nc.tensor.transpose(b_h0[:, s * T:(s + 1) * T], hn[:, s, 0:P], ident[:, :])
                                for s in range(G):
                                    if s == 0 and l == 2 and products:
                                        pe.wait_ge(S["lg_done"], g + 1)
                                    mm = nc.tensor.transpose(b_h1[0:DT, s * T:(s + 1) * T], hn[:, s, P:D], ident[:, :])
                                mm.then_inc(S["h_mm"], 1)
                            if products:
                                fc2(experts - 1)
                            if front and l == 2:
                                pe.wait_ge(S["set"], 2)
                                pe.wait_ge(S["h_done"], g * 2 * G + 4 * G)
                                for s in range(G):
                                    nc.tensor.matmul(b_lg[:, s * E:(s + 1) * E], h0[:, w, s * T:(s + 1) * T], w_main[2][:, off - E:off], start=True, stop=False)
                                    mm = nc.tensor.matmul(b_lg[:, s * E:(s + 1) * E], h1[:, w, s * T:(s + 1) * T], w_tail[2][:, off - E:off], start=False, stop=True)
                                mm.then_inc(S["lg_mm"], 1)

                        def t_done_mod(g, u, e, m):
                            return (u * experts * MT + e * MT + m) % 4 if (2 * experts * MT) % 4 == 0 else (u * 2 + m) % 4

                        def b_fc1_of(j):
                            return b_fc1[j]

                        drive(nc.tensor, step)

                    @block.scalar
                    def _(act):
                        def step(g, u, front=True, products=True):
                            w = 1 - u
                            if products:
                                for e in range(experts):
                                    for m in range(MT):
                                        tile = (g * experts + e) * MT + m
                                        j = (u * experts * MT + e * MT + m) % 4 if (2 * experts * MT) % 4 == 0 else (u * 2 + m) % 4
                                        if m == 0:
                                            if experts > 1 and (not isinstance(g, int) or g * experts + e >= 2):
                                                act.wait_ge(S["set"], 2)
                                                act.wait_ge(S["fc2_mm"], (g * experts + e) * 2 - 2)
                                            elif experts == 1 and (not isinstance(g, int) or g >= 1):
                                                act.wait_ge(S["fc2_mm"], g * 2)
                                        act.wait_ge(S["fc1_mm"], tile + 1)
                                        nc.scalar.activation(hid[0:width(m), e % 2 if experts > 1 else u, m, :], b_fc1[j][0:width(m), :], gelu).then_inc(S["gelu_done"], 1)
                            if front and l == 2:
                                act.wait_ge(S["route"], g + 2)
                                nc.scalar.activation(wts[:, w, :, :], lg[:, :, :], ACT.Exp).then_inc(S["exp_done"], 1)

                        drive(nc.scalar, step)

                    @block.gpsimd
                    def _(pool):
                        def step(g, u, front=True, products=True):
                            if products:
                                pool.wait_ge(S["var_new"], g * G + G)
                                nc.gpsimd.tensor_tensor(rstd_all[:, bass.ds(g * G, G)], var_all[:, bass.ds(g * G, G)], mhalf[:, :].to_broadcast([P, G]), ALU.pow).then_inc(S["rstd_new"], 1)

                        if l < 2:
                            drive(nc.gpsimd, step)
                            pool.wait_ge(S["rstd_new"], groups)

                    @block.sync
                    def _(sp):
                        if l < 2:
                            load_gates(sp, phase + 1)
                        else:
                            def step(g, u, front=True, products=True):
                                if products:
                                    sp.wait_ge(S["x_new"], g + 1)
                                    sp.dma_start(t["out"][bass.ds(g * G, G)].rearrange("b t d -> t b d"), x_all[:, bass.ds(g * G, G), :]).then_inc(S["stored"], 16)

                            drive(nc.sync, step)
                            sp.wait_ge(S["stored"], groups * 16)

                    @block.vector
                    def _(dve):
                        def step(g, u, front=True, products=True):
                            w = 1 - u
                            if front:
                                for s in range(G):
                                    q = g * G + G + s
                                    if products and s == 0:
                                        dve.wait_ge(S["h_mm"], g + 1)
                                    if l == 1:
                                        nc.vector.tensor_scalar(hn[:, s, :], x_all[:, q, :], rstd_all[:, bass.ds(q, 1)], gain[:, 1:2], ALU.mult, ALU.mult).then_inc(S["hn_done"], 1)
                                    else:
                                        nc.vector.tensor_scalar(hn[:, s, :], x_all[:, q, :], mean_all[:, bass.ds(q, 1)], rstd_all[:, bass.ds(q, 1)], ALU.subtract, ALU.mult).then_inc(S["hn_done"], 1)

                            def take(e):
                                for half in range(2):
                                    dve.wait_ge(S["fc2_mm"], (g * experts + e) * 2 + 1 + half)
                                    if experts == 1:
                                        nc.vector.tensor_tensor(upd[:, 2 * half:2 * half + 2, :], b_fc2[half][:, 0:2 * D].rearrange("p (s d) -> p s d", d=D),
                                                                gate_all[:, 1, bass.ds(g * G + 2 * half, 2), :], ALU.mult).then_inc(S["upd_done"], 1)
                                        continue
                                    for s in range(2 * half, 2 * half + 2):
                                        src = b_fc2[half][:, (s % 2) * D:(s % 2 + 1) * D]
                                        if e == 0:
                                            if s == 0:
                                                dve.wait_ge(S["wts_done"], g + 1)
                                            mm = nc.vector.tensor_scalar(upd[:, s, :], src, wts[:, u, s, e:e + 1], None, ALU.mult)
                                        else:
                                            if s == 2 * half:
                                                dve.wait_ge(S["upd_done"], (g * experts + e) * 2 + half - 1)
                                            mm = nc.vector.scalar_tensor_tensor(out=upd[:, s, :], in0=src, scalar=wts[:, u, s, e:e + 1], in1=upd[:, s, :], op0=ALU.mult, op1=ALU.add)
                                    mm.then_inc(S["upd_done"], 1)

                            if products:
                                for e in range(experts - 1):
                                    take(e)
                            if front:
                                dve.wait_ge(S["h_mm"], g + 2)
                                for s in range(G):
                                    q = g * G + G + s
                                    nc.vector.tensor_scalar(h0[:, w, s * T:(s + 1) * T], b_h0[:, s * T:(s + 1) * T], mod[:, l, 3, bass.ds(q, 1)], mod[:, l, 2, bass.ds(q, 1)], ALU.mult, ALU.add).then_inc(S["h_done"], 1)
                                for s in range(G):
                                    q = g * G + G + s
                                    nc.vector.tensor_scalar(h1[0:DT, w, s * T:(s + 1) * T], b_h1[0:DT, s * T:(s + 1) * T], modt[:, l, 3, bass.ds(q, 1)], modt[:, l, 2, bass.ds(q, 1)], ALU.mult, ALU.add).then_inc(S["h_done"], 1)
                            if products:
                                take(experts - 1)
                                xs = x_all[:, bass.ds(g * G, G), :]
                                dve.wait_ge(S["upd_done"], (g * experts + experts) * 2)
                                if experts > 1:
                                    nc.vector.tensor_tensor(upd[:, :, :], upd[:, :, :], gate_all[:, 1, bass.ds(g * G, G), :], ALU.mult).then_inc(S["gated"], 1)
                                    dve.wait_ge(S["gated"], g + 1)
                                nc.vector.tensor_tensor(xs, xs, upd[:, :, :], ALU.add).then_inc(S["x_new"], 1)
                                if l < 2:
                                    dve.wait_ge(ones_ready, 1)
                                    dve.wait_ge(S["x_new"], g + 1)
                                    for s in range(G):
                                        mm = nc.vector.bn_stats(st[:, s, :], x_all[:, g * G + s, :])
                                    mm.then_inc(S["stat_done"], 1)
                                    dve.wait_ge(ones_ready, 1)
                                    dve.wait_ge(S["stat_done"], g + 1)
                                    for s in range(G):
                                        mm = nc.vector.bn_aggr(ag[:, s, :], st[:, s, :])
                                    mm.then_inc(S["aggr_done"], 1)
                                    dve.wait_ge(S["aggr_done"], g + 1)
                                    for s in range(G):
                                        variance(dve, l == 0, ag[:, s], g * G + s, S["var_new"], S.get("ms_done"), g * G + s)
                            if front and l == 2:
                                dve.wait_ge(S["lg_mm"], g + 2)
                                nc.vector.tensor_copy(lg[:, :, :], b_lg[:, 0:G * E].rearrange("p (s e) -> p s e", e=E)).then_inc(S["lg_done"], 1)
                                dve.wait_ge(S["lg_done"], g + 2)
                                other = lg[:, :, :].unsqueeze(2).to_broadcast([P, G, E, E])
                                own = lg[:, :, :].unsqueeze(3).to_broadcast([P, G, E, E])
                                step_of = (g + 1) * 9
                                nc.vector.tensor_tensor(cmp[:, :, :, :], other, own, ALU.is_gt).then_inc(S["sel_done"], 1)
                                nc.vector.tensor_tensor(cmp2[:, :, :, :], other, own, ALU.is_equal).then_inc(S["sel_done"], 1)
                                nc.vector.tensor_reduce(tops[:, :], lg[:, :, :], AX.X, ALU.max).then_inc(S["sel_done"], 1)
                                dve.wait_ge(S["sel_done"], step_of + 3)
                                nc.vector.tensor_tensor(cmp2[:, :, :, :], cmp2[:, :, :, :], below[:, :, :].unsqueeze(1).to_broadcast([P, G, E, E]), ALU.mult).then_inc(S["sel_done"], 1)
                                nc.vector.tensor_tensor(lg[:, :, :], lg[:, :, :], tops[:, :].unsqueeze(2).to_broadcast([P, G, E]), ALU.subtract).then_inc(S["route"], 1)
                                dve.wait_ge(S["sel_done"], step_of + 4)
                                nc.vector.tensor_tensor(cmp[:, :, :, :], cmp[:, :, :, :], cmp2[:, :, :, :], ALU.add).then_inc(S["sel_done"], 1)
                                dve.wait_ge(S["sel_done"], step_of + 5)
                                nc.vector.tensor_reduce(sel[:, :, :], cmp[:, :, :, :], AX.X, ALU.add).then_inc(S["sel_done"], 1)
                                dve.wait_ge(S["sel_done"], step_of + 6)
                                dve.wait_ge(S["exp_done"], g + 2)
                                nc.vector.scalar_tensor_tensor(out=wts[:, w, :, :], in0=sel[:, :, :], scalar=1.5, in1=wts[:, w, :, :], op0=ALU.is_lt, op1=ALU.mult).then_inc(S["sel_done"], 1)
                                dve.wait_ge(S["sel_done"], step_of + 7)
                                nc.vector.tensor_reduce(tops[:, :], wts[:, w, :, :], AX.X, ALU.add).then_inc(S["sel_done"], 1)
                                dve.wait_ge(S["sel_done"], step_of + 8)
                                nc.vector.reciprocal(tops[:, :], tops[:, :]).then_inc(S["sel_done"], 1)
                                dve.wait_ge(S["sel_done"], step_of + 9)
                                nc.vector.tensor_tensor(wts[:, w, :, :], wts[:, w, :, :], tops[:, :].unsqueeze(2).to_broadcast([P, G, E]), ALU.mult).then_inc(S["wts_done"], 1)

                        nc.vector.memset(h1[:, :, :], 1.0).then_inc(S["set"], 1)
                        nc.vector.memset(hid[:, :, MT - 1, :], 1.0).then_inc(S["set"], 1)
                        if l == 2:
                            nc.vector.memset(below[:, :, :], 0.0).then_inc(S["set"], 1)
                            dve.wait_ge(S["set"], 3)
                            for e in range(1, E):
                                nc.vector.memset(below[:, e, 0:e], 1.0).then_inc(S["set"], 1)
                            dve.wait_ge(S["set"], 3 + E - 1)
                        else:
                            dve.wait_ge(S["set"], 2)
                        drive(nc.vector, step)
                        if l == 2:
                            dve.wait_ge(S["x_new"], groups)
                        else:
                            dve.wait_ge(S["var_new"], B)

        mlp(0)
        attention(1)
        mlp(1)
        attention(2)
        mlp(2)


def lay_out(x):
    def wb(w, b):
        return np.concatenate([w, b[None]], 0)

    def fc2(w, b):
        main = w[:4 * P].reshape(4, P, D).transpose(1, 0, 2).reshape(P, 4 * D)
        return main, np.concatenate([w[4 * P:], b[None]], 0)

    a = {"x": x["x"], "cond": x["cond_1152"], "pt": x["L0_cond_P"].T}
    iu, ju = np.triu_indices(R, 1)
    skew = np.zeros((D + 1, R, R), np.float32)
    for i, j in ((iu, ju), (ju, iu)):
        skew[:D, i, j] = x["L0_cond_W"].T
        skew[D, i, j] = x["L0_cond_b"]
    a["skew"] = skew.reshape(D + 1, R * R)
    sign = np.sign(np.arange(R)[None, :] - np.arange(R)[:, None]).astype(np.float32)
    a["sign"] = np.concatenate([sign, sign], 0)
    a["ident"] = np.eye(P, dtype=np.float32)
    a["gains"] = np.concatenate([x["L2_cond_g1"], x["L2_cond_g2"], x["L2_cond_qg"], x["L2_cond_kg"]])
    a["ada"] = np.stack([wb(x["L1_cond_ada_w"], x["L1_cond_ada_b"]), wb(x["L2_cond_ada_w"].T, x["L2_cond_ada_b"]),
                         wb(x["L3_cond_w_adaln"], x["L3_cond_b_adaln"])])
    for l, (qkv, proj, fc1, f2) in enumerate((
        (wb(x["L1_cond_qkv_w"], x["L1_cond_qkv_b"]), wb(x["L1_cond_proj_w"], x["L1_cond_proj_b"]),
         [wb(x["L1_cond_fc1_w"], x["L1_cond_fc1_b"])], [fc2(x["L1_cond_fc2_w"], x["L1_cond_fc2_b"])]),
        (wb(x["L2_cond_qkv_w"].T, x["L2_cond_qkv_b"]), wb(x["L2_cond_proj_w"].T, x["L2_cond_proj_b"]),
         [wb(x["L2_cond_fc1_w"].T, x["L2_cond_fc1_b"])], [fc2(x["L2_cond_fc2_w"].T, x["L2_cond_fc2_b"])]),
        (wb(x["L3_cond_w_qkv"], x["L3_cond_b_qkv"]), wb(x["L3_cond_w_proj"], x["L3_cond_b_proj"]),
         [wb(x["L3_cond_w_gate"], np.zeros(E, np.float32))] + [wb(x["L3_cond_w1"][e], x["L3_cond_b1"][e]) for e in range(E)],
         [fc2(x["L3_cond_w2"][e], x["L3_cond_b2"][e]) for e in range(E)]),
    )):
        first = np.concatenate([qkv, proj] + fc1, 1)
        a[f"main{l}"] = np.concatenate([first[:P]] + [m for m, _ in f2], 1)
        a[f"tail{l}"] = first[P:]
        a[f"last{l}"] = np.concatenate([m for _, m in f2], 1)
    return {k: np.ascontiguousarray(v) for k, v in a.items()}


def kernel(**inputs):
    import concourse.bacc as bacc
    from concourse.bass_utils import run_bass_kernel_spmd

    nc = bacc.Bacc("TRN2", target_bir_lowering=False, num_devices=1)
    arrays = lay_out({k: np.asarray(v) for k, v in inputs.items()})
    tensors = {k: nc.dram_tensor("in_" + k, a.shape, mybir.dt.from_np(a.dtype), kind="ExternalInput").ap() for k, a in arrays.items()}
    tensors["out"] = nc.dram_tensor("out", [B, T, D], F32, kind="ExternalOutput").ap()
    program(nc, tensors)
    r = run_bass_kernel_spmd(nc, [{"in_" + k: a for k, a in arrays.items()}], core_ids=[0])
    return r.results[0]["out"]
```

```python
from contextlib import ExitStack

import numpy as np
import concourse.bass as bass
from concourse import mybir

F32 = mybir.dt.float32
BF16 = mybir.dt.bfloat16
ACT = mybir.ActivationFunctionType
ALU = mybir.AluOpType
AX = mybir.AxisListType

P = 128
B = 32
T = 128
D = 144
DT = D - P
H = 16
DH = D // H
HID = 4 * D
MT = 5
HL = HID - 4 * P
R = 64
E = 4
L = 3
G = 4
PAIRS = B // 2
SLOT = 64
PIECES = 6
DOUBLINGS = 10
SM = DH ** -0.5

EXPERTS = [1, 1, E]
GATE_W = [0, 0, E]
MAIN_W = [3 * D + D + GATE_W[l] + EXPERTS[l] * (HID + 4 * D) for l in range(L)]
TAIL_W = [3 * D + D + GATE_W[l] + EXPERTS[l] * HID for l in range(L)]
LAST_W = [D, D, E * D]


def program(nc, t):
    ctx = ExitStack()
    with ctx:
        def sb(name, shape, dt=F32):
            return ctx.enter_context(nc.sbuf_tensor(name, shape, dt))

        def sem(name):
            return ctx.enter_context(nc.semaphore(name))

        bank = [ctx.enter_context(nc.psum_tensor(f"bank{i}", [P, 512], F32)) for i in range(8)]

        x_all = sb("x_all", [P, B, D])
        gate_all = sb("gate_all", [P, 2, B, D])
        ident = sb("ident", [P, P])
        identb = sb("identb", [P, P], BF16)
        w_main = [sb(f"w_main{l}", [P, MAIN_W[l]]) for l in range(L)]
        w_tail = [sb(f"w_tail{l}", [DT + 1, TAIL_W[l]]) for l in range(L)]
        w_last = [sb(f"w_last{l}", [HL + 1, LAST_W[l]]) for l in range(L)]
        mod = sb("mod", [P, L, 4, B])
        modt = sb("modt", [DT, L, 4, B])
        mean_all = sb("mean_all", [P, B])
        rstd_all = sb("rstd_all", [P, B])
        var_all = sb("var_all", [P, B])
        stats = sb("stats", [P, 2, 6])
        aggr = sb("aggr", [P, 2, 2])
        mhalf = sb("mhalf", [P, 1])
        phalf = sb("phalf", [P, 1])
        zero = sb("zero", [P, 1])
        gain = sb("gain", [P, 4])

        consts_in = sem("consts_in")
        w_in = [sem(f"w_in{l}") for l in range(L)]
        ones_ready = sem("ones_ready")
        gates_in = sem("gates_in")
        gates_out = sem("gates_out")
        scratch = nc.dram_tensor("gates_dram", [L * 2, B, D], F32, kind="Internal").ap()
        araw_dram = nc.dram_tensor("araw_dram", [B, R, R], F32, kind="Internal").ap()

        def load_gates(eng, phase):
            src = bass.AP(tensor=scratch.tensor, offset=phase * B * D, ap=[[0, P], [1, B * D]])
            eng.dma_start(gate_all[:, phase % 2].rearrange("p b d -> p (b d)"), src).then_inc(gates_in, 16)
            eng.wait_ge(gates_in, 16 * (phase + 1))

        adapter = ExitStack()
        with adapter:
            def asb(name, shape, dt=F32):
                return adapter.enter_context(nc.sbuf_tensor(name, shape, dt))

            qt = asb("qt", [P, D])
            u0 = asb("u0", [P, R])
            u1 = asb("u1", [DT, R])
            ex = asb("ex", [P, PAIRS, R])
            ey = asb("ey", [P, PAIRS, R])

            with ExitStack() as c:
                def tsb(name, shape, dt=F32):
                    return c.enter_context(nc.sbuf_tensor(name, shape, dt))

                def tsem(name):
                    return c.enter_context(nc.semaphore(name))

                cond = tsb("cond", [B, D])
                th = tsb("th", [B, D])
                sil = tsb("sil", [B, D])
                sc0 = tsb("sc0", [P, B])
                sc1 = tsb("sc1", [DT + 1, B])
                ada0 = tsb("ada0", [P, L, 6 * D])
                ada1 = tsb("ada1", [DT + 1, L, 6 * D])
                sk0 = tsb("sk0", [P, R * R])
                sk1 = tsb("sk1", [DT + 1, R * R])
                araw = tsb("araw", [B, R * R])
                gates = tsb("gates", [B, L * 2, D])
                sign = tsb("sign", [P, R])
                cond_in = tsem("cond_in")
                ada_in = tsem("ada_in")
                skew_in = tsem("skew_in")
                th_done = tsem("th_done")
                sil_done = tsem("sil_done")
                sct_done = tsem("sct_done")
                sc_done = tsem("sc_done")
                ones_set = ones_ready
                ada_done = tsem("ada_done")
                gate_mm = tsem("gate_mm")
                gate_ev = tsem("gate_ev")
                mod_ev = tsem("mod_ev")
                raw_mm = tsem("raw_mm")
                raw_ev_act = tsem("raw_ev_act")
                raw_ev_dve = tsem("raw_ev_dve")
                raw_out = tsem("raw_out")
                raw_back = tsem("raw_back")

                with nc.Block() as block:
                    @block.sync
                    def _(sp):
                        sp.dma_start(ident[:, :], t["ident"]).then_inc(consts_in, 16)
                        sp.dma_start(cond[:, :], t["cond"]).then_inc(cond_in, 16)
                        sp.dma_start(sign[:, :], t["sign"]).then_inc(consts_in, 16)
                        sp.dma_start(qt[0:R, :], t["pt"]).then_inc(consts_in, 16)
                        for j in range(4):
                            sp.dma_start(gain[:, j:j + 1], bass.AP(tensor=t["gains"].tensor, offset=j, ap=[[0, P], [1, 1]])).then_inc(consts_in, 16)
                        sp.dma_start(ada0[:, :, :], t["ada"][:, 0:P].rearrange("l k n -> k l n")).then_inc(ada_in, 16)
                        sp.dma_start(ada1[:, :, :], t["ada"][:, P:].rearrange("l k n -> k l n")).then_inc(ada_in, 16)
                        sp.dma_start(x_all[:, :, :], t["x"].rearrange("b t d -> t b d")).then_inc(consts_in, 16)
                        sp.wait_ge(raw_ev_act, 4)
                        sp.wait_ge(raw_ev_dve, 4)
                        sp.dma_start(araw_dram.rearrange("b i j -> b (i j)"), araw[:, :]).then_inc(raw_out, 16)
                        sp.wait_ge(raw_out, 16)
                        halves = araw_dram.rearrange("(q h) i j -> h i q j", h=2)
                        for half in range(2):
                            sp.dma_start(ex[half * R:(half + 1) * R, :, :], halves[half]).then_inc(raw_back, 16)
                        sp.wait_ge(gate_ev, L * 2)
                        sp.dma_start(scratch.rearrange("g b d -> b g d"), gates[:, :, :]).then_inc(gates_out, 16)
                        sp.wait_ge(gates_out, 16)
                        load_gates(sp, 0)
                        load_gates(sp, 1)

                    @block.scalar
                    def _(act):
                        act.dma_start(sk0[:, :], t["skew"][0:P]).then_inc(skew_in, 16)
                        act.dma_start(sk1[:, :], t["skew"][P:]).then_inc(skew_in, 16)
                        act.wait_ge(cond_in, 16)
                        nc.scalar.activation(th[:, :], cond[:, :], ACT.Tanh, scale=0.5).then_inc(th_done, 1)
                        for l in range(L):
                            act.dma_start(w_main[l][:, :], t[f"main{l}"]).then_inc(w_in[l], 16)
                            act.dma_start(w_tail[l][:, :], t[f"tail{l}"]).then_inc(w_in[l], 16)
                            act.dma_start(w_last[l][:, :], t[f"last{l}"]).then_inc(w_in[l], 16)
                        for g in range(L * 2):
                            act.wait_ge(gate_mm, g + 1)
                            f = ACT.Tanh if g // 2 == 1 else ACT.Copy
                            nc.scalar.activation(gates[:, g, :], bank[2 + g // 3][0:B, (g % 3) * D:(g % 3 + 1) * D], f).then_inc(gate_ev, 1)
                        for n in range(0, 8, 2):
                            act.wait_ge(raw_mm, n + 1)
                            nc.scalar.copy(araw[:, n * 512:(n + 1) * 512], bank[4 + n % 4][0:B, :]).then_inc(raw_ev_act, 1)

                    @block.vector
                    def _(dve):
                        nc.vector.memset(mhalf[:, :], -0.5).then_inc(ones_set, 1)
                        nc.vector.memset(phalf[:, :], 0.5).then_inc(ones_set, 1)
                        nc.vector.memset(zero[:, :], 0.0).then_inc(ones_set, 1)
                        nc.vector.memset(sc1[:, :], 1.0).then_inc(ones_set, 1)
                        dve.wait_ge(consts_in, 16 * 8)
                        nc.vector.tensor_copy(identb[:, :], ident[:, :]).then_inc(ones_set, 1)
                        dve.wait_ge(th_done, 1)
                        nc.vector.scalar_tensor_tensor(out=sil[:, :], in0=th[:, :], scalar=1.0, in1=cond[:, :], op0=ALU.add, op1=ALU.mult).then_inc(sil_done, 1)
                        dve.wait_ge(sct_done, 1)
                        dve.wait_ge(ones_set, 5)
                        nc.vector.tensor_scalar(sc0[:, :], bank[0][:, 0:B], 0.5, None, ALU.mult).then_inc(sc_done, 1)
                        nc.vector.tensor_scalar(sc1[0:DT, :], bank[0][0:DT, B:2 * B], 0.5, None, ALU.mult).then_inc(sc_done, 1)
                        for which in range(4):
                            dve.wait_ge(ada_done, 1)
                            one = float(which % 2)
                            nc.vector.tensor_scalar(mod[:, :, which, :], bank[0][:, 0:L * 4 * B].rearrange("p (l w b) -> p l w b", l=L, w=4)[:, :, which, :], one, None, ALU.add).then_inc(mod_ev, 1)
                            nc.vector.tensor_scalar(modt[:, :, which, :], bank[1][0:DT, 0:L * 4 * B].rearrange("p (l w b) -> p l w b", l=L, w=4)[:, :, which, :], one, None, ALU.add).then_inc(mod_ev, 1)
                        for n in range(1, 8, 2):
                            dve.wait_ge(raw_mm, n + 1)
                            nc.vector.tensor_copy(araw[:, n * 512:(n + 1) * 512], bank[4 + n % 4][0:B, :]).then_inc(raw_ev_dve, 1)
                        dve.wait_ge(raw_back, 32)
                        nc.vector.scalar_tensor_tensor(out=ex[:, :, :], in0=ex[:, :, :], scalar=2.0 ** -DOUBLINGS,
                                                       in1=sign[:, :].unsqueeze(1).to_broadcast([P, PAIRS, R]), op0=ALU.mult, op1=ALU.mult).then_inc(mod_ev, 1)
                        dve.wait_ge(mod_ev, 9)
                        dve.wait_ge(gates_in, 32)

                    @block.tensor
                    def _(pe):
                        pe.wait_ge(sil_done, 1)
                        nc.tensor.transpose(bank[0][:, 0:B], sil[:, 0:P], ident[0:B, 0:B])
                        nc.tensor.transpose(bank[0][0:DT, B:2 * B], sil[:, P:D], ident[0:B, 0:B]).then_inc(sct_done, 1)
                        pe.wait_ge(sc_done, 2)
                        pe.wait_ge(ada_in, 32)
                        for l in range(L):
                            for w, col in enumerate((0, 1, 3, 4)):
                                o = (l * 4 + w) * B
                                nc.tensor.matmul(bank[0][:, o:o + B], ada0[:, l, col * D:col * D + P], sc0[:, :], start=True, stop=False)
                                nc.tensor.matmul(bank[0][:, o:o + B], ada1[:, l, col * D:col * D + P], sc1[:, :], start=False, stop=True)
                                nc.tensor.matmul(bank[1][0:DT, o:o + B], ada0[:, l, col * D + P:(col + 1) * D], sc0[:, :], start=True, stop=False)
                                last = nc.tensor.matmul(bank[1][0:DT, o:o + B], ada1[:, l, col * D + P:(col + 1) * D], sc1[:, :], start=False, stop=True)
                        last.then_inc(ada_done, 1)
                        for g in range(L * 2):
                            col = 2 + 3 * (g % 2)
                            o = (g % 3) * D
                            if g == 3:
                                pass
                            nc.tensor.matmul(bank[2 + g // 3][0:B, o:o + D], sc0[:, :], ada0[:, g // 2, col * D:(col + 1) * D], start=True, stop=False)
                            last = nc.tensor.matmul(bank[2 + g // 3][0:B, o:o + D], sc1[:, :], ada1[:, g // 2, col * D:(col + 1) * D], start=False, stop=True)
                            if g % 3 == 2:
                                last.then_inc(gate_mm, 3)
                        pe.wait_ge(skew_in, 32)
                        for n in range(8):
                            if n >= 4:
                                pe.wait_ge(raw_ev_dve if n % 2 else raw_ev_act, (n - 4) // 2 + 1)
                            nc.tensor.matmul(bank[4 + n % 4][0:B, :], sc0[:, :], sk0[:, n * 512:(n + 1) * 512], start=True, stop=False)
                            nc.tensor.matmul(bank[4 + n % 4][0:B, :], sc1[:, :], sk1[:, n * 512:(n + 1) * 512], start=False, stop=True).then_inc(raw_mm, 1)
            with ExitStack() as c:
                def tsb(name, shape, dt=F32):
                    return c.enter_context(nc.sbuf_tensor(name, shape, dt))

                def tsem(name):
                    return c.enter_context(nc.semaphore(name))

                vs = tsb("vs", [R, R, D])
                inv_t = tsb("inv_t", [R, R])
                junk = tsb("junk", [R, D])
                junk2 = tsb("junk2", [R, D])
                acc = tsb("acc", [R, 16])
                nrm2, dot, half_sign, signed, w, tt, coef, nrm = (acc[:, j:j + 1] for j in range(8))
                qa = tsb("qa", [R, D])
                reduced = tsem("reduced")
                row_done = tsem("row_done")
                chain = tsem("chain")
                nrm2_done = tsem("nrm2_done")
                nrm_done = tsem("nrm_done")
                setup_qr = tsem("setup_qr")
                back = tsem("back")
                ut_mm = tsem("ut_mm")
                STEPS = 9

                with nc.Block() as block:
                    @block.gpsimd
                    def _(pool):
                        for k in range(R):
                            pool.wait_ge(nrm2_done, k + 1)
                            pool.wait_ge(ones_ready, 1)
                            nc.gpsimd.tensor_tensor(nrm, nrm2, phalf[0:R, :], ALU.pow).then_inc(nrm_done, 1)

                    @block.tensor
                    def _(pe):
                        for k in range(R):
                            pe.wait_ge(reduced, k + 1)
                            nc.tensor.matmul(bank[k % 2][0:R, 0:D], ident[0:R, k:k + 1].to_broadcast([R, R]), qa[:, :], start=True, stop=True).then_inc(row_done, 1)
                        pe.wait_ge(back, 2 * R + 3)
                        nc.tensor.transpose(bank[0][:, 0:R], qt[0:R, 0:P], ident[0:R, 0:R])
                        nc.tensor.transpose(bank[0][0:DT, R:2 * R], qt[0:R, P:D], ident[0:R, 0:R]).then_inc(ut_mm, 1)

                    @block.vector
                    def _(dve):
                        nc.vector.tensor_copy(qa[:, :], qt[0:R, :]).then_inc(reduced, 1)
                        for k in range(R):
                            done = k * STEPS
                            v = vs[:, k, :]
                            dve.wait_ge(row_done, k + 1)
                            nc.vector.tensor_copy(v, bank[k % 2][0:R, 0:D]).then_inc(chain, 1)
                            dve.wait_ge(chain, done + 1)
                            nc.vector.tensor_tensor(junk[:, :], v, v, ALU.mult).then_inc(chain, 1)
                            nc.vector.tensor_tensor(junk2[:, :], v, qa[:, :], ALU.mult).then_inc(chain, 1)
                            dve.wait_ge(chain, done + 2)
                            nc.vector.tensor_reduce(nrm2, junk[:, :], AX.X, ALU.add).then_inc(nrm2_done, 1)
                            dve.wait_ge(chain, done + 3)
                            nc.vector.tensor_reduce(dot, junk2[:, :], AX.X, ALU.add).then_inc(chain, 1)
                            nc.vector.tensor_scalar(half_sign, vs[:, k, k:k + 1], 0.0, 0.5, ALU.is_ge, ALU.subtract).then_inc(chain, 1)
                            dve.wait_ge(chain, done + 5)
                            dve.wait_ge(nrm_done, k + 1)
                            nc.vector.scalar_tensor_tensor(out=signed, in0=nrm, scalar=2.0, in1=half_sign, op0=ALU.mult, op1=ALU.mult).then_inc(chain, 1)
                            dve.wait_ge(chain, done + 6)
                            nc.vector.tensor_tensor(vs[:, k, k:k + 1], vs[:, k, k:k + 1], signed, ALU.add).then_inc(chain, 1)
                            nc.vector.scalar_tensor_tensor(out=w, in0=qa[:, k:k + 1], scalar=signed, in1=dot, op0=ALU.mult, op1=ALU.add)
                            dve.wait_ge(chain, done + 7)
                            nc.vector.tensor_tensor(tt, vs[:, k, k:k + 1], signed, ALU.mult).then_inc(chain, 1)
                            dve.wait_ge(chain, done + 8)
                            nc.vector.reciprocal(inv_t[:, k:k + 1], tt).then_inc(chain, 1)
                            dve.wait_ge(chain, done + 9)
                            nc.vector.scalar_tensor_tensor(out=coef, in0=w, scalar=-1.0, in1=inv_t[:, k:k + 1], op0=ALU.mult, op1=ALU.mult).then_inc(back, 1)
                            dve.wait_ge(back, k + 1)
                            nc.vector.scalar_tensor_tensor(out=qa[:, :], in0=v, scalar=coef, in1=qa[:, :], op0=ALU.mult, op1=ALU.add).then_inc(setup_qr, 1)
                            dve.wait_ge(setup_qr, k + 1)
                            nc.vector.memset(qa[:, k:k + 1], 0.0).then_inc(reduced, 1)
                        nc.vector.memset(qt[:, :], 0.0).then_inc(back, 1)
                        dve.wait_ge(back, R + 1)
                        nc.vector.tensor_copy(qt[0:R, 0:R], ident[0:R, 0:R]).then_inc(back, 1)
                        for i in range(R):
                            k = R - 1 - i
                            dve.wait_ge(back, R + 2 + i)
                            nc.vector.tensor_tensor(junk[:, :], vs[:, k, :], qt[0:R, :], ALU.mult).then_inc(chain, 1)
                            dve.wait_ge(chain, i * 3 + (R * STEPS + 1))
                            nc.vector.tensor_reduce(dot, junk[:, :], AX.X, ALU.add).then_inc(chain, 1)
                            dve.wait_ge(chain, i * 3 + (R * STEPS + 2))
                            nc.vector.scalar_tensor_tensor(out=coef, in0=dot, scalar=-1.0, in1=inv_t[:, k:k + 1], op0=ALU.mult, op1=ALU.mult).then_inc(chain, 1)
                            dve.wait_ge(chain, i * 3 + (R * STEPS + 3))
                            nc.vector.scalar_tensor_tensor(out=qt[0:R, :], in0=vs[:, k, :], scalar=coef, in1=qt[0:R, :], op0=ALU.mult, op1=ALU.add).then_inc(back, 1)
                        dve.wait_ge(back, 2 * R + 2)
                        nc.vector.tensor_copy(qt[R:P, :], qt[0:R, :]).then_inc(back, 1)
                        dve.wait_ge(ut_mm, 1)
                        nc.vector.tensor_copy(u0[:, :], bank[0][:, 0:R]).then_inc(ut_mm, 1)
                        nc.vector.tensor_copy(u1[:, :], bank[0][0:DT, R:2 * R]).then_inc(ut_mm, 1)
                        dve.wait_ge(ut_mm, 3)
            with ExitStack() as c:
                def tsb(name, shape, dt=F32):
                    return c.enter_context(nc.sbuf_tensor(name, shape, dt))

                def tsem(name):
                    return c.enter_context(nc.semaphore(name))

                a2, a4, a6, poly = (tsb(n, [P, PAIRS, R]) for n in ("a2", "a4", "a6", "poly"))
                prod_done = tsem("prod_done")
                evac_done = tsem("evac_done")
                term = tsem("term")
                HALF = PAIRS // 2

                def halves(m, h):
                    return m[:, h * HALF:(h + 1) * HALF, :].rearrange("p q j -> p (q j)")

                with nc.Block() as block:
                    @block.tensor
                    def _(pe):
                        def product(lhs, rhs, h, dst):
                            for q in range(HALF):
                                for half in range(2):
                                    rows = slice(half * R, (half + 1) * R)
                                    last = nc.tensor.matmul(bank[dst][rows, q * R:(q + 1) * R], lhs[rows, h * HALF + q, :], rhs[rows, h * HALF + q, :],
                                                            start=True, stop=True)
                            last.then_inc(prod_done, 1)

                        for n, (lhs, rhs) in enumerate(((ex, ex), (a2, a2), (a4, a2), (ex, poly))):
                            for h in range(2):
                                if n:
                                    pe.wait_ge(evac_done, 2 * n - 1 + h)
                                if n == 3:
                                    pe.wait_ge(term, 2)
                                product(lhs, rhs, h, 2 * (n % 2) + h)
                        for s in range(DOUBLINGS):
                            pe.wait_ge(term, 6)
                            for h in range(2):
                                pe.wait_ge(evac_done, 10 + (4 * (s - 1) + 2 * h + 2 if s else 0))
                                product(ey, ex, h, 4 * (s % 2) + 2 * h)
                                product(ex, ey, h, 4 * (s % 2) + 2 * h + 1)

                    @block.vector
                    def _(dve):
                        for h in range(2):
                            dve.wait_ge(prod_done, 1 + h)
                            nc.vector.tensor_scalar(halves(a2, h), bank[h][:, :], -1.0, None, ALU.mult).then_inc(evac_done, 1)
                        for h in range(2):
                            dve.wait_ge(prod_done, 3 + h)
                            nc.vector.tensor_copy(halves(a4, h), bank[2 + h][:, :]).then_inc(evac_done, 1)
                        for h in range(2):
                            dve.wait_ge(prod_done, 5 + h)
                            nc.vector.tensor_copy(halves(a6, h), bank[h][:, :]).then_inc(evac_done, 1)
                        dve.wait_ge(evac_done, 6)
                        nc.vector.tensor_scalar(poly[:, :, :], a2[:, :, :], 1 / 6, None, ALU.mult).then_inc(term, 1)
                        dve.wait_ge(term, 1)
                        nc.vector.scalar_tensor_tensor(out=poly[:, :, :], in0=a4[:, :, :], scalar=1 / 120, in1=poly[:, :, :], op0=ALU.mult, op1=ALU.add).then_inc(evac_done, 1)
                        dve.wait_ge(evac_done, 7)
                        nc.vector.scalar_tensor_tensor(out=poly[:, :, :], in0=a6[:, :, :], scalar=1 / 5040, in1=poly[:, :, :], op0=ALU.mult, op1=ALU.add).then_inc(term, 1)
                        nc.vector.tensor_scalar(a2[:, :, :], a2[:, :, :], 0.5, None, ALU.mult).then_inc(term, 1)
                        dve.wait_ge(term, 3)
                        nc.vector.scalar_tensor_tensor(out=a2[:, :, :], in0=a4[:, :, :], scalar=1 / 24, in1=a2[:, :, :], op0=ALU.mult, op1=ALU.add).then_inc(term, 1)
                        dve.wait_ge(term, 4)
                        nc.vector.scalar_tensor_tensor(out=a2[:, :, :], in0=a6[:, :, :], scalar=1 / 720, in1=a2[:, :, :], op0=ALU.mult, op1=ALU.add).then_inc(term, 1)
                        for h in range(2):
                            dve.wait_ge(prod_done, 7 + h)
                            dve.wait_ge(term, 5)
                            nc.vector.tensor_tensor(halves(a4, h), halves(ex, h), bank[2 + h][:, :], ALU.subtract).then_inc(evac_done, 1)
                        dve.wait_ge(evac_done, 9)
                        nc.vector.tensor_tensor(ex[:, :, :], a2[:, :, :], a4[:, :, :], ALU.add).then_inc(evac_done, 1)
                        nc.vector.tensor_tensor(ey[:, :, :], a2[:, :, :], a4[:, :, :], ALU.subtract).then_inc(term, 1)
                        dve.wait_ge(term, 6)
                        for s in range(DOUBLINGS):
                            for h in range(2):
                                dve.wait_ge(prod_done, 8 + 4 * s + 2 * h + 2)
                                for m, b in ((ex, 0), (ey, 1)):
                                    if s == 0 and h == 0 and b == 0:
                                        dve.wait_ge(evac_done, 10)
                                    elif s:
                                        dve.wait_ge(evac_done, 10 + 4 * s - 4 + 2 * h + 1 + b)
                                    nc.vector.scalar_tensor_tensor(out=halves(m, h), in0=halves(m, h), scalar=2.0, in1=bank[4 * (s % 2) + 2 * h + b][:, :],
                                                                   op0=ALU.mult, op1=ALU.add).then_inc(evac_done, 1)
                        dve.wait_ge(evac_done, 10 + 4 * DOUBLINGS)
            with ExitStack() as c:
                def tsb(name, shape, dt=F32):
                    return c.enter_context(nc.sbuf_tensor(name, shape, dt))

                def tsem(name):
                    return c.enter_context(nc.semaphore(name))

                xc = tsb("xc", [P, 2, 2, D])
                yc = tsb("yc", [P, 2, R])
                xt0 = tsb("xt0", [P, 2, 2 * T])
                xt1 = tsb("xt1", [DT, 2, 2 * T])
                zt = tsb("zt", [P, 2, T])
                bm = tsb("bm", [P, 2, D])
                staged = tsem("staged")
                xt_mm = tsem("xt_mm")
                xt_done = tsem("xt_done")
                z_mm = tsem("z_mm")
                z_done = tsem("z_done")
                rot_mm = tsem("rot_mm")
                x_done = tsem("x_done")
                st_done = tsem("st_done")
                var_done = tsem("var_done")
                rs_done = tsem("rs_done")

                with nc.Block() as block:
                    @block.gpsimd
                    def _(pool):
                        def stage(q, u):
                            nc.gpsimd.tensor_copy(xc[:, u, :, :], x_all[:, bass.ds(q * 2, 2), :]).then_inc(staged, 1)
                            nc.gpsimd.tensor_copy(yc[:, u, :], ey[:, q, :]).then_inc(staged, 1)

                        stage(0, 0)
                        stage(1, 1)
                        with nc.gpsimd.Fori(1, PAIRS // 2) as i:
                            for u in range(2):
                                pool.wait_ge(ones_ready, 1)
                                pool.wait_ge(x_done, i * 2 - 1 + u)
                                stage(i * 2 + u, u)

                    @block.tensor
                    def _(pe):
                        with nc.tensor.Fori(0, PAIRS // 2) as i:
                            for u in range(2):
                                n = i * 2 + u
                                pe.wait_ge(staged, n * 2 + 2)
                                for s in range(2):
                                    nc.tensor.transpose(bank[0][:, s * T:(s + 1) * T], xc[:, u, s, 0:P], ident[:, :])
                                for s in range(2):
                                    last = nc.tensor.transpose(bank[1][0:DT, s * T:(s + 1) * T], xc[:, u, s, P:D], ident[:, :])
                                last.then_inc(xt_mm, 1)
                                for s in range(2):
                                    h = slice(s * R, (s + 1) * R)
                                    nc.tensor.matmul(bank[3][h, 0:D], yc[h, u, :], qt[h, :], start=True, stop=True)
                                pe.wait_ge(ones_ready, 1)
                                pe.wait_ge(xt_done, n + 1)
                                for s in range(2):
                                    h = slice(s * R, (s + 1) * R)
                                    nc.tensor.matmul(bank[2][h, 0:T], u0[:, :], xt0[:, u, s * T:(s + 1) * T], start=True, stop=False)
                                    last = nc.tensor.matmul(bank[2][h, 0:T], u1[:, :], xt1[:, u, s * T:(s + 1) * T], start=False, stop=True)
                                last.then_inc(z_mm, 1)
                                pe.wait_ge(z_done, n + 1)
                                for s in range(2):
                                    h = slice(s * R, (s + 1) * R)
                                    last = nc.tensor.matmul(bank[4 + s][:, 0:D], zt[h, u, :], bm[h, u, :], start=True, stop=True)
                                last.then_inc(rot_mm, 1)

                    @block.scalar
                    def _(act):
                        with nc.scalar.Fori(0, PAIRS // 2) as i:
                            for u in range(2):
                                n = i * 2 + u
                                act.wait_ge(z_mm, n + 1)
                                nc.scalar.copy(zt[:, u, :], bank[2][:, 0:T])
                                nc.scalar.copy(bm[:, u, :], bank[3][:, 0:D]).then_inc(z_done, 1)

                    @block.vector
                    def _(dve):
                        with nc.vector.Fori(0, PAIRS // 2) as i:
                            for u in range(2):
                                n = i * 2 + u
                                dve.wait_ge(xt_mm, n + 1)
                                nc.vector.tensor_copy(xt0[:, u, :], bank[0][:, 0:2 * T])
                                nc.vector.tensor_copy(xt1[:, u, :], bank[1][0:DT, 0:2 * T]).then_inc(xt_done, 1)
                                dve.wait_ge(rot_mm, n + 1)
                                for s in range(2):
                                    seq = n * 2 + s
                                    last = nc.vector.tensor_tensor(x_all[:, seq, :], xc[:, u, s, :], bank[4 + s][:, 0:D], ALU.add)
                                last.then_inc(x_done, 1)
                                dve.wait_ge(ones_ready, 1)
                                dve.wait_ge(x_done, n + 1)
                                nc.vector.bn_stats(stats[:, 0, :], x_all[:, n * 2, :])
                                nc.vector.bn_stats(stats[:, 1, :], x_all[:, n * 2 + 1, :]).then_inc(st_done, 1)
                                dve.wait_ge(ones_ready, 1)
                                dve.wait_ge(st_done, n + 1)
                                nc.vector.bn_aggr(aggr[:, 0, :], stats[:, 0, :])
                                nc.vector.bn_aggr(aggr[:, 1, :], stats[:, 1, :]).then_inc(var_done, 1)
                                dve.wait_ge(var_done, n + 1)
                                nc.vector.tensor_copy(mean_all[:, bass.ds(n * 2, 2)], aggr[:, :, 0])
                                nc.vector.tensor_scalar(var_all[:, bass.ds(n * 2, 2)], aggr[:, :, 1], 1e-6, None, ALU.add).then_inc(rs_done, 1)
                        dve.wait_ge(rs_done, PAIRS)
                with nc.Block() as block:
                    @block.gpsimd
                    def _(pool):
                        nc.gpsimd.tensor_tensor(rstd_all[:, :], var_all[:, :], mhalf[:, :].to_broadcast([P, B]), ALU.pow).then_inc(rs_done, 1)
                        pool.wait_ge(rs_done, PAIRS + 1)
        def variance(dve, rms, both, b, done, ms, count):
            if rms:
                nc.vector.scalar_tensor_tensor(out=both[:, 1:2], in0=both[:, 0:1], scalar=both[:, 0:1], in1=both[:, 1:2], op0=ALU.mult, op1=ALU.add).then_inc(ms, 1)
                dve.wait_ge(ms, count + 1)
                nc.vector.tensor_scalar(var_all[:, bass.ds(b, 1)], both[:, 1:2], 1e-24 / D, None, ALU.max).then_inc(done, 1)
            else:
                nc.vector.tensor_copy(mean_all[:, bass.ds(b, 1)], both[:, 0:1])
                nc.vector.tensor_scalar(var_all[:, bass.ds(b, 1)], both[:, 1:2], 1e-6, None, ALU.add).then_inc(done, 1)

        with ExitStack() as c:
            def tsb(name, shape, dt=F32):
                return c.enter_context(nc.sbuf_tensor(name, shape, dt))

            turned = nc.dram_tensor("turned", [B, H, T, DH], F32, kind="Internal").ap()
            hn = tsb("h_hn", [P, 2, D])
            ht0 = tsb("h_ht0", [P, 2, T])
            ht1 = tsb("h_ht1", [DT + 1, 2, T])
            qkv = tsb("h_qkv", [P, 2, 3 * D])
            qk_prod = tsb("h_qk_prod", [P, H, H, DH])
            score = tsb("h_score", [P, 2, H, H])
            top = tsb("h_top", [P, H])
            prob = tsb("h_prob", [P, 2, H, H])
            rsum = tsb("h_rsum", [P, 2, H])
            pv_prod = tsb("h_pv_prod", [P, 2, H, H, DH])
            out_h = tsb("h_out", [P, 2, D])
            y = tsb("h_y", [P, 2, D])
            at0 = tsb("h_at0", [P, 2, T])
            at1 = tsb("h_at1", [DT + 1, 2, T])
            upd = tsb("h_upd", [P, 2, D])
            names = ("set hn_done ht_mm ht_done qkv_mm qkv_done qk_done score_done max_done sub_done exp_done sum_done rsum_done pv_done "
                     "pvsum_mm out_done turn_out turn_in y_mm y_done proj_mm upd_done x_new stat_done aggr_done var_new rstd_new").split()
            S = {k: sem("h_" + k) for k in names}
            b_tp, b_mm, b_sum, b_ty, b_pj = bank[0:5]

            def drive(eng, step):
                step(-1, 1, middle=False, sums=False, last=False)
                step(0, 0, sums=False, last=False)
                step(1, 1, last=False)
                step(2, 0)
                step(3, 1)
                with eng.Fori(0, (B - 6) // 2) as i:
                    step(i * 2 + 4, 0)
                    step(i * 2 + 5, 1)
                step(B - 2, 0)
                step(B - 1, 1, front=False)
                step(B, 0, front=False, middle=False)
                step(B + 1, 1, front=False, middle=False, sums=False)

            with nc.Block() as block:
                @block.tensor
                def _(pe):
                    def step(b, u, front=True, middle=True, sums=True, last=True):
                        w = 1 - u
                        if front:
                            pe.wait_ge(S["hn_done"], b + 2)
                            nc.tensor.transpose(b_tp[:, 0:T], hn[:, w, 0:P], ident[:, :])
                            nc.tensor.transpose(b_tp[0:DT, T:2 * T], hn[:, w, P:D], ident[:, :]).then_inc(S["ht_mm"], 1)
                        if sums:
                            pe.wait_ge(S["pv_done"], b)
                            if last:
                                pe.wait_ge(S["out_done"], b - 1)
                            for k in range(H):
                                mm = nc.tensor.matmul(b_sum[:, 0:D], ident[:, :], pv_prod[:, w, k, :, :].rearrange("p h d -> p (h d)"), start=(k == 0), stop=(k == H - 1))
                            mm.then_inc(S["pvsum_mm"], 1)
                        if last:
                            pe.wait_ge(S["turn_in"], (b - 1) * 16)
                            nc.tensor.transpose(b_ty[:, 0:T], y[:, u, 0:P], ident[:, :])
                            nc.tensor.transpose(b_ty[0:DT, T:2 * T], y[:, u, P:D], ident[:, :]).then_inc(S["y_mm"], 1)
                        if front:
                            pe.wait_ge(S["set"], 2)
                            pe.wait_ge(S["ht_done"], b * 2 + 4)
                            if middle:
                                pe.wait_ge(S["qkv_done"], b + 1)
                            nc.tensor.matmul(b_mm[:, 0:3 * D], ht0[:, w, :], w_main[0][:, 0:3 * D], start=True, stop=False)
                            nc.tensor.matmul(b_mm[:, 0:3 * D], ht1[:, w, :], w_tail[0][:, 0:3 * D], start=False, stop=True).then_inc(S["qkv_mm"], 1)
                        if last:
                            pe.wait_ge(S["y_done"], b * 2 - 2)
                            if not isinstance(b, int) or b > 2:
                                pe.wait_ge(S["upd_done"], b - 2)
                            nc.tensor.matmul(b_pj[:, 0:D], at0[:, u, :], w_main[0][:, 3 * D:4 * D], start=True, stop=False)
                            nc.tensor.matmul(b_pj[:, 0:D], at1[:, u, :], w_tail[0][:, 3 * D:4 * D], start=False, stop=True).then_inc(S["proj_mm"], 1)

                    pe.wait_ge(w_in[0], 48)
                    drive(nc.tensor, step)

                @block.scalar
                def _(act):
                    def step(b, u, front=True, middle=True, sums=True, last=True):
                        w = 1 - u
                        if middle:
                            act.wait_ge(S["sub_done"], b + 1)
                            nc.scalar.activation(prob[:, u, :, :], score[:, u, :, :], ACT.Exp, scale=SM).then_inc(S["exp_done"], 1)
                        if front:
                            act.wait_ge(S["qkv_mm"], b + 2)
                            nc.scalar.copy(qkv[:, w, :], b_mm[:, 0:3 * D]).then_inc(S["qkv_done"], 1)
                        if last:
                            act.wait_ge(S["y_mm"], b - 1)
                            nc.scalar.copy(at0[:, u, :], b_ty[:, 0:T]).then_inc(S["y_done"], 1)
                            nc.scalar.copy(at1[0:DT, u, :], b_ty[0:DT, T:2 * T]).then_inc(S["y_done"], 1)

                    drive(nc.scalar, step)

                @block.gpsimd
                def _(pool):
                    def step(b, u, front=True, middle=True, sums=True, last=True):
                        w = 1 - u
                        if middle:
                            pool.wait_ge(S["exp_done"], b + 1)
                            if sums and last:
                                pool.wait_ge(S["pvsum_mm"], b - 1)
                            nc.gpsimd.tensor_tensor(pv_prod[:, u, :, :, :], prob[:, u, :, :].rearrange("p h k -> p k h").unsqueeze(3).to_broadcast([P, H, H, DH]),
                                                    qkv[:, u, 2 * D:3 * D].rearrange("p (k d) -> p k d", d=DH).unsqueeze(2).to_broadcast([P, H, H, DH]), ALU.mult).then_inc(S["pv_done"], 1)
                        if last:
                            pool.wait_ge(S["var_new"], b - 1)
                            nc.gpsimd.tensor_tensor(rstd_all[:, bass.ds(b - 2, 1)], var_all[:, bass.ds(b - 2, 1)], mhalf[:, :], ALU.pow).then_inc(S["rstd_new"], 1)

                    drive(nc.gpsimd, step)
                    pool.wait_ge(S["rstd_new"], B)

                @block.sync
                def _(sp):
                    def step(b, u, front=True, middle=True, sums=True, last=True):
                        if not sums:
                            return
                        w = 1 - u
                        sp.wait_ge(S["out_done"], b)
                        sp.dma_start(turned[b - 1].rearrange("h t d -> t h d"), out_h[:, w, :].rearrange("p (h d) -> p h d", d=DH)).then_inc(S["turn_out"], 16)
                        sp.wait_ge(S["turn_out"], b * 16)
                        sp.dma_start(y[:, w, :], turned[b - 1].rearrange("h t d -> (h t d)").rearrange("(p q) -> p q", q=D)).then_inc(S["turn_in"], 16)

                    drive(nc.sync, step)

                @block.vector
                def _(dve):
                    def step(b, u, front=True, middle=True, sums=True, last=True):
                        w = 1 - u
                        nb = b + 1
                        if front:
                            nc.vector.tensor_scalar(hn[:, w, :], x_all[:, nb, :], mean_all[:, bass.ds(nb, 1)], rstd_all[:, bass.ds(nb, 1)], ALU.subtract, ALU.mult).then_inc(S["hn_done"], 1)
                        if middle:
                            dve.wait_ge(S["qkv_done"], b + 1)
                            heads = qkv[:, u, :].rearrange("p (s h d) -> p s h d", s=3, d=DH)
                            nc.vector.tensor_tensor(qk_prod[:, :, :, :], heads[:, 0].unsqueeze(2).to_broadcast([P, H, H, DH]),
                                                    heads[:, 1].unsqueeze(1).to_broadcast([P, H, H, DH]), ALU.mult).then_inc(S["qk_done"], 1)
                        if front:
                            dve.wait_ge(S["ht_mm"], b + 2)
                            nc.vector.tensor_scalar(ht0[:, w, :], b_tp[:, 0:T], mod[:, 0, 1, bass.ds(nb, 1)], mod[:, 0, 0, bass.ds(nb, 1)], ALU.mult, ALU.add).then_inc(S["ht_done"], 1)
                            nc.vector.tensor_scalar(ht1[0:DT, w, :], b_tp[0:DT, T:2 * T], modt[:, 0, 1, bass.ds(nb, 1)], modt[:, 0, 0, bass.ds(nb, 1)], ALU.mult, ALU.add).then_inc(S["ht_done"], 1)
                        if middle:
                            dve.wait_ge(S["qk_done"], b + 1)
                            nc.vector.tensor_reduce(score[:, u, :, :], qk_prod[:, :, :, :], AX.X, ALU.add).then_inc(S["score_done"], 1)
                            dve.wait_ge(S["score_done"], b + 1)
                            nc.vector.tensor_reduce(top[:, :], score[:, u, :, :], AX.X, ALU.max).then_inc(S["max_done"], 1)
                            dve.wait_ge(S["max_done"], b + 1)
                            nc.vector.tensor_tensor(score[:, u, :, :], score[:, u, :, :], top[:, :].unsqueeze(2).to_broadcast([P, H, H]), ALU.subtract).then_inc(S["sub_done"], 1)
                        if sums:
                            dve.wait_ge(S["rsum_done"], b)
                            dve.wait_ge(S["pvsum_mm"], b)
                            if last:
                                dve.wait_ge(S["turn_out"], (b - 1) * 16)
                            nc.vector.tensor_tensor(out_h[:, w, :].rearrange("p (h d) -> p h d", d=DH), b_sum[:, 0:D].rearrange("p (h d) -> p h d", d=DH),
                                                    rsum[:, w, :].unsqueeze(2).to_broadcast([P, H, DH]), ALU.mult).then_inc(S["out_done"], 1)
                        if last:
                            pb = b - 2
                            dve.wait_ge(S["proj_mm"], b - 1)
                            nc.vector.tensor_tensor(upd[:, u, :], b_pj[:, 0:D], gate_all[:, 0, pb, :], ALU.mult).then_inc(S["upd_done"], 1)
                            dve.wait_ge(S["upd_done"], b - 1)
                            nc.vector.tensor_tensor(x_all[:, pb, :], x_all[:, pb, :], upd[:, u, :], ALU.add).then_inc(S["x_new"], 1)
                            dve.wait_ge(ones_ready, 1)
                            dve.wait_ge(S["x_new"], b - 1)
                            nc.vector.bn_stats(stats[:, u, :], x_all[:, pb, :]).then_inc(S["stat_done"], 1)
                            dve.wait_ge(ones_ready, 1)
                            dve.wait_ge(S["stat_done"], b - 1)
                            nc.vector.bn_aggr(aggr[:, u, :], stats[:, u, :]).then_inc(S["aggr_done"], 1)
                            dve.wait_ge(S["aggr_done"], b - 1)
                            variance(dve, False, aggr[:, u], pb, S["var_new"], None, b - 2)
                        if middle:
                            dve.wait_ge(S["exp_done"], b + 1)
                            nc.vector.tensor_reduce(rsum[:, u, :], prob[:, u, :, :], AX.X, ALU.add).then_inc(S["sum_done"], 1)
                            dve.wait_ge(S["sum_done"], b + 1)
                            nc.vector.reciprocal(rsum[:, u, :], rsum[:, u, :]).then_inc(S["rsum_done"], 1)

                    nc.vector.memset(ht1[:, :, :], 1.0).then_inc(S["set"], 1)
                    nc.vector.memset(at1[:, :, :], 1.0).then_inc(S["set"], 1)
                    dve.wait_ge(S["set"], 2)
                    drive(nc.vector, step)
                    dve.wait_ge(S["var_new"], B)
                    dve.wait_ge(S["rsum_done"], B)
        hn = sb("hn", [P, 2, D])
        ht0 = sb("ht0", [P, 2, T])
        ht1 = sb("ht1", [DT + 1, 2, T])
        qkvs = sb("qkvs", [P, 2, 3 * D])
        sq = sb("sq", [P, 2 * D])
        ssum = sb("ssum", [P, 2 * H])
        rq = sb("rq", [P, 2 * H])
        gq = sb("gq", [P, 2 * H])
        qk = sb("qk", [P, 2 * D])
        rest = sb("rest", [P, 2 * D])
        stack = sb("stack", [P, 2, H, SLOT], BF16)
        qs = sb("qs", [P, 2, H // 2, T], BF16)
        ks = sb("ks", [P, 2, H // 2, T], BF16)
        va = sb("va", [P, 2, H, 32])
        rmax = sb("rmax", [P, H])
        neg = sb("neg", [P, 2, SLOT], BF16)
        negt = sb("negt", [P, T], BF16)
        pick = sb("pick", [P, H // 2, T], BF16)
        pt = sb("pt", [P, 2, H, T])
        ot = sb("ot", [P, 4, T])
        rsum = sb("rsum", [P, H])
        at = sb("at", [P, 2, D])
        at0 = sb("at0", [P, T])
        at1 = sb("at1", [DT + 1, T])
        upd = sb("upd", [P, 2, D])

        names = ("hn_done ht_mm ht_done qkv_mm qkv_done square_done ssum_done rq_done qkn_done high_done va_done rest_done "
                 "midp_done low_done qs_mm qs_done ks_mm ks_done s_mm max_done neg_done negt_mm negt_done st_mm exp_done "
                 "pv_mm ot_done back_mm rsum_done at_done at_mm at_ev proj_mm upd_done x_new stat_done aggr_done var_new rstd_new ms_done set_done").split()
        S = {k: sem("a_" + k) for k in names}

        bank_hs = [bank[0:2], bank[2:4]]
        b_t, b_mm, b_tp, b_ov = bank[4], bank[5], bank[6], bank[7]
        tp16 = b_tp[:, :].bitcast(BF16).rearrange("p (c t) -> p c t", t=T)
        t16 = b_t[:, :].bitcast(BF16)

        with nc.Block() as block:
            @block.vector
            def _(dve):
                nc.vector.memset(ht1[:, :, :], 1.0).then_inc(S["set_done"], 1)
                nc.vector.memset(at1[:, :], 1.0).then_inc(S["set_done"], 1)
                nc.vector.memset(va[:, :, :, :], 0.0).then_inc(S["set_done"], 1)
                nc.vector.memset(stack[:, :, :, :], 0.0).then_inc(S["set_done"], 1)
                nc.vector.memset(neg[:, :, :], 0.0).then_inc(S["set_done"], 1)
                for s in range(2):
                    nc.vector.tensor_scalar(gq[:, s * H:(s + 1) * H], gain[:, 2 + s:3 + s].to_broadcast([P, H]), DH ** 0.5, None, ALU.mult).then_inc(S["set_done"], 1)
                for c in range(2):
                    r = slice(SLOT * c, SLOT * c + H)
                    nc.vector.tensor_tensor(pick[r, :, :], ident[r, SLOT * c:SLOT * c + H:2].unsqueeze(2).to_broadcast([H, H // 2, T]),
                                            ident[r, SLOT * c + 1:SLOT * c + H:2].unsqueeze(2).to_broadcast([H, H // 2, T]), ALU.add).then_inc(S["set_done"], 1)
                dve.wait_ge(S["set_done"], 9)
                nc.vector.memset(va[:, :, :, DH:DH + 1], 1.0).then_inc(S["set_done"], 1)
                dve.wait_ge(S["set_done"], 10)
                for l in range(L):
                    dve.wait_ge(w_in[l], 48)

        def attention(l):
            base = (l - 1) * B
            wq0, wq1 = w_main[l][:, 0:3 * D], w_tail[l][:, 0:3 * D]
            wp0, wp1 = w_main[l][:, 3 * D:4 * D], w_tail[l][:, 3 * D:4 * D]
            rms = l == 1

            def drive(eng, step):
                step(-2, 0, B_=False, C=False, D_=False, F=False)
                step(-1, 1, C=False, D_=False, F=False)
                step(0, 0, D_=False, F=False)
                step(1, 1, F=False)
                step(2, 0)
                step(3, 1)
                with eng.Fori(0, (B - 6) // 2) as i:
                    step(i * 2 + 4, 0)
                    step(i * 2 + 5, 1)
                step(B - 2, 0, A=False)
                step(B - 1, 1, A=False, B_=False)
                step(B, 0, A=False, B_=False, C=False)
                step(B + 1, 1, A=False, B_=False, C=False, D_=False)

            with nc.Block() as block:
                @block.sync
                def _(sp):
                    load_gates(sp, 2 * l + 1)

                @block.tensor
                def _(pe):
                    def step(b, u, A=True, B_=True, C=True, D_=True, F=True):
                        n = b + base
                        w = 1 - u
                        if A:
                            pe.wait_ge(S["hn_done"], n + 3)
                            if D_:
                                pe.wait_ge(S["negt_done"], n)
                            nc.tensor.transpose(b_t[:, 0:T], hn[:, u, 0:P], ident[:, :])
                            nc.tensor.transpose(b_t[0:DT, T:2 * T], hn[:, u, P:D], ident[:, :]).then_inc(S["ht_mm"], 1)
                        if D_:
                            pe.wait_ge(S["va_done"], n)
                            if F:
                                pe.wait_ge(S["at_done"], n - 1)
                            for h in range(H):
                                if h % 8 == 0:
                                    pe.wait_ge(S["exp_done"], n * 4 - 2 + h // 4)
                                r = 32 * (h % 4)
                                mm = nc.tensor.matmul(b_ov[r:r + 32, h // 4 * T:(h // 4 + 1) * T], va[:, w, h, :], pt[:, w, h, :], start=True, stop=True)
                            mm.then_inc(S["pv_mm"], 1)
                        if F:
                            pe.wait_ge(S["at_done"], n - 1)
                            if A:
                                pe.wait_ge(S["ht_done"], 2 * n + 6)
                            elif D_:
                                pe.wait_ge(S["negt_done"], n)
                            nc.tensor.transpose(b_t[:, 0:T], at[:, u, 0:P], ident[:, :])
                            nc.tensor.transpose(b_t[0:DT, T:2 * T], at[:, u, P:D], ident[:, :]).then_inc(S["at_mm"], 1)
                        if C:
                            pe.wait_ge(S["qs_done"], n + 1)
                            pe.wait_ge(S["ks_done"], n + 1)
                            for half in range(2):
                                if D_:
                                    pe.wait_ge(S["exp_done"], n * 4 - 2 + 2 * half)
                                for h in range(8 * half, 8 * half + 8):
                                    r = slice(SLOT * (h % 2), SLOT * (h % 2) + PIECES * DH)
                                    mm = nc.tensor.matmul(bank_hs[half][h % 2][:, (h % 8) // 2 * T:((h % 8) // 2 + 1) * T], qs[r, u, h // 2, :], ks[r, u, h // 2, :],
                                                          start=True, stop=True)
                                mm.then_inc(S["s_mm"], 1)
                        if A:
                            pe.wait_ge(S["ht_done"], 2 * n + 6)
                            if F:
                                if not (isinstance(b, int) and b < 3):
                                    pe.wait_ge(S["upd_done"], n - 2)
                            elif B_:
                                pe.wait_ge(S["qkv_done"], n + 2)
                            nc.tensor.matmul(b_mm[:, 0:3 * D], ht0[:, u, :], wq0, start=True, stop=False)
                            nc.tensor.matmul(b_mm[:, 0:3 * D], ht1[:, u, :], wq1, start=False, stop=True).then_inc(S["qkv_mm"], 1)
                        if D_:
                            pe.wait_ge(S["ot_done"], n)
                            for g in range(4):
                                mm = nc.tensor.transpose(b_ov[:, g * T:(g + 1) * T], ot[:, g, :], ident[:, :])
                            mm.then_inc(S["back_mm"], 1)
                        if F:
                            pe.wait_ge(S["at_ev"], 2 * n - 2)
                            if A:
                                pe.wait_ge(S["qkv_done"], n + 3)
                            else:
                                pe.wait_ge(S["upd_done"], n - 2)
                            nc.tensor.matmul(b_mm[:, 0:D], at0[:, :], wp0, start=True, stop=False)
                            nc.tensor.matmul(b_mm[:, 0:D], at1[:, :], wp1, start=False, stop=True).then_inc(S["proj_mm"], 1)
                        if C:
                            pe.wait_ge(S["neg_done"], 2 * n + 2)
                            if F:
                                pe.wait_ge(S["at_ev"], 2 * n - 2)
                            elif A:
                                pe.wait_ge(S["ht_done"], 2 * n + 6)
                            nc.tensor.transpose(t16[:, 0:T], neg[:, :, :].rearrange("p c s -> p (c s)"), identb[:, :]).then_inc(S["negt_mm"], 1)
                        if B_:
                            pe.wait_ge(S["low_done"], 2 * n + 4)
                            if C:
                                pe.wait_ge(S["ks_done"], n + 1)
                            for c in range(8):
                                mm = nc.tensor.transpose(tp16[:, c, :], stack[:, 0, 2 * c:2 * c + 2, :].rearrange("p h s -> p (h s)"), identb[:, :])
                            mm.then_inc(S["qs_mm"], 1)
                        if C:
                            pe.wait_ge(S["negt_done"], n + 1)
                            for half in range(2):
                                pe.wait_ge(S["max_done"], 2 * n + 1 + half)
                                for h in range(8 * half, 8 * half + 8):
                                    r = SLOT * (h % 2)
                                    dst = bank_hs[half][h % 2][:, (h % 8) // 2 * T:((h % 8) // 2 + 1) * T]
                                    nc.tensor.matmul(dst, ks[r:r + PIECES * DH, u, h // 2, :], qs[r:r + PIECES * DH, u, h // 2, :], start=True, stop=False)
                                    mm = nc.tensor.matmul(dst, pick[r:r + H, h // 2, :], negt[r:r + H, :], start=False, stop=True)
                                mm.then_inc(S["st_mm"], 1)
                        if B_:
                            pe.wait_ge(S["qs_done"], n + 2)
                            for c in range(8):
                                mm = nc.tensor.transpose(tp16[:, c, :], stack[:, 1, 2 * c:2 * c + 2, :].rearrange("p h s -> p (h s)"), identb[:, :])
                            mm.then_inc(S["ks_mm"], 1)

                    drive(nc.tensor, step)

                @block.scalar
                def _(act):
                    def step(b, u, A=True, B_=True, C=True, D_=True, F=True):
                        n = b + base
                        w = 1 - u
                        if C:
                            if not (isinstance(b, int) and b < 2):
                                act.wait_ge(S["pv_mm"], n - 1)
                            act.wait_ge(S["qkv_done"], n + 1)
                            nc.scalar.copy(va[:, u, :, 0:DH], qkvs[:, u, 2 * D:3 * D].rearrange("p (h d) -> p h d", d=DH)).then_inc(S["va_done"], 1)
                        if B_:
                            act.wait_ge(S["qkv_done"], n + 2)
                            src = qkvs[:, w, 0:2 * D]
                            if rms:
                                act.wait_ge(S["qkn_done"], n + 2)
                                src = qk[:, :]
                            src = src.rearrange("p (s h d) -> p s h d", s=2, d=DH)
                            for s in range(2):
                                dst = stack[:, s, :, 0:PIECES * DH].rearrange("p h (c d) -> p h c d", d=DH)
                                dst = dst[:, :, 1::2, :] if s == 0 else dst[:, :, 0:3, :]
                                nc.scalar.copy(dst, src[:, s].unsqueeze(2).to_broadcast([P, H, 3, DH])).then_inc(S["high_done"], 1)
                        if D_:
                            act.wait_ge(S["pv_mm"], n)
                            nc.scalar.copy(ot[:, :, :].rearrange("p g t -> p (g t)"), b_ov[:, :]).then_inc(S["ot_done"], 1)
                        if B_:
                            act.wait_ge(S["rest_done"], n + 2)
                            less = rest[:, :].rearrange("p (s h d) -> p s h d", s=2, d=DH)
                            for s in range(2):
                                dst = stack[:, s, :, 0:PIECES * DH].rearrange("p h (c d) -> p h c d", d=DH)
                                dst = dst[:, :, 2::2, :] if s == 0 else dst[:, :, 3:5, :]
                                nc.scalar.copy(dst, less[:, s].unsqueeze(2).to_broadcast([P, H, 2, DH])).then_inc(S["midp_done"], 1)
                        if F:
                            act.wait_ge(S["at_mm"], n - 1)
                            nc.scalar.copy(at0[:, :], b_t[:, 0:T]).then_inc(S["at_ev"], 1)
                            nc.scalar.copy(at1[0:DT, :], b_t[0:DT, T:2 * T]).then_inc(S["at_ev"], 1)
                        if A:
                            act.wait_ge(S["qkv_mm"], n + 3)
                            nc.scalar.copy(qkvs[:, u, :], b_mm[:, 0:3 * D]).then_inc(S["qkv_done"], 1)
                            if rms:
                                act.wait_ge(S["qkv_done"], n + 3)
                                nc.scalar.activation(sq[:, :], qkvs[:, u, 0:2 * D], ACT.Square).then_inc(S["square_done"], 1)
                        if C:
                            for c in range(4):
                                act.wait_ge(S["st_mm"], 2 * n + 1 + c // 2)
                                nc.scalar.activation(pt[:, u, 8 * (c // 2) + c % 2:8 * (c // 2) + 8:2, :], bank[c][:, :].rearrange("p (h t) -> p h t", t=T), ACT.Exp, scale=SM).then_inc(S["exp_done"], 1)
                        if B_:
                            act.wait_ge(S["ks_mm"], n + 2)
                            nc.scalar.copy(ks[:, w, :, :], tp16).then_inc(S["ks_done"], 1)

                    drive(nc.scalar, step)

                @block.gpsimd
                def _(pool):
                    def step(b, u, A=True, B_=True, C=True, D_=True, F=True):
                        n = b + base
                        w = 1 - u
                        if B_:
                            pieces = stack[:, :, :, 0:PIECES * DH].rearrange("p s h (c d) -> p s h c d", d=DH)
                            less = rest[:, :].rearrange("p (s h d) -> p s h d", s=2, d=DH)
                            pool.wait_ge(S["midp_done"], 2 * n + 4)
                            for s in range(2):
                                nc.gpsimd.tensor_tensor(pieces[:, s, :, 5 * s, :], less[:, s], pieces[:, s, :, 4, :], ALU.subtract).then_inc(S["low_done"], 1)
                        if A and rms:
                            pool.wait_ge(S["ssum_done"], 2 * n + 6)
                            nc.gpsimd.tensor_tensor(ssum[:, :], ssum[:, :], mhalf[:, :].to_broadcast([P, 2 * H]), ALU.pow).then_inc(S["rq_done"], 1)
                            pool.wait_ge(S["rq_done"], 2 * n + 5)
                            nc.gpsimd.tensor_tensor(rq[:, :], ssum[:, :], gq[:, :], ALU.mult).then_inc(S["rq_done"], 1)
                        if F:
                            pool.wait_ge(S["var_new"], n - 1)
                            nc.gpsimd.tensor_tensor(rstd_all[:, bass.ds(b - 2, 1)], var_all[:, bass.ds(b - 2, 1)], mhalf[:, :], ALU.pow).then_inc(S["rstd_new"], 1)

                    drive(nc.gpsimd, step)
                    pool.wait_ge(S["rstd_new"], base + B)

                @block.vector
                def _(dve):
                    def step(b, u, A=True, B_=True, C=True, D_=True, F=True):
                        n = b + base
                        w = 1 - u

                        def row_max(half):
                            dve.wait_ge(S["s_mm"], 2 * n + 1 + half)
                            for c in range(2):
                                mm = nc.vector.tensor_reduce(rmax[:, 8 * half + c:8 * half + 8:2], bank_hs[half][c][:, :].rearrange("p (h t) -> p h t", t=T), AX.X, ALU.max)
                            mm.then_inc(S["max_done"], 1)

                        if A:
                            if not (isinstance(b, int) and b < 0):
                                dve.wait_ge(S["ht_mm"], n + 1)
                            if rms:
                                nc.vector.tensor_scalar(hn[:, u, :], x_all[:, b + 2, :], rstd_all[:, bass.ds(b + 2, 1)], gain[:, 0:1], ALU.mult, ALU.mult).then_inc(S["hn_done"], 1)
                            else:
                                nc.vector.tensor_scalar(hn[:, u, :], x_all[:, b + 2, :], mean_all[:, bass.ds(b + 2, 1)], rstd_all[:, bass.ds(b + 2, 1)], ALU.subtract, ALU.mult).then_inc(S["hn_done"], 1)
                        if B_ and rms:
                            dve.wait_ge(S["rq_done"], 2 * n + 4)
                            nc.vector.tensor_tensor(qk[:, :].rearrange("p (g d) -> p g d", d=DH), qkvs[:, w, 0:2 * D].rearrange("p (g d) -> p g d", d=DH),
                                                    rq[:, :].unsqueeze(2).to_broadcast([P, 2 * H, DH]), ALU.mult).then_inc(S["qkn_done"], 1)
                        if A:
                            dve.wait_ge(S["ht_mm"], n + 3)
                            nc.vector.tensor_scalar(ht0[:, u, :], b_t[:, 0:T], mod[:, l, 1, bass.ds(b + 2, 1)], mod[:, l, 0, bass.ds(b + 2, 1)], ALU.mult, ALU.add).then_inc(S["ht_done"], 1)
                            nc.vector.tensor_scalar(ht1[0:DT, u, :], b_t[0:DT, T:2 * T], modt[:, l, 1, bass.ds(b + 2, 1)], modt[:, l, 0, bass.ds(b + 2, 1)], ALU.mult, ALU.add).then_inc(S["ht_done"], 1)
                        if B_:
                            dve.wait_ge(S["high_done"], 2 * n + 4)
                            src = qk[:, :] if rms else qkvs[:, w, 0:2 * D]
                            pieces = stack[:, :, :, 0:PIECES * DH].rearrange("p s h (c d) -> p s h c d", d=DH)
                            nc.vector.tensor_tensor(rest[:, :].rearrange("p (s h d) -> p s h d", s=2, d=DH), src.rearrange("p (s h d) -> p s h d", s=2, d=DH),
                                                    pieces[:, :, :, 1, :], ALU.subtract).then_inc(S["rest_done"], 1)
                        if C:
                            row_max(0)
                            row_max(1)
                            dve.wait_ge(S["max_done"], 2 * n + 2)
                            top = rmax[:, :].rearrange("p (j c) -> p c j", c=2)
                            high, low = neg[:, :, 0:H:2], neg[:, :, 1:H:2]
                            nc.vector.tensor_scalar(high, top, -1.0, None, ALU.mult).then_inc(S["neg_done"], 1)
                            dve.wait_ge(S["neg_done"], 2 * n + 1)
                            nc.vector.scalar_tensor_tensor(out=low, in0=top, scalar=-1.0, in1=high, op0=ALU.mult, op1=ALU.subtract).then_inc(S["neg_done"], 1)
                        if D_:
                            heads = b_ov[:, :].rearrange("p (h s) -> p h s", s=32)
                            dve.wait_ge(S["back_mm"], n)
                            nc.vector.reciprocal(rsum[:, :], heads[:, :, DH]).then_inc(S["rsum_done"], 1)
                            dve.wait_ge(S["rsum_done"], n)
                            nc.vector.tensor_tensor(at[:, w, :].rearrange("p (h d) -> p h d", d=DH), heads[:, :, 0:DH], rsum[:, :].unsqueeze(2).to_broadcast([P, H, DH]), ALU.mult).then_inc(S["at_done"], 1)
                        if C:
                            dve.wait_ge(S["negt_mm"], n + 1)
                            nc.vector.tensor_copy(negt[:, :], t16[:, 0:T]).then_inc(S["negt_done"], 1)
                        if A and rms:
                            dve.wait_ge(S["square_done"], n + 3)
                            nc.vector.tensor_reduce(ssum[:, :], sq[:, :].rearrange("p (g d) -> p g d", d=DH), AX.X, ALU.add).then_inc(S["ssum_done"], 1)
                            dve.wait_ge(S["ssum_done"], 2 * n + 5)
                            nc.vector.tensor_scalar(ssum[:, :], ssum[:, :], 1e-24, None, ALU.max).then_inc(S["ssum_done"], 1)
                        if B_:
                            dve.wait_ge(S["qs_mm"], n + 2)
                            nc.vector.tensor_copy(qs[:, w, :, :], tp16).then_inc(S["qs_done"], 1)
                        if F:
                            dve.wait_ge(S["proj_mm"], n - 1)
                            nc.vector.tensor_tensor(upd[:, u, :], b_mm[:, 0:D], gate_all[:, 0, b - 2, :], ALU.mult).then_inc(S["upd_done"], 1)
                            dve.wait_ge(S["upd_done"], n - 1)
                            nc.vector.tensor_tensor(x_all[:, b - 2, :], x_all[:, b - 2, :], upd[:, u, :], ALU.add).then_inc(S["x_new"], 1)
                            dve.wait_ge(ones_ready, 1)
                            dve.wait_ge(S["x_new"], n - 1)
                            nc.vector.bn_stats(stats[:, u, :], x_all[:, b - 2, :]).then_inc(S["stat_done"], 1)
                            dve.wait_ge(ones_ready, 1)
                            dve.wait_ge(S["stat_done"], n - 1)
                            nc.vector.bn_aggr(aggr[:, u, :], stats[:, u, :]).then_inc(S["aggr_done"], 1)
                            dve.wait_ge(S["aggr_done"], n - 1)
                            variance(dve, rms, aggr[:, u], b - 2, S["var_new"], S["ms_done"], b - 2)
                    drive(nc.vector, step)
                    dve.wait_ge(S["var_new"], base + B)


        def mlp(l):
            experts = E if l == 2 else 1
            phase = 2 * l + 1
            rms = l == 1
            gelu = ACT.Gelu if l == 0 else ACT.Gelu_apprx_tanh
            off = 3 * D + D + GATE_W[l]
            off2 = off + experts * HID
            groups = B // G
            with ExitStack() as c:
                def tsb(name, shape, dt=F32):
                    return c.enter_context(nc.sbuf_tensor(f"m{l}_{name}", shape, dt))

                hn = tsb("hn", [P, G, D])
                h0 = tsb("h0", [P, 2, G * T])
                h1 = tsb("h1", [DT + 1, 2, G * T])
                hid = tsb("hid", [P, 2, MT, G * T])
                upd = tsb("upd", [P, G, D])
                st = tsb("st", [P, G, 6])
                ag = tsb("ag", [P, G, 2])
                lg = tsb("lg", [P, G, E])
                cmp = tsb("cmp", [P, G, E, E])
                cmp2 = tsb("cmp2", [P, G, E, E])
                sel = tsb("sel", [P, G, E])
                wts = tsb("wts", [P, 2, G, E])
                tops = tsb("tops", [P, G])
                below = tsb("below", [P, E, E])
                names = "set hn_done h_mm h_done fc1_mm gelu_done fc2_mm upd_done x_new ".split()
                names += ("stat_done aggr_done var_new rstd_new" + " ms_done" * (l == 0) if l < 2 else
                          "lg_mm lg_done route exp_done sel_done wts_done gated stored").split()
                S = {k: sem(f"m{l}_" + k) for k in names}
                b_h0, b_h1, b_lg = bank[0], bank[1], bank[1]
                b_fc1 = [bank[2], bank[3], bank[4], bank[5]]
                b_fc2 = [bank[6], bank[7]]

                def drive(eng, step):
                    step(-1, 1, products=False)
                    step(0, 0)
                    with eng.Fori(0, (groups - 2) // 2) as i:
                        step(i * 2 + 1, 1)
                        step(i * 2 + 2, 0)
                    step(groups - 1, 1, front=False)

                def width(m):
                    return P if m < MT - 1 else HL

                with nc.Block() as block:
                    @block.tensor
                    def _(pe):
                        def step(g, u, front=True, products=True):
                            w = 1 - u

                            def fc1(e):
                                for m in range(MT):
                                    t_done = (g * experts + e) * MT + m
                                    if not isinstance(g, int) or t_done >= 4:
                                        pe.wait_ge(S["set"], 2)
                                        pe.wait_ge(S["gelu_done"], t_done - 3)
                                    o = off + e * HID + m * P
                                    dst = b_fc1_of(t_done_mod(g, u, e, m))[0:width(m), :]
                                    nc.tensor.matmul(dst, w_main[l][:, o:o + width(m)], h0[:, u, :], start=True, stop=False)
                                    nc.tensor.matmul(dst, w_tail[l][:, o:o + width(m)], h1[:, u, :], start=False, stop=True).then_inc(S["fc1_mm"], 1)

                            def fc2(e):
                                pe.wait_ge(S["gelu_done"], (g * experts + e + 1) * MT)
                                if not isinstance(g, int) or g or e:
                                    pe.wait_ge(S["upd_done"], (g * experts + e) * 2)
                                for s in range(G):
                                    for m in range(MT):
                                        k = P if m < MT - 1 else HL + 1
                                        wt = w_main[l][:, off2 + (e * 4 + m) * D:off2 + (e * 4 + m + 1) * D] if m < MT - 1 else w_last[l][:, e * D:(e + 1) * D]
                                        mm = nc.tensor.matmul(b_fc2[s // 2][:, (s % 2) * D:(s % 2 + 1) * D], hid[0:k, e % 2 if experts > 1 else u, m, s * T:(s + 1) * T], wt,
                                                              start=(m == 0), stop=(m == MT - 1))
                                    if s % 2:
                                        mm.then_inc(S["fc2_mm"], 1)

                            if products:
                                pe.wait_ge(S["h_done"], g * 2 * G + 2 * G)
                                fc1(0)
                                for e in range(1, experts):
                                    fc1(e)
                                    fc2(e - 1)
                            if front:
                                pe.wait_ge(S["hn_done"], g * G + 2 * G)
                                for s in range(G):
                                    nc.tensor.transpose(b_h0[:, s * T:(s + 1) * T], hn[:, s, 0:P], ident[:, :])
                                for s in range(G):
                                    if s == 0 and l == 2 and products:
                                        pe.wait_ge(S["lg_done"], g + 1)
                                    mm = nc.tensor.transpose(b_h1[0:DT, s * T:(s + 1) * T], hn[:, s, P:D], ident[:, :])
                                mm.then_inc(S["h_mm"], 1)
                            if products:
                                fc2(experts - 1)
                            if front and l == 2:
                                pe.wait_ge(S["set"], 2)
                                pe.wait_ge(S["h_done"], g * 2 * G + 4 * G)
                                for s in range(G):
                                    nc.tensor.matmul(b_lg[:, s * E:(s + 1) * E], h0[:, w, s * T:(s + 1) * T], w_main[2][:, off - E:off], start=True, stop=False)
                                    mm = nc.tensor.matmul(b_lg[:, s * E:(s + 1) * E], h1[:, w, s * T:(s + 1) * T], w_tail[2][:, off - E:off], start=False, stop=True)
                                mm.then_inc(S["lg_mm"], 1)

                        def t_done_mod(g, u, e, m):
                            return (u * experts * MT + e * MT + m) % 4 if (2 * experts * MT) % 4 == 0 else (u * 2 + m) % 4

                        def b_fc1_of(j):
                            return b_fc1[j]

                        drive(nc.tensor, step)

                    @block.scalar
                    def _(act):
                        def step(g, u, front=True, products=True):
                            w = 1 - u
                            if products:
                                for e in range(experts):
                                    for m in range(MT):
                                        tile = (g * experts + e) * MT + m
                                        j = (u * experts * MT + e * MT + m) % 4 if (2 * experts * MT) % 4 == 0 else (u * 2 + m) % 4
                                        if m == 0:
                                            if experts > 1 and (not isinstance(g, int) or g * experts + e >= 2):
                                                act.wait_ge(S["set"], 2)
                                                act.wait_ge(S["fc2_mm"], (g * experts + e) * 2 - 2)
                                            elif experts == 1 and (not isinstance(g, int) or g >= 1):
                                                act.wait_ge(S["fc2_mm"], g * 2)
                                        act.wait_ge(S["fc1_mm"], tile + 1)
                                        nc.scalar.activation(hid[0:width(m), e % 2 if experts > 1 else u, m, :], b_fc1[j][0:width(m), :], gelu).then_inc(S["gelu_done"], 1)
                            if front and l == 2:
                                act.wait_ge(S["route"], g + 2)
                                nc.scalar.activation(wts[:, w, :, :], lg[:, :, :], ACT.Exp).then_inc(S["exp_done"], 1)

                        drive(nc.scalar, step)

                    @block.gpsimd
                    def _(pool):
                        def step(g, u, front=True, products=True):
                            if products:
                                pool.wait_ge(S["var_new"], g * G + G)
                                nc.gpsimd.tensor_tensor(rstd_all[:, bass.ds(g * G, G)], var_all[:, bass.ds(g * G, G)], mhalf[:, :].to_broadcast([P, G]), ALU.pow).then_inc(S["rstd_new"], 1)

                        if l < 2:
                            drive(nc.gpsimd, step)
                            pool.wait_ge(S["rstd_new"], groups)

                    @block.sync
                    def _(sp):
                        if l < 2:
                            load_gates(sp, phase + 1)
                        else:
                            def step(g, u, front=True, products=True):
                                if products:
                                    sp.wait_ge(S["x_new"], g + 1)
                                    sp.dma_start(t["out"][bass.ds(g * G, G)].rearrange("b t d -> t b d"), x_all[:, bass.ds(g * G, G), :]).then_inc(S["stored"], 16)

                            drive(nc.sync, step)
                            sp.wait_ge(S["stored"], groups * 16)

                    @block.vector
                    def _(dve):
                        def step(g, u, front=True, products=True):
                            w = 1 - u
                            if front:
                                for s in range(G):
                                    q = g * G + G + s
                                    if products and s == 0:
                                        dve.wait_ge(S["h_mm"], g + 1)
                                    if l == 1:
                                        nc.vector.tensor_scalar(hn[:, s, :], x_all[:, q, :], rstd_all[:, bass.ds(q, 1)], gain[:, 1:2], ALU.mult, ALU.mult).then_inc(S["hn_done"], 1)
                                    else:
                                        nc.vector.tensor_scalar(hn[:, s, :], x_all[:, q, :], mean_all[:, bass.ds(q, 1)], rstd_all[:, bass.ds(q, 1)], ALU.subtract, ALU.mult).then_inc(S["hn_done"], 1)

                            def take(e):
                                for half in range(2):
                                    dve.wait_ge(S["fc2_mm"], (g * experts + e) * 2 + 1 + half)
                                    if experts == 1:
                                        nc.vector.tensor_tensor(upd[:, 2 * half:2 * half + 2, :], b_fc2[half][:, 0:2 * D].rearrange("p (s d) -> p s d", d=D),
                                                                gate_all[:, 1, bass.ds(g * G + 2 * half, 2), :], ALU.mult).then_inc(S["upd_done"], 1)
                                        continue
                                    for s in range(2 * half, 2 * half + 2):
                                        src = b_fc2[half][:, (s % 2) * D:(s % 2 + 1) * D]
                                        if e == 0:
                                            if s == 0:
                                                dve.wait_ge(S["wts_done"], g + 1)
                                            mm = nc.vector.tensor_scalar(upd[:, s, :], src, wts[:, u, s, e:e + 1], None, ALU.mult)
                                        else:
                                            if s == 2 * half:
                                                dve.wait_ge(S["upd_done"], (g * experts + e) * 2 + half - 1)
                                            mm = nc.vector.scalar_tensor_tensor(out=upd[:, s, :], in0=src, scalar=wts[:, u, s, e:e + 1], in1=upd[:, s, :], op0=ALU.mult, op1=ALU.add)
                                    mm.then_inc(S["upd_done"], 1)

                            if products:
                                for e in range(experts - 1):
                                    take(e)
                            if front:
                                dve.wait_ge(S["h_mm"], g + 2)
                                for s in range(G):
                                    q = g * G + G + s
                                    nc.vector.tensor_scalar(h0[:, w, s * T:(s + 1) * T], b_h0[:, s * T:(s + 1) * T], mod[:, l, 3, bass.ds(q, 1)], mod[:, l, 2, bass.ds(q, 1)], ALU.mult, ALU.add).then_inc(S["h_done"], 1)
                                for s in range(G):
                                    q = g * G + G + s
                                    nc.vector.tensor_scalar(h1[0:DT, w, s * T:(s + 1) * T], b_h1[0:DT, s * T:(s + 1) * T], modt[:, l, 3, bass.ds(q, 1)], modt[:, l, 2, bass.ds(q, 1)], ALU.mult, ALU.add).then_inc(S["h_done"], 1)
                            if products:
                                take(experts - 1)
                                xs = x_all[:, bass.ds(g * G, G), :]
                                dve.wait_ge(S["upd_done"], (g * experts + experts) * 2)
                                if experts > 1:
                                    nc.vector.tensor_tensor(upd[:, :, :], upd[:, :, :], gate_all[:, 1, bass.ds(g * G, G), :], ALU.mult).then_inc(S["gated"], 1)
                                    dve.wait_ge(S["gated"], g + 1)
                                nc.vector.tensor_tensor(xs, xs, upd[:, :, :], ALU.add).then_inc(S["x_new"], 1)
                                if l < 2:
                                    dve.wait_ge(ones_ready, 1)
                                    dve.wait_ge(S["x_new"], g + 1)
                                    for s in range(G):
                                        mm = nc.vector.bn_stats(st[:, s, :], x_all[:, g * G + s, :])
                                    mm.then_inc(S["stat_done"], 1)
                                    dve.wait_ge(ones_ready, 1)
                                    dve.wait_ge(S["stat_done"], g + 1)
                                    for s in range(G):
                                        mm = nc.vector.bn_aggr(ag[:, s, :], st[:, s, :])
                                    mm.then_inc(S["aggr_done"], 1)
                                    dve.wait_ge(S["aggr_done"], g + 1)
                                    for s in range(G):
                                        variance(dve, l == 0, ag[:, s], g * G + s, S["var_new"], S.get("ms_done"), g * G + s)
                            if front and l == 2:
                                dve.wait_ge(S["lg_mm"], g + 2)
                                nc.vector.tensor_copy(lg[:, :, :], b_lg[:, 0:G * E].rearrange("p (s e) -> p s e", e=E)).then_inc(S["lg_done"], 1)
                                dve.wait_ge(S["lg_done"], g + 2)
                                other = lg[:, :, :].unsqueeze(2).to_broadcast([P, G, E, E])
                                own = lg[:, :, :].unsqueeze(3).to_broadcast([P, G, E, E])
                                step_of = (g + 1) * 9
                                nc.vector.tensor_tensor(cmp[:, :, :, :], other, own, ALU.is_gt).then_inc(S["sel_done"], 1)
                                nc.vector.tensor_tensor(cmp2[:, :, :, :], other, own, ALU.is_equal).then_inc(S["sel_done"], 1)
                                nc.vector.tensor_reduce(tops[:, :], lg[:, :, :], AX.X, ALU.max).then_inc(S["sel_done"], 1)
                                dve.wait_ge(S["sel_done"], step_of + 3)
                                nc.vector.tensor_tensor(cmp2[:, :, :, :], cmp2[:, :, :, :], below[:, :, :].unsqueeze(1).to_broadcast([P, G, E, E]), ALU.mult).then_inc(S["sel_done"], 1)
                                nc.vector.tensor_tensor(lg[:, :, :], lg[:, :, :], tops[:, :].unsqueeze(2).to_broadcast([P, G, E]), ALU.subtract).then_inc(S["route"], 1)
                                dve.wait_ge(S["sel_done"], step_of + 4)
                                nc.vector.tensor_tensor(cmp[:, :, :, :], cmp[:, :, :, :], cmp2[:, :, :, :], ALU.add).then_inc(S["sel_done"], 1)
                                dve.wait_ge(S["sel_done"], step_of + 5)
                                nc.vector.tensor_reduce(sel[:, :, :], cmp[:, :, :, :], AX.X, ALU.add).then_inc(S["sel_done"], 1)
                                dve.wait_ge(S["sel_done"], step_of + 6)
                                dve.wait_ge(S["exp_done"], g + 2)
                                nc.vector.scalar_tensor_tensor(out=wts[:, w, :, :], in0=sel[:, :, :], scalar=1.5, in1=wts[:, w, :, :], op0=ALU.is_lt, op1=ALU.mult).then_inc(S["sel_done"], 1)
                                dve.wait_ge(S["sel_done"], step_of + 7)
                                nc.vector.tensor_reduce(tops[:, :], wts[:, w, :, :], AX.X, ALU.add).then_inc(S["sel_done"], 1)
                                dve.wait_ge(S["sel_done"], step_of + 8)
                                nc.vector.reciprocal(tops[:, :], tops[:, :]).then_inc(S["sel_done"], 1)
                                dve.wait_ge(S["sel_done"], step_of + 9)
                                nc.vector.tensor_tensor(wts[:, w, :, :], wts[:, w, :, :], tops[:, :].unsqueeze(2).to_broadcast([P, G, E]), ALU.mult).then_inc(S["wts_done"], 1)

                        nc.vector.memset(h1[:, :, :], 1.0).then_inc(S["set"], 1)
                        nc.vector.memset(hid[:, :, MT - 1, :], 1.0).then_inc(S["set"], 1)
                        if l == 2:
                            nc.vector.memset(below[:, :, :], 0.0).then_inc(S["set"], 1)
                            dve.wait_ge(S["set"], 3)
                            for e in range(1, E):
                                nc.vector.memset(below[:, e, 0:e], 1.0).then_inc(S["set"], 1)
                            dve.wait_ge(S["set"], 3 + E - 1)
                        else:
                            dve.wait_ge(S["set"], 2)
                        drive(nc.vector, step)
                        if l == 2:
                            dve.wait_ge(S["x_new"], groups)
                        else:
                            dve.wait_ge(S["var_new"], B)

        mlp(0)
        attention(1)
        mlp(1)
        attention(2)
        mlp(2)


def lay_out(x):
    def wb(w, b):
        return np.concatenate([w, b[None]], 0)

    def fc2(w, b):
        main = w[:4 * P].reshape(4, P, D).transpose(1, 0, 2).reshape(P, 4 * D)
        return main, np.concatenate([w[4 * P:], b[None]], 0)

    a = {"x": x["x"], "cond": x["cond_1152"], "pt": x["L0_cond_P"].T}
    iu, ju = np.triu_indices(R, 1)
    skew = np.zeros((D + 1, R, R), np.float32)
    for i, j in ((iu, ju), (ju, iu)):
        skew[:D, i, j] = x["L0_cond_W"].T
        skew[D, i, j] = x["L0_cond_b"]
    a["skew"] = skew.reshape(D + 1, R * R)
    sign = np.sign(np.arange(R)[None, :] - np.arange(R)[:, None]).astype(np.float32)
    a["sign"] = np.concatenate([sign, sign], 0)
    a["ident"] = np.eye(P, dtype=np.float32)
    a["gains"] = np.concatenate([x["L2_cond_g1"], x["L2_cond_g2"], x["L2_cond_qg"], x["L2_cond_kg"]])
    a["ada"] = np.stack([wb(x["L1_cond_ada_w"], x["L1_cond_ada_b"]), wb(x["L2_cond_ada_w"].T, x["L2_cond_ada_b"]),
                         wb(x["L3_cond_w_adaln"], x["L3_cond_b_adaln"])])
    for l, (qkv, proj, fc1, f2) in enumerate((
        (wb(x["L1_cond_qkv_w"], x["L1_cond_qkv_b"]), wb(x["L1_cond_proj_w"], x["L1_cond_proj_b"]),
         [wb(x["L1_cond_fc1_w"], x["L1_cond_fc1_b"])], [fc2(x["L1_cond_fc2_w"], x["L1_cond_fc2_b"])]),
        (wb(x["L2_cond_qkv_w"].T, x["L2_cond_qkv_b"]), wb(x["L2_cond_proj_w"].T, x["L2_cond_proj_b"]),
         [wb(x["L2_cond_fc1_w"].T, x["L2_cond_fc1_b"])], [fc2(x["L2_cond_fc2_w"].T, x["L2_cond_fc2_b"])]),
        (wb(x["L3_cond_w_qkv"], x["L3_cond_b_qkv"]), wb(x["L3_cond_w_proj"], x["L3_cond_b_proj"]),
         [wb(x["L3_cond_w_gate"], np.zeros(E, np.float32))] + [wb(x["L3_cond_w1"][e], x["L3_cond_b1"][e]) for e in range(E)],
         [fc2(x["L3_cond_w2"][e], x["L3_cond_b2"][e]) for e in range(E)]),
    )):
        first = np.concatenate([qkv, proj] + fc1, 1)
        a[f"main{l}"] = np.concatenate([first[:P]] + [m for m, _ in f2], 1)
        a[f"tail{l}"] = first[P:]
        a[f"last{l}"] = np.concatenate([m for _, m in f2], 1)
    return {k: np.ascontiguousarray(v) for k, v in a.items()}


def kernel(**inputs):
    import concourse.bacc as bacc
    from concourse.bass_utils import run_bass_kernel_spmd

    nc = bacc.Bacc("TRN2", target_bir_lowering=False, num_devices=1)
    arrays = lay_out({k: np.asarray(v) for k, v in inputs.items()})
    tensors = {k: nc.dram_tensor("in_" + k, a.shape, mybir.dt.from_np(a.dtype), kind="ExternalInput").ap() for k, a in arrays.items()}
    tensors["out"] = nc.dram_tensor("out", [B, T, D], F32, kind="ExternalOutput").ap()
    program(nc, tensors)
    r = run_bass_kernel_spmd(nc, [{"in_" + k: a for k, a in arrays.items()}], core_ids=[0])
    return r.results[0]["out"]
```

```python
from contextlib import ExitStack

import numpy as np
import concourse.bass as bass
from concourse import mybir

F32 = mybir.dt.float32
BF16 = mybir.dt.bfloat16
F32R = mybir.dt.float32r
ACT = mybir.ActivationFunctionType
ALU = mybir.AluOpType
AX = mybir.AxisListType

P = 128
B = 32
T = 128
D = 144
DT = D - P
H = 16
DH = D // H
HID = 4 * D
MT = 5
HL = HID - 4 * P
R = 64
E = 4
L = 3
G = 4
PAIRS = B // 2
SLOT = 64
PIECES = 6
DOUBLINGS = 10
SM = DH ** -0.5

EXPERTS = [1, 1, E]
GATE_W = [0, 0, E]
QKV_W = [3 * D, 0, 0]
SPLIT_QKV_W = [0, 3 * D, 3 * D]
MAIN_W = [QKV_W[l] + D + GATE_W[l] + EXPERTS[l] * 4 * D for l in range(L)]
TAIL_W = [QKV_W[l] + D + GATE_W[l] for l in range(L)]
SPLIT_W = [SPLIT_QKV_W[l] + EXPERTS[l] * HID for l in range(L)]
LAST_W = [D, D, E * D]
W_LOADED = 5 * 16


def program(nc, t):
    ctx = ExitStack()
    with ctx:
        def sb(name, shape, dt=F32):
            return ctx.enter_context(nc.sbuf_tensor(name, shape, dt))

        def sem(name):
            return ctx.enter_context(nc.semaphore(name))

        bank = [ctx.enter_context(nc.psum_tensor(f"bank{i}", [P, 512], F32)) for i in range(8)]

        x_all = sb("x_all", [P, B, D])
        ident = sb("ident", [P, P])
        identb = sb("identb", [P, P], BF16)
        w_main = [sb(f"w_main{l}", [P, MAIN_W[l]]) for l in range(L)]
        w_tail = [sb(f"w_tail{l}", [DT + 1, TAIL_W[l]]) for l in range(L)]
        w_last = [sb(f"w_last{l}", [HL + 1, LAST_W[l]]) for l in range(L)]
        w_hi = [sb(f"w_hi{l}", [P, SPLIT_W[l]], F32R) for l in range(L)]
        w_lo = [sb(f"w_lo{l}", [P, SPLIT_W[l]], F32R) for l in range(L)]
        w_st = [sb(f"w_st{l}", [P, SPLIT_W[l]], F32R) for l in range(L)]
        mod = sb("mod", [P, L, 4, B])
        modt = sb("modt", [P, L, 4, B])
        mean_all = sb("mean_all", [P, B])
        rstd_all = sb("rstd_all", [P, B])
        var_all = sb("var_all", [P, B])
        stats = sb("stats", [P, 2, 6])
        aggr = sb("aggr", [P, 2, 2])
        mhalf = sb("mhalf", [P, 1])
        phalf = sb("phalf", [P, 1])
        zero = sb("zero", [P, 1])
        gain = sb("gain", [P, 4])

        consts_in = sem("consts_in")
        w_in = [sem(f"w_in{l}") for l in range(L)]
        ones_ready = sem("ones_ready")
        gates_in = sem("gates_in")
        gates_out = sem("gates_out")
        scratch = nc.dram_tensor("gates_dram", [L * 2, B, D], F32, kind="Internal").ap()
        araw_dram = nc.dram_tensor("araw_dram", [B, R, R], F32, kind="Internal").ap()

        def load_gates(eng, phase):
            src = bass.AP(tensor=scratch.tensor, offset=phase * B * D, ap=[[0, P], [1, B * D]])
            eng.dma_start(gate_all[:, phase % 2].rearrange("p b d -> p (b d)"), src).then_inc(gates_in, 16)
            eng.wait_ge(gates_in, 16 * (phase + 1))

        adapter = ExitStack()
        with adapter:
            def asb(name, shape, dt=F32):
                return adapter.enter_context(nc.sbuf_tensor(name, shape, dt))

            qt = asb("qt", [P, D])
            u0 = asb("u0", [P, R])
            u1 = asb("u1", [DT, R])
            ex = asb("ex", [P, PAIRS, R])
            ey = asb("ey", [P, PAIRS, R])
            ez = asb("ez", [P, PAIRS, R])
            ew = asb("ew", [P, PAIRS, R])

            with ExitStack() as c:
                def tsb(name, shape, dt=F32):
                    return c.enter_context(nc.sbuf_tensor(name, shape, dt))

                def tsem(name):
                    return c.enter_context(nc.semaphore(name))

                cond = tsb("cond", [B, D])
                th = tsb("th", [B, D])
                sil = tsb("sil", [B, D])
                sc0 = tsb("sc0", [P, B])
                sc1 = tsb("sc1", [DT + 1, B])
                ada0 = tsb("ada0", [P, L, 6 * D])
                ada1 = tsb("ada1", [DT + 1, L, 6 * D])
                adat0 = tsb("adat0", [P, L, 4, P])
                adat1 = tsb("adat1", [DT + 1, L, 4, P])
                sk0 = tsb("sk0", [P, R * R])
                sk1 = tsb("sk1", [DT + 1, R * R])
                araw = tsb("araw", [B, R * R])
                gates = tsb("gates", [B, L * 2, D])
                sign = tsb("sign", [P, R])
                cond_in = tsem("cond_in")
                ada_in = tsem("ada_in")
                skew_in = tsem("skew_in")
                th_done = tsem("th_done")
                sil_done = tsem("sil_done")
                sct_done = tsem("sct_done")
                sc_done = tsem("sc_done")
                ada_done = tsem("ada_done")
                gate_mm = tsem("gate_mm")
                gate_ev = tsem("gate_ev")
                mod_ev = tsem("mod_ev")
                raw_mm = tsem("raw_mm")
                raw_ev_act = tsem("raw_ev_act")
                raw_ev_dve = tsem("raw_ev_dve")
                raw_out = tsem("raw_out")
                raw_back = tsem("raw_back")

                with nc.Block() as block:
                    @block.sync
                    def _(sp):
                        sp.dma_start(ident[:, :], t["ident"]).then_inc(consts_in, 16)
                        sp.dma_start(cond[:, :], t["cond"]).then_inc(cond_in, 16)
                        sp.dma_start(sign[:, :], t["sign"]).then_inc(consts_in, 16)
                        sp.dma_start(qt[0:R, :], t["pt"]).then_inc(consts_in, 16)
                        for j in range(4):
                            sp.dma_start(gain[:, j:j + 1], bass.AP(tensor=t["gains"].tensor, offset=j, ap=[[0, P], [1, 1]])).then_inc(consts_in, 16)
                        sp.dma_start(ada0[:, :, :], t["ada"][:, 0:P].rearrange("l k n -> k l n")).then_inc(ada_in, 16)
                        sp.dma_start(ada1[:, :, :], t["ada"][:, P:].rearrange("l k n -> k l n")).then_inc(ada_in, 16)
                        sp.dma_start(adat0[:, :, :, :], t["adat"][:, :, 0:P].rearrange("l w k n -> k l w n")).then_inc(ada_in, 16)
                        sp.dma_start(adat1[:, :, :, :], t["adat"][:, :, P:].rearrange("l w k n -> k l w n")).then_inc(ada_in, 16)
                        sp.dma_start(x_all[:, :, :], t["x"].rearrange("b t d -> t b d")).then_inc(consts_in, 16)
                        sp.wait_ge(raw_ev_act, 4)
                        sp.wait_ge(raw_ev_dve, 4)
                        sp.dma_start(araw_dram.rearrange("b i j -> b (i j)"), araw[:, :]).then_inc(raw_out, 16)
                        sp.wait_ge(raw_out, 16)
                        halves = araw_dram.rearrange("(q h) i j -> h i q j", h=2)
                        for half in range(2):
                            sp.dma_start(ex[half * R:(half + 1) * R, :, :], halves[half]).then_inc(raw_back, 16)
                        sp.wait_ge(gate_ev, L * 2)
                        sp.dma_start(scratch.rearrange("g b d -> b g d"), gates[:, :, :]).then_inc(gates_out, 16)
                        sp.wait_ge(gates_out, 16)

                    @block.scalar
                    def _(act):
                        act.dma_start(sk0[:, :], t["skew"][0:P]).then_inc(skew_in, 16)
                        act.dma_start(sk1[:, :], t["skew"][P:]).then_inc(skew_in, 16)
                        act.wait_ge(cond_in, 16)
                        nc.scalar.activation(th[:, :], cond[:, :], ACT.Tanh, scale=0.5).then_inc(th_done, 1)
                        for l in range(L):
                            act.dma_start(w_main[l][:, :], t[f"main{l}"]).then_inc(w_in[l], 16)
                            act.dma_start(w_tail[l][:, :], t[f"tail{l}"]).then_inc(w_in[l], 16)
                            act.dma_start(w_last[l][:, :], t[f"last{l}"]).then_inc(w_in[l], 16)
                        for g in range(L * 2):
                            act.wait_ge(gate_mm, g + 1)
                            f = ACT.Tanh if g // 2 == 1 else ACT.Copy
                            nc.scalar.activation(gates[:, g, :], bank[2 + g // 3][0:B, (g % 3) * D:(g % 3 + 1) * D], f).then_inc(gate_ev, 1)
                        for n in range(0, 8, 2):
                            act.wait_ge(raw_mm, n + 1)
                            nc.scalar.copy(araw[:, n * 512:(n + 1) * 512], bank[4 + n % 4][0:B, :]).then_inc(raw_ev_act, 1)

                    @block.vector
                    def _(dve):
                        nc.vector.memset(mhalf[:, :], -0.5).then_inc(ones_ready, 1)
                        nc.vector.memset(phalf[:, :], 0.5).then_inc(ones_ready, 1)
                        nc.vector.memset(zero[:, :], 0.0).then_inc(ones_ready, 1)
                        nc.vector.memset(sc1[:, :], 1.0).then_inc(ones_ready, 1)
                        dve.wait_ge(consts_in, 16 * 8)
                        nc.vector.tensor_copy(identb[:, :], ident[:, :]).then_inc(ones_ready, 1)
                        dve.wait_ge(th_done, 1)
                        nc.vector.scalar_tensor_tensor(out=sil[:, :], in0=th[:, :], scalar=1.0, in1=cond[:, :], op0=ALU.add, op1=ALU.mult).then_inc(sil_done, 1)
                        dve.wait_ge(sct_done, 1)
                        dve.wait_ge(ones_ready, 5)
                        nc.vector.tensor_scalar(sc0[:, :], bank[0][:, 0:B], 0.5, None, ALU.mult).then_inc(sc_done, 1)
                        nc.vector.tensor_scalar(sc1[0:DT, :], bank[0][0:DT, B:2 * B], 0.5, None, ALU.mult).then_inc(sc_done, 1)
                        for which in range(4):
                            dve.wait_ge(ada_done, 1)
                            one = float(which % 2)
                            nc.vector.tensor_scalar(mod[:, :, which, :], bank[0][:, 0:L * 4 * B].rearrange("p (l w b) -> p l w b", l=L, w=4)[:, :, which, :], one, None, ALU.add).then_inc(mod_ev, 1)
                            nc.vector.tensor_scalar(modt[:, :, which, :], bank[1][:, 0:L * 4 * B].rearrange("p (l w b) -> p l w b", l=L, w=4)[:, :, which, :], one, None, ALU.add).then_inc(mod_ev, 1)
                        for n in range(1, 8, 2):
                            dve.wait_ge(raw_mm, n + 1)
                            nc.vector.tensor_copy(araw[:, n * 512:(n + 1) * 512], bank[4 + n % 4][0:B, :]).then_inc(raw_ev_dve, 1)
                        dve.wait_ge(raw_back, 32)
                        nc.vector.scalar_tensor_tensor(out=ex[:, :, :], in0=ex[:, :, :], scalar=2.0 ** -DOUBLINGS,
                                                       in1=sign[:, :].unsqueeze(1).to_broadcast([P, PAIRS, R]), op0=ALU.mult, op1=ALU.mult).then_inc(mod_ev, 1)
                        dve.wait_ge(mod_ev, 9)

                    @block.tensor
                    def _(pe):
                        pe.wait_ge(sil_done, 1)
                        nc.tensor.transpose(bank[0][:, 0:B], sil[:, 0:P], ident[0:B, 0:B])
                        nc.tensor.transpose(bank[0][0:DT, B:2 * B], sil[:, P:D], ident[0:B, 0:B]).then_inc(sct_done, 1)
                        pe.wait_ge(sc_done, 2)
                        pe.wait_ge(ada_in, 64)
                        for l in range(L):
                            for w, col in enumerate((0, 1, 3, 4)):
                                o = (l * 4 + w) * B
                                nc.tensor.matmul(bank[0][:, o:o + B], ada0[:, l, col * D:col * D + P], sc0[:, :], start=True, stop=False)
                                nc.tensor.matmul(bank[0][:, o:o + B], ada1[:, l, col * D:col * D + P], sc1[:, :], start=False, stop=True)
                                nc.tensor.matmul(bank[1][:, o:o + B], adat0[:, l, w, :], sc0[:, :], start=True, stop=False)
                                last = nc.tensor.matmul(bank[1][:, o:o + B], adat1[:, l, w, :], sc1[:, :], start=False, stop=True)
                        last.then_inc(ada_done, 1)
                        for g in range(L * 2):
                            col = 2 + 3 * (g % 2)
                            o = (g % 3) * D
                            nc.tensor.matmul(bank[2 + g // 3][0:B, o:o + D], sc0[:, :], ada0[:, g // 2, col * D:(col + 1) * D], start=True, stop=False)
                            last = nc.tensor.matmul(bank[2 + g // 3][0:B, o:o + D], sc1[:, :], ada1[:, g // 2, col * D:(col + 1) * D], start=False, stop=True)
                            if g % 3 == 2:
                                last.then_inc(gate_mm, 3)
                        pe.wait_ge(skew_in, 32)
                        for n in range(8):
                            if n >= 4:
                                pe.wait_ge(raw_ev_dve if n % 2 else raw_ev_act, (n - 4) // 2 + 1)
                            nc.tensor.matmul(bank[4 + n % 4][0:B, :], sc0[:, :], sk0[:, n * 512:(n + 1) * 512], start=True, stop=False)
                            nc.tensor.matmul(bank[4 + n % 4][0:B, :], sc1[:, :], sk1[:, n * 512:(n + 1) * 512], start=False, stop=True).then_inc(raw_mm, 1)
            w_raw = [asb(f"w_raw{l}", [P, 2, SPLIT_W[l]]) for l in range(L)]
            with ExitStack() as c:
                def tsb(name, shape, dt=F32):
                    return c.enter_context(nc.sbuf_tensor(name, shape, dt))

                def tsem(name):
                    return c.enter_context(nc.semaphore(name))

                vs = tsb("vs", [R, R, D])
                inv_t = tsb("inv_t", [R, R])
                prod = tsb("prod", [R, D])
                square = tsb("square", [R, D])
                acc = tsb("acc", [R, 16])
                nrm2, dot, half_sign, signed, w, tt, coef, nrm = (acc[:, j:j + 1] for j in range(8))
                qa = tsb("qa", [R, D])
                reduced = tsem("reduced")
                row_done = tsem("row_done")
                chain = tsem("chain")
                nrm2_done = tsem("nrm2_done")
                nrm_done = tsem("nrm_done")
                back = tsem("back")
                ut_mm = tsem("ut_mm")
                STEPS = 8
                twice = tsb("twice", [P, P])
                unit_mm = tsem("unit_mm")
                unit_ev = tsem("unit_ev")
                first_ev = tsem("first_ev")
                hi_done = tsem("hi_done")
                lo_done = tsem("lo_done")
                HALF = PAIRS // 2
                TERMS = 7
                GAP_PAIRS = 7

                def halves(m, h):
                    return m[:, h * HALF:(h + 1) * HALF, :].rearrange("p q j -> p (q j)")

                units = []
                y, z = ez, ew
                for k in range(TERMS - 1, 0, -1):
                    for h in range(2):
                        units.append(((ident, ex), ey, y, z, 1 / k, h, len(units) - 1))
                    y, z = z, y
                for h in range(2):
                    units.append((None, y, None, z, 1.0, h, len(units) - 1))
                e, et, spare, spare_t = y, z, ex, ey
                for s in range(DOUBLINGS):
                    start = len(units)
                    for h in range(2):
                        before = start - 1 + h if s == 0 else start - 2 + 2 * h
                        units.append(((twice, e), et, e, spare, 1.0, h, before))
                        units.append(((twice, et), e, et, spare_t, 1.0, h, before))
                    e, et, spare, spare_t = spare, spare_t, e, et
                assert e is ez and et is ew
                parts, todo = [[] for _ in range(R + 1)], []
                for u, unit in enumerate(units):
                    todo += ([(u, None)] if unit[0] else []) + [(u, q) for q in range(HALF)]
                for k in range(1, R):
                    room = GAP_PAIRS
                    while todo and room >= (1 if todo[0][1] is not None else 2):
                        room -= 1 if todo[0][1] is not None else 2
                        parts[k].append(todo.pop(0))
                parts[R] = todo

                with nc.Block() as block:
                    @block.sync
                    def _(sp):
                        for l in range(L):
                            sp.dma_start(w_raw[l][:, 0, :], t[f"split{l}"]).then_inc(w_in[l], 16)
                            sp.dma_start(w_raw[l][:, 1, :], t[f"stack{l}"]).then_inc(w_in[l], 16)

                    @block.gpsimd
                    def _(pool):
                        for k in range(R):
                            pool.wait_ge(nrm2_done, k + 1)
                            pool.wait_ge(ones_ready, 1)
                            nc.gpsimd.tensor_tensor(nrm, nrm2, phalf[0:R, :], ALU.pow).then_inc(nrm_done, 1)
                        for l in range(L):
                            pool.wait_ge(hi_done, 2 * l + 2)
                            if l:
                                pool.wait_ge(lo_done, 3 * l)
                            nc.gpsimd.tensor_tensor(w_lo[l][:, :], w_raw[l][:, 0, :], w_hi[l][:, :], ALU.subtract).then_inc(lo_done, 1)
                            for i, r in enumerate((slice(32, 64), slice(96, 128))):
                                pool.wait_ge(lo_done, 3 * l + 1 + i)
                                nc.gpsimd.tensor_tensor(w_st[l][r, :], w_raw[l][r, 1, :], w_st[l][r, :], ALU.subtract).then_inc(lo_done, 1)
                        pool.wait_ge(lo_done, 3 * L)

                    @block.scalar
                    def _(act):
                        nc.scalar.mul(ey[:, :, :], ex[:, :, :], -1.0).then_inc(first_ev, 1)
                        nc.scalar.mul(ez[:, :, :], ex[:, :, :], 1 / TERMS).then_inc(first_ev, 1)
                        nc.scalar.mul(twice[:, :], ident[:, :], 2.0).then_inc(first_ev, 1)
                        for k in range(R + 1):
                            for u, q in parts[k]:
                                if q == HALF - 1:
                                    act.wait_ge(unit_mm, u + 1)
                                    nc.scalar.mul(halves(units[u][3], units[u][5]), bank[2 + u % 6][:, :], units[u][4]).then_inc(unit_ev, 1)
                            if k < R:
                                act.wait_ge(chain, k * STEPS + 1)
                                if k:
                                    act.wait_ge(nrm_done, k)
                                nc.scalar.activation(square[:, k:D], vs[:, k, k:D], ACT.Square, accum_out=nrm2).then_inc(nrm2_done, 1)
                        for l in range(L):
                            act.wait_ge(w_in[l], W_LOADED)
                            nc.scalar.copy(w_hi[l][:, :], w_raw[l][:, 0, :]).then_inc(hi_done, 1)
                            nc.scalar.copy(w_st[l][:, :], w_raw[l][:, 1, :]).then_inc(hi_done, 1)
                        act.wait_ge(unit_ev, len(units))

                    @block.tensor
                    def _(pe):
                        def part(u, q):
                            added, lhs, rhs, _, _, h, before = units[u]
                            dst = bank[2 + u % 6]
                            if q is None or (q == 0 and added is None):
                                pe.wait_ge(first_ev, 3)
                                if before > 0:
                                    pe.wait_ge(unit_ev, before)
                            if q is None:
                                nc.tensor.matmul(dst[:, :], added[0][:, :], halves(added[1], h), start=True, stop=False)
                                return
                            for half in range(2):
                                rows = slice(half * R, (half + 1) * R)
                                mm = nc.tensor.matmul(dst[rows, q * R:(q + 1) * R], lhs[rows, h * HALF + q, :], ident[rows, rows] if rhs is None else rhs[rows, h * HALF + q, :],
                                                      start=added is None, stop=added is None or q == HALF - 1)
                            if q == HALF - 1:
                                mm.then_inc(unit_mm, 1)

                        for k in range(R):
                            for u, q in parts[k]:
                                part(u, q)
                            pe.wait_ge(reduced, k + 1)
                            nc.tensor.matmul(bank[k % 2][0:R, k:D], ident[0:R, k:k + 1].to_broadcast([R, R]), qa[:, k:D], start=True, stop=True).then_inc(row_done, 1)
                        for u, q in parts[R]:
                            part(u, q)
                        pe.wait_ge(back, 2 * R + 3)
                        nc.tensor.transpose(bank[0][:, 0:R], qt[0:R, 0:P], ident[0:R, 0:R])
                        nc.tensor.transpose(bank[0][0:DT, R:2 * R], qt[0:R, P:D], ident[0:R, 0:R]).then_inc(ut_mm, 1)

                    @block.vector
                    def _(dve):
                        nc.vector.tensor_copy(qa[:, :], qt[0:R, :]).then_inc(reduced, 1)
                        for k in range(R):
                            done = k * STEPS
                            v = vs[:, k, k:D]
                            dve.wait_ge(row_done, k + 1)
                            nc.vector.tensor_copy(v, bank[k % 2][0:R, k:D]).then_inc(chain, 1)
                            dve.wait_ge(chain, done + 1)
                            nc.vector.tensor_tensor(prod[:, k:D], v, qa[:, k:D], ALU.mult).then_inc(chain, 1)
                            nc.vector.tensor_scalar(half_sign, vs[:, k, k:k + 1], 0.0, 0.5, ALU.is_ge, ALU.subtract).then_inc(chain, 1)
                            dve.wait_ge(chain, done + 3)
                            nc.vector.tensor_reduce(dot, prod[:, k:D], AX.X, ALU.add).then_inc(chain, 1)
                            dve.wait_ge(chain, done + 4)
                            dve.wait_ge(nrm_done, k + 1)
                            nc.vector.scalar_tensor_tensor(out=signed, in0=nrm, scalar=2.0, in1=half_sign, op0=ALU.mult, op1=ALU.mult).then_inc(chain, 1)
                            dve.wait_ge(chain, done + 5)
                            nc.vector.tensor_tensor(vs[:, k, k:k + 1], vs[:, k, k:k + 1], signed, ALU.add).then_inc(chain, 1)
                            nc.vector.scalar_tensor_tensor(out=w, in0=qa[:, k:k + 1], scalar=signed, in1=dot, op0=ALU.mult, op1=ALU.add)
                            dve.wait_ge(chain, done + 6)
                            nc.vector.tensor_tensor(tt, vs[:, k, k:k + 1], signed, ALU.mult).then_inc(chain, 1)
                            dve.wait_ge(chain, done + 7)
                            nc.vector.reciprocal(inv_t[:, k:k + 1], tt).then_inc(chain, 1)
                            dve.wait_ge(chain, done + 8)
                            nc.vector.scalar_tensor_tensor(out=coef, in0=w, scalar=-1.0, in1=inv_t[:, k:k + 1], op0=ALU.mult, op1=ALU.mult).then_inc(back, 1)
                            dve.wait_ge(back, k + 1)
                            nc.vector.scalar_tensor_tensor(out=qa[:, k:D], in0=v, scalar=coef, in1=qa[:, k:D], op0=ALU.mult, op1=ALU.add).then_inc(reduced, 1)
                            dve.wait_ge(reduced, k + 2)
                        nc.vector.memset(qt[:, :], 0.0).then_inc(back, 1)
                        dve.wait_ge(back, R + 1)
                        nc.vector.tensor_copy(qt[0:R, 0:R], ident[0:R, 0:R]).then_inc(back, 1)
                        for i in range(R):
                            k = R - 1 - i
                            dve.wait_ge(back, R + 2 + i)
                            nc.vector.tensor_tensor(prod[:, k:D], vs[:, k, k:D], qt[0:R, k:D], ALU.mult).then_inc(chain, 1)
                            dve.wait_ge(chain, i * 3 + (R * STEPS + 1))
                            nc.vector.tensor_reduce(dot, prod[:, k:D], AX.X, ALU.add).then_inc(chain, 1)
                            dve.wait_ge(chain, i * 3 + (R * STEPS + 2))
                            nc.vector.scalar_tensor_tensor(out=coef, in0=dot, scalar=-1.0, in1=inv_t[:, k:k + 1], op0=ALU.mult, op1=ALU.mult).then_inc(chain, 1)
                            dve.wait_ge(chain, i * 3 + (R * STEPS + 3))
                            nc.vector.scalar_tensor_tensor(out=qt[0:R, k:D], in0=vs[:, k, k:D], scalar=coef, in1=qt[0:R, k:D], op0=ALU.mult, op1=ALU.add).then_inc(back, 1)
                        dve.wait_ge(back, 2 * R + 2)
                        nc.vector.tensor_copy(qt[R:P, :], qt[0:R, :]).then_inc(back, 1)
                        dve.wait_ge(ut_mm, 1)
                        nc.vector.tensor_copy(u0[:, :], bank[0][:, 0:R]).then_inc(ut_mm, 1)
                        nc.vector.tensor_copy(u1[:, :], bank[0][0:DT, R:2 * R]).then_inc(ut_mm, 1)
                        dve.wait_ge(ut_mm, 3)
            with ExitStack() as c:
                def tsb(name, shape, dt=F32):
                    return c.enter_context(nc.sbuf_tensor(name, shape, dt))

                def tsem(name):
                    return c.enter_context(nc.semaphore(name))

                xc = tsb("xc", [P, 2, 2, D])
                yc = tsb("yc", [P, 2, R])
                xt0 = tsb("xt0", [P, 2, 2 * T])
                xt1 = tsb("xt1", [DT, 2, 2 * T])
                zt = tsb("zt", [P, 2, T])
                bm = tsb("bm", [P, 2, D])
                staged = tsem("staged")
                xt_mm = tsem("xt_mm")
                xt_done = tsem("xt_done")
                z_mm = tsem("z_mm")
                z_done = tsem("z_done")
                rot_mm = tsem("rot_mm")
                x_done = tsem("x_done")
                st_done = tsem("st_done")
                var_done = tsem("var_done")
                rs_done = tsem("rs_done")

                xt_at = [bank[4 * u][:, :].rearrange("p (k c) -> p k c", k=2) for u in range(2)]
                z_at = [bank[4 * u + 1][:, 0:T] for u in range(2)]
                bm_at = [bank[4 * u + 1][:, T:T + D] for u in range(2)]
                rot_at = [[bank[4 * u + 2 + s][:, 0:D] for s in range(2)] for u in range(2)]

                with nc.Block() as block:
                    @block.gpsimd
                    def _(pool):
                        def stage(q, u):
                            nc.gpsimd.tensor_copy(xc[:, u, :, :], x_all[:, bass.ds(q * 2, 2), :]).then_inc(staged, 1)
                            nc.gpsimd.tensor_copy(yc[:, u, :], ew[:, q, :]).then_inc(staged, 1)

                        stage(0, 0)
                        stage(1, 1)
                        with nc.gpsimd.Fori(1, PAIRS // 2) as i:
                            for u in range(2):
                                pool.wait_ge(ones_ready, 1)
                                pool.wait_ge(x_done, i * 2 - 1 + u)
                                stage(i * 2 + u, u)

                    @block.tensor
                    def _(pe):
                        with nc.tensor.Fori(0, PAIRS // 2) as i:
                            for u in range(2):
                                n = i * 2 + u
                                pe.wait_ge(staged, n * 2 + 2)
                                for s in range(2):
                                    nc.tensor.transpose(xt_at[u][:, 0, s * T:(s + 1) * T], xc[:, u, s, 0:P], ident[:, :])
                                for s in range(2):
                                    last = nc.tensor.transpose(xt_at[u][0:DT, 1, s * T:(s + 1) * T], xc[:, u, s, P:D], ident[:, :])
                                last.then_inc(xt_mm, 1)
                                for s in range(2):
                                    h = slice(s * R, (s + 1) * R)
                                    nc.tensor.matmul(bm_at[u][h, :], yc[h, u, :], qt[h, :], start=True, stop=True)
                            for u in range(2):
                                n = i * 2 + u
                                pe.wait_ge(ones_ready, 1)
                                pe.wait_ge(xt_done, n + 1)
                                for s in range(2):
                                    h = slice(s * R, (s + 1) * R)
                                    z = z_at[u][h, :]
                                    nc.tensor.matmul(z, u0[:, :], xt0[:, u, s * T:(s + 1) * T], start=True, stop=False)
                                    last = nc.tensor.matmul(z, u1[:, :], xt1[:, u, s * T:(s + 1) * T], start=False, stop=True)
                                last.then_inc(z_mm, 1)
                            for u in range(2):
                                n = i * 2 + u
                                pe.wait_ge(z_done, n + 1)
                                for s in range(2):
                                    h = slice(s * R, (s + 1) * R)
                                    last = nc.tensor.matmul(rot_at[u][s], zt[h, u, :], bm[h, u, :], start=True, stop=True)
                                last.then_inc(rot_mm, 1)

                    @block.scalar
                    def _(act):
                        with nc.scalar.Fori(0, PAIRS // 2) as i:
                            for u in range(2):
                                n = i * 2 + u
                                act.wait_ge(z_mm, n + 1)
                                nc.scalar.copy(zt[:, u, :], z_at[u])
                                nc.scalar.copy(bm[:, u, :], bm_at[u]).then_inc(z_done, 1)

                    @block.vector
                    def _(dve):
                        with nc.vector.Fori(0, PAIRS // 2) as i:
                            for u in range(2):
                                n = i * 2 + u
                                dve.wait_ge(xt_mm, n + 1)
                                nc.vector.tensor_copy(xt0[:, u, :], xt_at[u][:, 0, :])
                                nc.vector.tensor_copy(xt1[:, u, :], xt_at[u][0:DT, 1, :]).then_inc(xt_done, 1)
                            for u in range(2):
                                n = i * 2 + u
                                dve.wait_ge(rot_mm, n + 1)
                                for s in range(2):
                                    seq = n * 2 + s
                                    last = nc.vector.tensor_tensor(x_all[:, seq, :], xc[:, u, s, :], rot_at[u][s], ALU.add)
                                last.then_inc(x_done, 1)
                                dve.wait_ge(ones_ready, 1)
                                dve.wait_ge(x_done, n + 1)
                                nc.vector.bn_stats(stats[:, 0, :], x_all[:, n * 2, :])
                                nc.vector.bn_stats(stats[:, 1, :], x_all[:, n * 2 + 1, :]).then_inc(st_done, 1)
                                dve.wait_ge(ones_ready, 1)
                                dve.wait_ge(st_done, n + 1)
                                nc.vector.bn_aggr(aggr[:, 0, :], stats[:, 0, :])
                                nc.vector.bn_aggr(aggr[:, 1, :], stats[:, 1, :]).then_inc(var_done, 1)
                                dve.wait_ge(var_done, n + 1)
                                nc.vector.tensor_copy(mean_all[:, bass.ds(n * 2, 2)], aggr[:, :, 0])
                                nc.vector.tensor_scalar(var_all[:, bass.ds(n * 2, 2)], aggr[:, :, 1], 1e-6, None, ALU.add).then_inc(rs_done, 1)
                        dve.wait_ge(rs_done, PAIRS)
        gate_all = sb("gate_all", [P, 2, B, D])
        with nc.Block() as block:
            @block.sync
            def _(sp):
                load_gates(sp, 0)
                load_gates(sp, 1)

            @block.gpsimd
            def _(pool):
                nc.gpsimd.tensor_tensor(rstd_all[:, :], var_all[:, :], mhalf[:, :].to_broadcast([P, B]), ALU.pow).then_inc(ones_ready, 1)
                pool.wait_ge(ones_ready, 6)
        def variance(dve, rms, both, b, done, ms, count):
            if rms:
                nc.vector.scalar_tensor_tensor(out=both[:, 1:2], in0=both[:, 0:1], scalar=both[:, 0:1], in1=both[:, 1:2], op0=ALU.mult, op1=ALU.add).then_inc(ms, 1)
                dve.wait_ge(ms, count + 1)
                nc.vector.tensor_scalar(var_all[:, bass.ds(b, 1)], both[:, 1:2], 1e-24 / D, None, ALU.max).then_inc(done, 1)
            else:
                nc.vector.tensor_copy(mean_all[:, bass.ds(b, 1)], both[:, 0:1])
                nc.vector.tensor_scalar(var_all[:, bass.ds(b, 1)], both[:, 1:2], 1e-6, None, ALU.add).then_inc(done, 1)

        with ExitStack() as c:
            def tsb(name, shape, dt=F32):
                return c.enter_context(nc.sbuf_tensor(name, shape, dt))

            turned = nc.dram_tensor("turned", [B, H, T, DH], F32, kind="Internal").ap()
            hn = tsb("h_hn", [P, 2, D])
            ht0 = tsb("h_ht0", [P, 2, T])
            ht1 = tsb("h_ht1", [DT + 1, 2, T])
            qkv = tsb("h_qkv", [P, 2, 3 * D])
            qk_prod = tsb("h_qk_prod", [P, H, H, DH])
            score = tsb("h_score", [P, 2, H, H])
            top = tsb("h_top", [P, H])
            prob = tsb("h_prob", [P, 2, H, H])
            rsum = tsb("h_rsum", [P, 2, H])
            pv_prod = tsb("h_pv_prod", [P, 2, H, H, DH])
            out_h = tsb("h_out", [P, 2, D])
            y = tsb("h_y", [P, 2, D])
            at0 = tsb("h_at0", [P, 2, T])
            at1 = tsb("h_at1", [DT + 1, 2, T])
            upd = tsb("h_upd", [P, 2, D])
            names = ("set hn_done ht_mm ht_done qkv_mm qkv_done qk_done score_done max_done sub_done exp_done sum_done rsum_done pv_done "
                     "pvsum_mm out_done turn_out turn_in y_mm y_done proj_mm upd_done x_new stat_done aggr_done var_new rstd_new").split()
            S = {k: sem("h_" + k) for k in names}
            b_tp, b_mm, b_sum, b_ty, b_pj = bank[0:5]

            def drive(eng, step):
                step(-1, 1, middle=False, sums=False, last=False)
                step(0, 0, sums=False, last=False)
                step(1, 1, last=False)
                step(2, 0)
                step(3, 1)
                with eng.Fori(0, (B - 6) // 2) as i:
                    step(i * 2 + 4, 0)
                    step(i * 2 + 5, 1)
                step(B - 2, 0)
                step(B - 1, 1, front=False)
                step(B, 0, front=False, middle=False)
                step(B + 1, 1, front=False, middle=False, sums=False)

            with nc.Block() as block:
                @block.tensor
                def _(pe):
                    def step(b, u, front=True, middle=True, sums=True, last=True):
                        w = 1 - u
                        if front:
                            pe.wait_ge(S["hn_done"], b + 2)
                            nc.tensor.transpose(b_tp[:, 0:T], hn[:, w, 0:P], ident[:, :])
                            nc.tensor.transpose(b_tp[0:DT, T:2 * T], hn[:, w, P:D], ident[:, :]).then_inc(S["ht_mm"], 1)
                        if sums:
                            pe.wait_ge(S["pv_done"], b)
                            if last:
                                pe.wait_ge(S["out_done"], b - 1)
                            for k in range(H):
                                mm = nc.tensor.matmul(b_sum[:, 0:D], ident[:, :], pv_prod[:, w, k, :, :].rearrange("p h d -> p (h d)"), start=(k == 0), stop=(k == H - 1))
                            mm.then_inc(S["pvsum_mm"], 1)
                        if last:
                            pe.wait_ge(S["turn_in"], (b - 1) * 16)
                            nc.tensor.transpose(b_ty[:, 0:T], y[:, u, 0:P], ident[:, :])
                            nc.tensor.transpose(b_ty[0:DT, T:2 * T], y[:, u, P:D], ident[:, :]).then_inc(S["y_mm"], 1)
                        if last:
                            pe.wait_ge(S["y_done"], b * 2 - 2)
                            if not isinstance(b, int) or b > 2:
                                pe.wait_ge(S["upd_done"], b - 2)
                            nc.tensor.matmul(b_pj[:, 0:D], at0[:, u, :], w_main[0][:, 3 * D:4 * D], start=True, stop=False)
                            nc.tensor.matmul(b_pj[:, 0:D], at1[:, u, :], w_tail[0][:, 3 * D:4 * D], start=False, stop=True).then_inc(S["proj_mm"], 1)
                        if front:
                            pe.wait_ge(S["set"], 2)
                            pe.wait_ge(S["ht_done"], b * 2 + 4)
                            if middle:
                                pe.wait_ge(S["qkv_done"], b + 1)
                            nc.tensor.matmul(b_mm[:, 0:3 * D], ht0[:, w, :], w_main[0][:, 0:3 * D], start=True, stop=False)
                            nc.tensor.matmul(b_mm[:, 0:3 * D], ht1[:, w, :], w_tail[0][:, 0:3 * D], start=False, stop=True).then_inc(S["qkv_mm"], 1)

                    pe.wait_ge(w_in[0], W_LOADED)
                    drive(nc.tensor, step)

                @block.scalar
                def _(act):
                    def step(b, u, front=True, middle=True, sums=True, last=True):
                        w = 1 - u
                        if last:
                            act.wait_ge(S["y_mm"], b - 1)
                            nc.scalar.copy(at0[:, u, :], b_ty[:, 0:T]).then_inc(S["y_done"], 1)
                            nc.scalar.copy(at1[0:DT, u, :], b_ty[0:DT, T:2 * T]).then_inc(S["y_done"], 1)
                        if middle:
                            act.wait_ge(S["sub_done"], b + 1)
                            nc.scalar.activation(prob[:, u, :, :], score[:, u, :, :], ACT.Exp, scale=SM).then_inc(S["exp_done"], 1)
                        if front:
                            if sums:
                                act.wait_ge(S["pv_done"], b)
                            act.wait_ge(S["qkv_mm"], b + 2)
                            nc.scalar.copy(qkv[:, w, :], b_mm[:, 0:3 * D]).then_inc(S["qkv_done"], 1)

                    drive(nc.scalar, step)

                @block.gpsimd
                def _(pool):
                    def step(b, u, front=True, middle=True, sums=True, last=True):
                        w = 1 - u
                        if middle:
                            pool.wait_ge(S["exp_done"], b + 1)
                            if sums and last:
                                pool.wait_ge(S["pvsum_mm"], b - 1)
                            nc.gpsimd.tensor_tensor(pv_prod[:, u, :, :, :], prob[:, u, :, :].rearrange("p h k -> p k h").unsqueeze(3).to_broadcast([P, H, H, DH]),
                                                    qkv[:, u, 2 * D:3 * D].rearrange("p (k d) -> p k d", d=DH).unsqueeze(2).to_broadcast([P, H, H, DH]), ALU.mult).then_inc(S["pv_done"], 1)
                        if last:
                            pool.wait_ge(S["var_new"], b - 1)
                            nc.gpsimd.tensor_tensor(rstd_all[:, bass.ds(b - 2, 1)], var_all[:, bass.ds(b - 2, 1)], mhalf[:, :], ALU.pow).then_inc(S["rstd_new"], 1)

                    drive(nc.gpsimd, step)
                    pool.wait_ge(S["rstd_new"], B)

                @block.sync
                def _(sp):
                    def step(b, u, front=True, middle=True, sums=True, last=True):
                        if not sums:
                            return
                        w = 1 - u
                        sp.wait_ge(S["out_done"], b)
                        sp.dma_start(turned[b - 1].rearrange("h t d -> t h d"), out_h[:, w, :].rearrange("p (h d) -> p h d", d=DH)).then_inc(S["turn_out"], 16)
                        sp.wait_ge(S["turn_out"], b * 16)
                        sp.dma_start(y[:, w, :], turned[b - 1].rearrange("h t d -> (h t d)").rearrange("(p q) -> p q", q=D)).then_inc(S["turn_in"], 16)

                    drive(nc.sync, step)

                @block.vector
                def _(dve):
                    def step(b, u, front=True, middle=True, sums=True, last=True):
                        w = 1 - u
                        nb = b + 1
                        if front:
                            nc.vector.tensor_scalar(hn[:, w, :], x_all[:, nb, :], mean_all[:, bass.ds(nb, 1)], rstd_all[:, bass.ds(nb, 1)], ALU.subtract, ALU.mult).then_inc(S["hn_done"], 1)
                        if middle:
                            dve.wait_ge(S["qkv_done"], b + 1)
                            heads = qkv[:, u, :].rearrange("p (s h d) -> p s h d", s=3, d=DH)
                            nc.vector.tensor_tensor(qk_prod[:, :, :, :], heads[:, 0].unsqueeze(2).to_broadcast([P, H, H, DH]),
                                                    heads[:, 1].unsqueeze(1).to_broadcast([P, H, H, DH]), ALU.mult).then_inc(S["qk_done"], 1)
                        if front:
                            dve.wait_ge(S["ht_mm"], b + 2)
                            nc.vector.tensor_scalar(ht0[:, w, :], b_tp[:, 0:T], mod[:, 0, 1, bass.ds(nb, 1)], mod[:, 0, 0, bass.ds(nb, 1)], ALU.mult, ALU.add).then_inc(S["ht_done"], 1)
                            nc.vector.tensor_scalar(ht1[0:DT, w, :], b_tp[0:DT, T:2 * T], modt[0:DT, 0, 1, bass.ds(nb, 1)], modt[0:DT, 0, 0, bass.ds(nb, 1)], ALU.mult, ALU.add).then_inc(S["ht_done"], 1)
                        if middle:
                            dve.wait_ge(S["qk_done"], b + 1)
                            nc.vector.tensor_reduce(score[:, u, :, :], qk_prod[:, :, :, :], AX.X, ALU.add).then_inc(S["score_done"], 1)
                        if sums:
                            dve.wait_ge(S["rsum_done"], b)
                            dve.wait_ge(S["pvsum_mm"], b)
                            if last:
                                dve.wait_ge(S["turn_out"], (b - 1) * 16)
                            nc.vector.tensor_tensor(out_h[:, w, :].rearrange("p (h d) -> p h d", d=DH), b_sum[:, 0:D].rearrange("p (h d) -> p h d", d=DH),
                                                    rsum[:, w, :].unsqueeze(2).to_broadcast([P, H, DH]), ALU.mult).then_inc(S["out_done"], 1)
                        if middle:
                            dve.wait_ge(S["score_done"], b + 1)
                            nc.vector.tensor_reduce(top[:, :], score[:, u, :, :], AX.X, ALU.max).then_inc(S["max_done"], 1)
                            dve.wait_ge(S["max_done"], b + 1)
                            nc.vector.tensor_tensor(score[:, u, :, :], score[:, u, :, :], top[:, :].unsqueeze(2).to_broadcast([P, H, H]), ALU.subtract).then_inc(S["sub_done"], 1)
                        if last:
                            pb = b - 2
                            dve.wait_ge(S["proj_mm"], b - 1)
                            nc.vector.tensor_tensor(upd[:, u, :], b_pj[:, 0:D], gate_all[:, 0, pb, :], ALU.mult).then_inc(S["upd_done"], 1)
                            dve.wait_ge(S["upd_done"], b - 1)
                            nc.vector.tensor_tensor(x_all[:, pb, :], x_all[:, pb, :], upd[:, u, :], ALU.add).then_inc(S["x_new"], 1)
                            dve.wait_ge(ones_ready, 1)
                            dve.wait_ge(S["x_new"], b - 1)
                            nc.vector.bn_stats(stats[:, u, :], x_all[:, pb, :]).then_inc(S["stat_done"], 1)
                            dve.wait_ge(ones_ready, 1)
                            dve.wait_ge(S["stat_done"], b - 1)
                            nc.vector.bn_aggr(aggr[:, u, :], stats[:, u, :]).then_inc(S["aggr_done"], 1)
                            dve.wait_ge(S["aggr_done"], b - 1)
                            variance(dve, False, aggr[:, u], pb, S["var_new"], None, b - 2)
                        if middle:
                            dve.wait_ge(S["exp_done"], b + 1)
                            nc.vector.tensor_reduce(rsum[:, u, :], prob[:, u, :, :], AX.X, ALU.add).then_inc(S["sum_done"], 1)
                            dve.wait_ge(S["sum_done"], b + 1)
                            nc.vector.reciprocal(rsum[:, u, :], rsum[:, u, :]).then_inc(S["rsum_done"], 1)

                    nc.vector.memset(ht1[:, :, :], 1.0).then_inc(S["set"], 1)
                    nc.vector.memset(at1[:, :, :], 1.0).then_inc(S["set"], 1)
                    dve.wait_ge(S["set"], 2)
                    drive(nc.vector, step)
                    dve.wait_ge(S["var_new"], B)
                    dve.wait_ge(S["rsum_done"], B)
        names = ("hn_done ht_mm ht_done qkv_mm qkv_done square_done ssum_done rq_done qkn_done high_done va_done rest_done "
                 "midp_done low_done hi_done lo_done qs_mm qs_done ks_mm ks_done s_mm max_done neg_done q2_mm q2_done st_mm exp_done "
                 "pv_mm ot_done back_mm rsum_done at_done at_mm at_ev proj_mm upd_done x_new stat_done aggr_done var_new rstd_new ms_done set_done").split()
        S = {k: sem("a_" + k) for k in names}

        bank_hs = [bank[0:2], bank[2:4]]
        b_t, b_mm, b_tp, b_ov = bank[4], bank[5], bank[6], bank[7]
        tp16 = b_tp[:, :].bitcast(BF16).rearrange("p (c t) -> p c t", t=T)
        tk16 = b_ov[:, :].bitcast(BF16).rearrange("p (c t) -> p c t", t=T)
        t16 = b_t[:, :].bitcast(BF16).rearrange("p (c t) -> p c t", t=T)

        def attention(l):
            with ExitStack() as c:
                def tsb(name, shape, dt=F32):
                    return c.enter_context(nc.sbuf_tensor(name, shape, dt))

                hn = tsb(f"a{l}_hn", [P, 2, P])
                hn_st = tsb(f"a{l}_hn_st", [P, 2, 4, 32])
                ht = tsb(f"a{l}_ht", [P, 2, T])
                hi = tsb(f"a{l}_hi", [P, 2, T], F32R)
                lo = tsb(f"a{l}_lo", [P, T], F32R)
                qkvs = tsb(f"a{l}_qkvs", [P, 2, 3 * D])
                sq = tsb(f"a{l}_sq", [P, 2 * D])
                ssum = tsb(f"a{l}_ssum", [P, 2 * H])
                rq = tsb(f"a{l}_rq", [P, 2 * H])
                gq = tsb(f"a{l}_gq", [P, 2 * H])
                qk = tsb(f"a{l}_qk", [P, 2 * D])
                rest = tsb(f"a{l}_rest", [P, 2 * D])
                stack = tsb(f"a{l}_stack", [P, 3, H, SLOT], BF16)
                qs = tsb(f"a{l}_qs", [P, 2, H // 2, T], BF16)
                ks = tsb(f"a{l}_ks", [P, 2, H // 2, T], BF16)
                va = tsb(f"a{l}_va", [P, 2, H, 32])
                rmax = tsb(f"a{l}_rmax", [P, H])
                pt = tsb(f"a{l}_pt", [P, 2, H, T])
                ot = tsb(f"a{l}_ot", [P, 4, T])
                rsum = tsb(f"a{l}_rsum", [P, H])
                at = tsb(f"a{l}_at", [P, 2, D])
                at0 = tsb(f"a{l}_at0", [P, T])
                at1 = tsb(f"a{l}_at1", [DT + 1, T])
                upd = tsb(f"a{l}_upd", [P, 2, D])

                with nc.Block() as block:
                    @block.vector
                    def _(dve):
                        nc.vector.memset(hn_st[:, :, :, :], 0.0).then_inc(S["set_done"], 1)
                        nc.vector.memset(at1[:, :], 1.0).then_inc(S["set_done"], 1)
                        nc.vector.memset(va[:, :, :, :], 0.0).then_inc(S["set_done"], 1)
                        nc.vector.memset(stack[:, :, :, :], 0.0).then_inc(S["set_done"], 1)
                        for s in range(2):
                            nc.vector.tensor_scalar(gq[:, s * H:(s + 1) * H], gain[:, 2 + s:3 + s].to_broadcast([P, H]), DH ** 0.5, None, ALU.mult).then_inc(S["set_done"], 1)
                        dve.wait_ge(S["set_done"], 8 * (l - 1) + 6)
                        nc.vector.memset(va[:, :, :, DH:DH + 1], 1.0).then_inc(S["set_done"], 1)
                        nc.vector.memset(stack[:, 2, :, PIECES * DH:PIECES * DH + 2], 1.0).then_inc(S["set_done"], 1)
                        dve.wait_ge(S["set_done"], 8 * l)

                base = (l - 1) * B
                wq = slice(0, 3 * D)
                wp0, wp1 = w_main[l][:, 0:D], w_tail[l][:, 0:D]
                rms = l == 1

                def drive(eng, step):
                    step(-3, 1, A=False, B_=False, C=False, D_=False, F=False)
                    step(-2, 0, B_=False, C=False, D_=False, F=False)
                    step(-1, 1, C=False, D_=False, F=False)
                    step(0, 0, D_=False, F=False)
                    step(1, 1, F=False)
                    step(2, 0)
                    step(3, 1)
                    with eng.Fori(0, (B - 8) // 2) as i:
                        step(i * 2 + 4, 0)
                        step(i * 2 + 5, 1)
                    step(B - 4, 0)
                    step(B - 3, 1, N=False)
                    step(B - 2, 0, A=False, N=False)
                    step(B - 1, 1, A=False, B_=False, N=False)
                    step(B, 0, A=False, B_=False, C=False, N=False)
                    step(B + 1, 1, A=False, B_=False, C=False, D_=False, N=False)

                with nc.Block() as block:
                    @block.sync
                    def _(sp):
                        load_gates(sp, 2 * l + 1)

                    @block.tensor
                    def _(pe):
                        def step(b, u, A=True, B_=True, C=True, D_=True, F=True, N=True):
                            n = b + base
                            w = 1 - u
                            if C:
                                pe.wait_ge(S["qs_done"], n + 1)
                                pe.wait_ge(S["ks_done"], n + 1)
                                for half in range(2):
                                    if D_:
                                        pe.wait_ge(S["exp_done"], n * 4 - 2 + 2 * half)
                                    for h in range(8 * half, 8 * half + 8):
                                        r = slice(SLOT * (h % 2), SLOT * (h % 2) + PIECES * DH)
                                        mm = nc.tensor.matmul(bank_hs[half][h % 2][:, (h % 8) // 2 * T:((h % 8) // 2 + 1) * T], qs[r, u, h // 2, :], ks[r, u, h // 2, :],
                                                              start=True, stop=True)
                                    mm.then_inc(S["s_mm"], 1)
                            if F:
                                pe.wait_ge(S["at_done"], n - 1)
                                if B_:
                                    pe.wait_ge(S["qkv_done"], n + 2)
                                if not (isinstance(b, int) and b < 3):
                                    pe.wait_ge(S["upd_done"], n - 2)
                                nc.tensor.transpose(b_mm[:, 0:T], at[:, u, 0:P], ident[:, :])
                                nc.tensor.transpose(b_mm[0:DT, T:2 * T], at[:, u, P:D], ident[:, :]).then_inc(S["at_mm"], 1)
                            if A:
                                pe.wait_ge(S["hn_done"], 2 * n + 6)
                                if D_:
                                    pe.wait_ge(S["q2_done"], n)
                                nc.tensor.transpose(b_t[:, 0:T], hn[:, u, 0:P], ident[:, :])
                                nc.tensor.transpose(b_t[:, T:2 * T], hn_st[:, u, :, :].rearrange("p c f -> p (c f)"), ident[:, :]).then_inc(S["ht_mm"], 1)
                            if D_:
                                pe.wait_ge(S["va_done"], n)
                                if F:
                                    pe.wait_ge(S["at_done"], n - 1)
                                for h in range(H):
                                    if h % 8 == 0:
                                        pe.wait_ge(S["exp_done"], n * 4 - 2 + h // 4)
                                    r = 32 * (h % 4)
                                    mm = nc.tensor.matmul(b_ov[r:r + 32, h // 4 * T:(h // 4 + 1) * T], va[:, w, h, :], pt[:, w, h, :], start=True, stop=True)
                                mm.then_inc(S["pv_mm"], 1)
                            if A:
                                pe.wait_ge(S["lo_done"], 2 * n + 6)
                                if F:
                                    pe.wait_ge(S["at_ev"], 2 * n - 2)
                                elif B_:
                                    pe.wait_ge(S["qkv_done"], n + 2)
                                nc.tensor.matmul(b_mm[:, 0:3 * D], hi[:, 0, :], w_hi[l][:, wq], start=True, stop=False)
                                nc.tensor.matmul(b_mm[:, 0:3 * D], hi[:, 0, :], w_lo[l][:, wq], start=False, stop=False)
                                nc.tensor.matmul(b_mm[:, 0:3 * D], lo[:, :], w_hi[l][:, wq], start=False, stop=False)
                                nc.tensor.matmul(b_mm[:, 0:3 * D], hi[:, 1, :], w_st[l][:, wq], start=False, stop=True).then_inc(S["qkv_mm"], 1)
                            if C:
                                pe.wait_ge(S["neg_done"], 2 * n + 2)
                                if A:
                                    pe.wait_ge(S["ht_done"], 2 * n + 6)
                                elif D_:
                                    pe.wait_ge(S["q2_done"], n)
                                for c in range(8):
                                    mm = nc.tensor.transpose(t16[:, c, :], stack[:, u, 2 * c:2 * c + 2, :].rearrange("p h s -> p (h s)"), identb[:, :])
                                mm.then_inc(S["q2_mm"], 1)
                            if D_:
                                pe.wait_ge(S["ot_done"], n)
                                for g in range(4):
                                    mm = nc.tensor.transpose(b_ov[:, g * T:(g + 1) * T], ot[:, g, :], ident[:, :])
                                mm.then_inc(S["back_mm"], 1)
                            if B_:
                                pe.wait_ge(S["low_done"], 2 * n + 4)
                                for c in range(8):
                                    mm = nc.tensor.transpose(tp16[:, c, :], stack[:, w, 2 * c:2 * c + 2, :].rearrange("p h s -> p (h s)"), identb[:, :])
                                mm.then_inc(S["qs_mm"], 1)
                            if C:
                                pe.wait_ge(S["q2_done"], n + 1)
                                for half in range(2):
                                    pe.wait_ge(S["max_done"], 2 * n + 1 + half)
                                    for h in range(8 * half, 8 * half + 8):
                                        r = slice(SLOT * (h % 2), SLOT * (h % 2) + PIECES * DH + 2)
                                        mm = nc.tensor.matmul(bank_hs[half][h % 2][:, (h % 8) // 2 * T:((h % 8) // 2 + 1) * T], ks[r, u, h // 2, :], qs[r, u, h // 2, :],
                                                              start=True, stop=True)
                                    mm.then_inc(S["st_mm"], 1)
                            if B_:
                                if D_:
                                    pe.wait_ge(S["at_done"], n)
                                for c in range(8):
                                    mm = nc.tensor.transpose(tk16[:, c, :], stack[:, 2, 2 * c:2 * c + 2, :].rearrange("p h s -> p (h s)"), identb[:, :])
                                mm.then_inc(S["ks_mm"], 1)
                            if F:
                                pe.wait_ge(S["at_ev"], 2 * n - 2)
                                if A:
                                    pe.wait_ge(S["qkv_done"], n + 3)
                                else:
                                    pe.wait_ge(S["upd_done"], n - 2)
                                nc.tensor.matmul(b_mm[:, 0:D], at0[:, :], wp0, start=True, stop=False)
                                nc.tensor.matmul(b_mm[:, 0:D], at1[:, :], wp1, start=False, stop=True).then_inc(S["proj_mm"], 1)

                        drive(nc.tensor, step)

                    @block.scalar
                    def _(act):
                        def step(b, u, A=True, B_=True, C=True, D_=True, F=True, N=True):
                            n = b + base
                            w = 1 - u
                            if F:
                                act.wait_ge(S["at_mm"], n - 1)
                                nc.scalar.copy(at0[:, :], b_mm[:, 0:T]).then_inc(S["at_ev"], 1)
                                nc.scalar.copy(at1[0:DT, :], b_mm[0:DT, T:2 * T]).then_inc(S["at_ev"], 1)
                            if A:
                                act.wait_ge(S["ht_done"], 2 * n + 6)
                                nc.scalar.copy(hi[:, :, :], ht[:, :, :]).then_inc(S["hi_done"], 1)
                            if B_:
                                act.wait_ge(S["qkv_done"], n + 2)
                                src = qkvs[:, w, 0:2 * D]
                                if rms:
                                    act.wait_ge(S["qkn_done"], n + 2)
                                    src = qk[:, :]
                                src = src.rearrange("p (s h d) -> p s h d", s=2, d=DH)
                                for s in range(2):
                                    dst = stack[:, (w, 2)[s], :, 0:PIECES * DH].rearrange("p h (c d) -> p h c d", d=DH)
                                    dst = dst[:, :, 1::2, :] if s == 0 else dst[:, :, 0:3, :]
                                    nc.scalar.copy(dst, src[:, s].unsqueeze(2).to_broadcast([P, H, 3, DH])).then_inc(S["high_done"], 1)
                            if C:
                                if not (isinstance(b, int) and b < 2):
                                    act.wait_ge(S["pv_mm"], n - 1)
                                act.wait_ge(S["qkv_done"], n + 1)
                                nc.scalar.copy(va[:, u, :, 0:DH], qkvs[:, u, 2 * D:3 * D].rearrange("p (h d) -> p h d", d=DH)).then_inc(S["va_done"], 1)
                            if D_:
                                act.wait_ge(S["pv_mm"], n)
                                nc.scalar.copy(ot[:, :, :].rearrange("p g t -> p (g t)"), b_ov[:, :]).then_inc(S["ot_done"], 1)
                            if B_:
                                act.wait_ge(S["rest_done"], n + 2)
                                less = rest[:, :].rearrange("p (s h d) -> p s h d", s=2, d=DH)
                                for s in range(2):
                                    dst = stack[:, (w, 2)[s], :, 0:PIECES * DH].rearrange("p h (c d) -> p h c d", d=DH)
                                    dst = dst[:, :, 2::2, :] if s == 0 else dst[:, :, 3:5, :]
                                    nc.scalar.copy(dst, less[:, s].unsqueeze(2).to_broadcast([P, H, 2, DH])).then_inc(S["midp_done"], 1)
                            if A:
                                act.wait_ge(S["qkv_mm"], n + 3)
                                if C:
                                    act.wait_ge(S["va_done"], n + 1)
                                nc.scalar.copy(qkvs[:, u, :], b_mm[:, 0:3 * D]).then_inc(S["qkv_done"], 1)
                                if rms:
                                    act.wait_ge(S["qkv_done"], n + 3)
                                    nc.scalar.activation(sq[:, :], qkvs[:, u, 0:2 * D], ACT.Square).then_inc(S["square_done"], 1)
                            if C:
                                for c in range(2):
                                    act.wait_ge(S["st_mm"], 2 * n + 1 + c // 2)
                                    nc.scalar.activation(pt[:, u, 8 * (c // 2) + c % 2:8 * (c // 2) + 8:2, :], bank[c][:, :].rearrange("p (h t) -> p h t", t=T), ACT.Exp, scale=SM).then_inc(S["exp_done"], 1)
                            if B_:
                                act.wait_ge(S["ks_mm"], n + 2)
                                nc.scalar.copy(ks[:, w, :, :], tk16).then_inc(S["ks_done"], 1)
                            if C:
                                for c in range(2, 4):
                                    act.wait_ge(S["st_mm"], 2 * n + 1 + c // 2)
                                    nc.scalar.activation(pt[:, u, 8 * (c // 2) + c % 2:8 * (c // 2) + 8:2, :], bank[c][:, :].rearrange("p (h t) -> p h t", t=T), ACT.Exp, scale=SM).then_inc(S["exp_done"], 1)

                        drive(nc.scalar, step)

                    @block.gpsimd
                    def _(pool):
                        def step(b, u, A=True, B_=True, C=True, D_=True, F=True, N=True):
                            n = b + base
                            w = 1 - u
                            if A:
                                pool.wait_ge(S["hi_done"], n + 3)
                                nc.gpsimd.tensor_tensor(lo[:, :], ht[:, 0, :], hi[:, 0, :], ALU.subtract).then_inc(S["lo_done"], 1)
                                pool.wait_ge(S["lo_done"], 2 * n + 5)
                                nc.gpsimd.tensor_tensor(hi[SLOT:P, 1, :], ht[SLOT:P, 1, :], hi[SLOT:P, 1, :], ALU.subtract).then_inc(S["lo_done"], 1)
                                pool.wait_ge(S["lo_done"], 2 * n + 6)
                            if B_:
                                pieces = stack[:, w:3:2 - w, :, 0:PIECES * DH].rearrange("p s h (c d) -> p s h c d", d=DH)
                                less = rest[:, :].rearrange("p (s h d) -> p s h d", s=2, d=DH)
                                pool.wait_ge(S["midp_done"], 2 * n + 4)
                                for s in range(2):
                                    nc.gpsimd.tensor_tensor(pieces[:, s, :, 5 * s, :], less[:, s], pieces[:, s, :, 4, :], ALU.subtract).then_inc(S["low_done"], 1)
                            if A and rms:
                                pool.wait_ge(S["ssum_done"], 2 * n + 6)
                                nc.gpsimd.tensor_tensor(ssum[:, :], ssum[:, :], mhalf[:, :].to_broadcast([P, 2 * H]), ALU.pow).then_inc(S["rq_done"], 1)
                                pool.wait_ge(S["rq_done"], 2 * n + 5)
                                nc.gpsimd.tensor_tensor(rq[:, :], ssum[:, :], gq[:, :], ALU.mult).then_inc(S["rq_done"], 1)
                            if F:
                                pool.wait_ge(S["var_new"], n - 1)
                                nc.gpsimd.tensor_tensor(rstd_all[:, bass.ds(b - 2, 1)], var_all[:, bass.ds(b - 2, 1)], mhalf[:, :], ALU.pow).then_inc(S["rstd_new"], 1)

                        drive(nc.gpsimd, step)
                        pool.wait_ge(S["rstd_new"], base + B)

                    @block.vector
                    def _(dve):
                        def step(b, u, A=True, B_=True, C=True, D_=True, F=True, N=True):
                            n = b + base
                            w = 1 - u

                            def row_max(half):
                                dve.wait_ge(S["s_mm"], 2 * n + 1 + half)
                                for c in range(2):
                                    mm = nc.vector.tensor_reduce(rmax[:, 8 * half + c:8 * half + 8:2], bank_hs[half][c][:, :].rearrange("p (h t) -> p h t", t=T), AX.X, ALU.max)
                                mm.then_inc(S["max_done"], 1)
                            if C:
                                row_max(0)
                            if A:
                                dve.wait_ge(S["ht_mm"], n + 3)
                                if B_:
                                    dve.wait_ge(S["lo_done"], 2 * n + 4)
                                nc.vector.tensor_scalar(ht[:, 0, :], b_t[:, 0:T], mod[:, l, 1, bass.ds(b + 2, 1)], mod[:, l, 0, bass.ds(b + 2, 1)], ALU.mult, ALU.add).then_inc(S["ht_done"], 1)
                                nc.vector.tensor_scalar(ht[:, 1, :], b_t[:, T:2 * T], modt[:, l, 1, bass.ds(b + 2, 1)], modt[:, l, 0, bass.ds(b + 2, 1)], ALU.mult, ALU.add).then_inc(S["ht_done"], 1)
                            if B_ and rms:
                                dve.wait_ge(S["rq_done"], 2 * n + 4)
                                nc.vector.tensor_tensor(qk[:, :].rearrange("p (g d) -> p g d", d=DH), qkvs[:, w, 0:2 * D].rearrange("p (g d) -> p g d", d=DH),
                                                        rq[:, :].unsqueeze(2).to_broadcast([P, 2 * H, DH]), ALU.mult).then_inc(S["qkn_done"], 1)
                            if C:
                                row_max(1)
                            if B_:
                                dve.wait_ge(S["high_done"], 2 * n + 4)
                                src = qk[:, :] if rms else qkvs[:, w, 0:2 * D]
                                pieces = stack[:, w:3:2 - w, :, 0:PIECES * DH].rearrange("p s h (c d) -> p s h c d", d=DH)
                                nc.vector.tensor_tensor(rest[:, :].rearrange("p (s h d) -> p s h d", s=2, d=DH), src.rearrange("p (s h d) -> p s h d", s=2, d=DH),
                                                        pieces[:, :, :, 1, :], ALU.subtract).then_inc(S["rest_done"], 1)
                            if C:
                                dve.wait_ge(S["max_done"], 2 * n + 2)
                                c0 = PIECES * DH
                                nc.vector.tensor_scalar(stack[:, u, :, c0], rmax[:, :], -1.0, None, ALU.mult).then_inc(S["neg_done"], 1)
                                dve.wait_ge(S["neg_done"], 2 * n + 1)
                                nc.vector.scalar_tensor_tensor(out=stack[:, u, :, c0 + 1], in0=rmax[:, :], scalar=-1.0, in1=stack[:, u, :, c0], op0=ALU.mult, op1=ALU.subtract).then_inc(S["neg_done"], 1)
                            if A and rms:
                                dve.wait_ge(S["square_done"], n + 3)
                                nc.vector.tensor_reduce(ssum[:, :], sq[:, :].rearrange("p (g d) -> p g d", d=DH), AX.X, ALU.add).then_inc(S["ssum_done"], 1)
                                dve.wait_ge(S["ssum_done"], 2 * n + 5)
                                nc.vector.tensor_scalar(ssum[:, :], ssum[:, :], 1e-24, None, ALU.max).then_inc(S["ssum_done"], 1)
                            if C:
                                dve.wait_ge(S["q2_mm"], n + 1)
                                nc.vector.tensor_copy(qs[:, u, :, :], t16).then_inc(S["q2_done"], 1)
                            if D_:
                                heads = b_ov[:, :].rearrange("p (h s) -> p h s", s=32)
                                dve.wait_ge(S["back_mm"], n)
                                nc.vector.reciprocal(rsum[:, :], heads[:, :, DH]).then_inc(S["rsum_done"], 1)
                                dve.wait_ge(S["rsum_done"], n)
                                nc.vector.tensor_tensor(at[:, w, :].rearrange("p (h d) -> p h d", d=DH), heads[:, :, 0:DH], rsum[:, :].unsqueeze(2).to_broadcast([P, H, DH]), ALU.mult).then_inc(S["at_done"], 1)
                            if B_:
                                dve.wait_ge(S["qs_mm"], n + 2)
                                nc.vector.tensor_copy(qs[:, w, :, :], tp16).then_inc(S["qs_done"], 1)
                            if N:
                                if not (isinstance(b, int) and b < -1):
                                    dve.wait_ge(S["ht_mm"], n + 2)
                                for dst, src in ((hn[:, w, :], x_all[:, b + 3, 0:P]),
                                                 (hn_st[:, w, :, 0:DT], x_all[:, b + 3, P:D].unsqueeze(1).to_broadcast([P, 4, DT]))):
                                    if rms:
                                        nc.vector.tensor_scalar(dst, src, rstd_all[:, bass.ds(b + 3, 1)], gain[:, 0:1], ALU.mult, ALU.mult).then_inc(S["hn_done"], 1)
                                    else:
                                        nc.vector.tensor_scalar(dst, src, mean_all[:, bass.ds(b + 3, 1)], rstd_all[:, bass.ds(b + 3, 1)], ALU.subtract, ALU.mult).then_inc(S["hn_done"], 1)
                            if F:
                                dve.wait_ge(S["proj_mm"], n - 1)
                                nc.vector.tensor_tensor(upd[:, u, :], b_mm[:, 0:D], gate_all[:, 0, b - 2, :], ALU.mult).then_inc(S["upd_done"], 1)
                                dve.wait_ge(S["upd_done"], n - 1)
                                nc.vector.tensor_tensor(x_all[:, b - 2, :], x_all[:, b - 2, :], upd[:, u, :], ALU.add).then_inc(S["x_new"], 1)
                                dve.wait_ge(ones_ready, 1)
                                dve.wait_ge(S["x_new"], n - 1)
                                nc.vector.bn_stats(stats[:, u, :], x_all[:, b - 2, :]).then_inc(S["stat_done"], 1)
                                dve.wait_ge(ones_ready, 1)
                                dve.wait_ge(S["stat_done"], n - 1)
                                nc.vector.bn_aggr(aggr[:, u, :], stats[:, u, :]).then_inc(S["aggr_done"], 1)
                                dve.wait_ge(S["aggr_done"], n - 1)
                                variance(dve, rms, aggr[:, u], b - 2, S["var_new"], S["ms_done"], b - 2)

                        drive(nc.vector, step)
                        dve.wait_ge(S["var_new"], base + B)

    
        names = "set hn_done h_mm h_done hi_done lo_done fc1_mm gelu_done fc2_mm upd_done x_new ".split()
        plain_sems = {k: sem("m_" + k) for k in names + "stat_done aggr_done var_new rstd_new ms_done".split()}
        moe_sems = {k: sem("e_" + k) for k in names + "lg_mm lg_done route exp_done sel_done wts_done gated stored".split()}

        def mlp(l):
            experts = E if l == 2 else 1
            phase = 2 * l + 1
            rms = l == 1
            gelu = ACT.Gelu if l == 0 else ACT.Gelu_apprx_tanh
            off_gate = QKV_W[l] + D
            off2 = off_gate + GATE_W[l]
            off1 = SPLIT_QKV_W[l]
            groups = B // G
            with ExitStack() as c:
                def tsb(name, shape, dt=F32):
                    return c.enter_context(nc.sbuf_tensor(f"m{l}_{name}", shape, dt))

                hn = tsb("hn", [P, G, P])
                hn_st = tsb("hn_st", [P, G, 4, 32])
                h = tsb("h", [P, 2, G * T])
                hi = tsb("hi", [P, 2, 2, G * T], F32R)
                lo = tsb("lo", [P, 2, G * T], F32R)
                hid = tsb("hid", [P, 2, MT, G * T])
                upd = tsb("upd", [P, G, D])
                st = tsb("st", [P, G, 6])
                ag = tsb("ag", [P, G, 2])
                lg = tsb("lg", [P, G, E])
                cmp = tsb("cmp", [P, G, E, E])
                cmp2 = tsb("cmp2", [P, G, E, E])
                sel = tsb("sel", [P, G, E])
                wts = tsb("wts", [P, 2, G, E])
                tops = tsb("tops", [P, G])
                below = tsb("below", [P, E, E])
                S = moe_sems if l == 2 else plain_sems
                base = groups if l == 1 else 0
                b_h0, b_h1, b_lg = bank[0], bank[1], bank[1]
                b_fc1 = [bank[2], bank[3], bank[4], bank[5]]
                b_fc2 = [bank[6], bank[7]]

                def drive(eng, step):
                    step(-2, 0, front=False, products=False, stats_of_last=False)
                    step(-1, 1, products=False, stats_of_last=False)
                    step(0, 0, stats_of_last=False)
                    with eng.Fori(0, (groups - 4) // 2) as i:
                        step(i * 2 + 1, 1)
                        step(i * 2 + 2, 0)
                    step(groups - 3, 1)
                    step(groups - 2, 0, second=False)
                    step(groups - 1, 1, second=False, front=False)
                    step(groups, 0, second=False, front=False, products=False)

                def bank_of(u, e, m):
                    return b_fc1[(u * experts * MT + e * MT + m) % 4 if (2 * experts * MT) % 4 == 0 else (u * 2 + m) % 4]

                def width(m):
                    return P if m < MT - 1 else HL

                with nc.Block() as block:
                    @block.tensor
                    def _(pe):
                        def step(g, u, second=True, front=True, products=True, stats_of_last=True):
                            n = g + base
                            def fc1(e):
                                for m in range(MT):
                                    t_done = (n * experts + e) * MT + m
                                    if not isinstance(n, int) or t_done >= 4:
                                        pe.wait_ge(S["set"], 2)
                                        pe.wait_ge(S["gelu_done"], t_done - 3)
                                    o = off1 + e * HID + m * P
                                    dst = bank_of(u, e, m)[0:width(m), :]
                                    c = slice(o, o + width(m))
                                    nc.tensor.matmul(dst, w_hi[l][:, c], hi[:, u, 0, :], start=True, stop=False)
                                    nc.tensor.matmul(dst, w_lo[l][:, c], hi[:, u, 0, :], start=False, stop=False)
                                    nc.tensor.matmul(dst, w_hi[l][:, c], lo[:, u, :], start=False, stop=False)
                                    nc.tensor.matmul(dst, w_st[l][:, c], hi[:, u, 1, :], start=False, stop=True).then_inc(S["fc1_mm"], 1)

                            def fc2(e):
                                pe.wait_ge(S["gelu_done"], (n * experts + e + 1) * MT)
                                if not isinstance(n, int) or n or e:
                                    pe.wait_ge(S["upd_done"], (n * experts + e) * 2)
                                for s in range(G):
                                    for m in range(MT):
                                        k = P if m < MT - 1 else HL + 1
                                        wt = w_main[l][:, off2 + (e * 4 + m) * D:off2 + (e * 4 + m + 1) * D] if m < MT - 1 else w_last[l][:, e * D:(e + 1) * D]
                                        mm = nc.tensor.matmul(b_fc2[s // 2][:, (s % 2) * D:(s % 2 + 1) * D], hid[0:k, e % 2 if experts > 1 else u, m, s * T:(s + 1) * T], wt,
                                                              start=(m == 0), stop=(m == MT - 1))
                                    if s % 2:
                                        mm.then_inc(S["fc2_mm"], 1)

                            def transposes():
                                pe.wait_ge(S["hn_done"], n * 2 * G + 6 * G)
                                if front:
                                    pe.wait_ge(S["h_done"], n * 2 * G + 4 * G)
                                for s in range(G):
                                    nc.tensor.transpose(b_h0[:, s * T:(s + 1) * T], hn[:, s, 0:P], ident[:, :])
                                for s in range(G):
                                    if s == 0 and l == 2 and front:
                                        pe.wait_ge(S["lg_done"], n + 2)
                                    mm = nc.tensor.transpose(b_h1[:, s * T:(s + 1) * T], hn_st[:, s, :, :].rearrange("p c f -> p (c f)"), ident[:, :])
                                mm.then_inc(S["h_mm"], 1)

                            def logits():
                                pe.wait_ge(S["set"], 2)
                                pe.wait_ge(S["h_done"], n * 2 * G + 4 * G)
                                for s in range(G):
                                    nc.tensor.matmul(b_lg[:, s * E:(s + 1) * E], h[:, 0, s * T:(s + 1) * T], w_main[2][:, off_gate:off2], start=True, stop=False)
                                    mm = nc.tensor.matmul(b_lg[:, s * E:(s + 1) * E], h[0:DT + 1, 1, s * T:(s + 1) * T], w_tail[2][:, off_gate:off2], start=False, stop=True)
                                mm.then_inc(S["lg_mm"], 1)

                            if products:
                                pe.wait_ge(S["lo_done"], 2 * n + 2)
                                fc1(0)
                                if experts > 1:
                                    fc1(1)
                            if front and l == 2:
                                logits()
                            if products and experts > 1:
                                fc2(0)
                                fc1(2)
                            if second:
                                transposes()
                            if products and experts > 1:
                                fc2(1)
                                fc1(3)
                                fc2(2)
                            if products:
                                fc2(experts - 1)

                        drive(nc.tensor, step)

                    @block.scalar
                    def _(act):
                        def step(g, u, second=True, front=True, products=True, stats_of_last=True):
                            n = g + base
                            w = 1 - u

                            def high_parts():
                                act.wait_ge(S["h_done"], n * 2 * G + 4 * G)
                                nc.scalar.copy(hi[:, w, :, :], h[:, :, :]).then_inc(S["hi_done"], 1)

                            def routes():
                                act.wait_ge(S["route"], n + 2)
                                nc.scalar.activation(wts[:, w, :, :], lg[:, :, :], ACT.Exp).then_inc(S["exp_done"], 1)

                            if products:
                                for e in range(experts):
                                    for m in range(MT):
                                        tile = (n * experts + e) * MT + m
                                        if m == 0:
                                            if experts > 1 and (not isinstance(n, int) or n * experts + e >= 2):
                                                act.wait_ge(S["set"], 2)
                                                act.wait_ge(S["fc2_mm"], (n * experts + e) * 2 - 2)
                                            elif experts == 1 and (not isinstance(n, int) or n >= 1):
                                                act.wait_ge(S["fc2_mm"], n * 2)
                                        act.wait_ge(S["fc1_mm"], tile + 1)
                                        nc.scalar.activation(hid[0:width(m), e % 2 if experts > 1 else u, m, :], bank_of(u, e, m)[0:width(m), :], gelu).then_inc(S["gelu_done"], 1)
                                    if front and e == 0:
                                        high_parts()
                                    if e == 1 and front:
                                        routes()
                            elif front:
                                high_parts()
                                if l == 2:
                                    routes()

                        drive(nc.scalar, step)

                    @block.gpsimd
                    def _(pool):
                        def step(g, u, second=True, front=True, products=True, stats_of_last=True):
                            n = g + base
                            w = 1 - u
                            if front:
                                pool.wait_ge(S["hi_done"], n + 2)
                                nc.gpsimd.tensor_tensor(lo[:, w, :], h[:, 0, :], hi[:, w, 0, :], ALU.subtract).then_inc(S["lo_done"], 1)
                                pool.wait_ge(S["lo_done"], 2 * n + 3)
                                low = slice(2 * 32, P)
                                nc.gpsimd.tensor_tensor(hi[low, w, 1, :], h[low, 1, :], hi[low, w, 1, :], ALU.subtract).then_inc(S["lo_done"], 1)
                                pool.wait_ge(S["lo_done"], 2 * n + 4)
                            if stats_of_last and l < 2:
                                pool.wait_ge(S["var_new"], n * G)
                                nc.gpsimd.tensor_tensor(rstd_all[:, bass.ds((g - 1) * G, G)], var_all[:, bass.ds((g - 1) * G, G)], mhalf[:, :].to_broadcast([P, G]), ALU.pow).then_inc(S["rstd_new"], 1)

                        drive(nc.gpsimd, step)
                        if l < 2:
                            pool.wait_ge(S["rstd_new"], base + groups)

                    @block.sync
                    def _(sp):
                        if l < 2:
                            load_gates(sp, phase + 1)
                        else:
                            def step(g, u, second=True, front=True, products=True, stats_of_last=True):
                                n = g + base
                                if products:
                                    sp.wait_ge(S["x_new"], n + 1)
                                    sp.dma_start(t["out"][bass.ds(g * G, G)].rearrange("b t d -> t b d"), x_all[:, bass.ds(g * G, G), :]).then_inc(S["stored"], 16)

                            drive(nc.sync, step)
                            sp.wait_ge(S["stored"], groups * 16)

                    @block.vector
                    def _(dve):
                        def step(g, u, second=True, front=True, products=True, stats_of_last=True):
                            n = g + base
                            w = 1 - u
                            def take(e):
                                for half in range(2):
                                    dve.wait_ge(S["fc2_mm"], (n * experts + e) * 2 + 1 + half)
                                    if experts == 1:
                                        nc.vector.tensor_tensor(upd[:, 2 * half:2 * half + 2, :], b_fc2[half][:, 0:2 * D].rearrange("p (s d) -> p s d", d=D),
                                                                gate_all[:, 1, bass.ds(g * G + 2 * half, 2), :], ALU.mult).then_inc(S["upd_done"], 1)
                                        continue
                                    for s in range(2 * half, 2 * half + 2):
                                        src = b_fc2[half][:, (s % 2) * D:(s % 2 + 1) * D]
                                        if e == 0:
                                            if s == 0:
                                                dve.wait_ge(S["wts_done"], n + 1)
                                                if not isinstance(g, int) or g:
                                                    dve.wait_ge(S["x_new"], n)
                                            mm = nc.vector.tensor_scalar(upd[:, s, :], src, wts[:, u, s, e:e + 1], None, ALU.mult)
                                        else:
                                            if s == 2 * half:
                                                dve.wait_ge(S["upd_done"], (n * experts + e) * 2 + half - 1)
                                            mm = nc.vector.scalar_tensor_tensor(out=upd[:, s, :], in0=src, scalar=wts[:, u, s, e:e + 1], in1=upd[:, s, :], op0=ALU.mult, op1=ALU.add)
                                    mm.then_inc(S["upd_done"], 1)

                            if front:
                                dve.wait_ge(S["h_mm"], n + 2)
                                if products:
                                    dve.wait_ge(S["lo_done"], 2 * n + 2)
                                    if l == 2:
                                        dve.wait_ge(S["lg_mm"], n + 1)
                                for s in range(G):
                                    q = g * G + G + s
                                    nc.vector.tensor_scalar(h[:, 0, s * T:(s + 1) * T], b_h0[:, s * T:(s + 1) * T], mod[:, l, 3, bass.ds(q, 1)], mod[:, l, 2, bass.ds(q, 1)], ALU.mult, ALU.add).then_inc(S["h_done"], 1)
                                for s in range(G):
                                    q = g * G + G + s
                                    nc.vector.tensor_scalar(h[:, 1, s * T:(s + 1) * T], b_h1[:, s * T:(s + 1) * T], modt[:, l, 3, bass.ds(q, 1)], modt[:, l, 2, bass.ds(q, 1)], ALU.mult, ALU.add).then_inc(S["h_done"], 1)
                            if second:
                                for s in range(G):
                                    q = g * G + 2 * G + s
                                    for dst, src in ((hn[:, s, :], x_all[:, q, 0:P]),
                                                     (hn_st[:, s, :, 0:DT], x_all[:, q, P:D].unsqueeze(1).to_broadcast([P, 4, DT]))):
                                        if l == 1:
                                            nc.vector.tensor_scalar(dst, src, rstd_all[:, bass.ds(q, 1)], gain[:, 1:2], ALU.mult, ALU.mult).then_inc(S["hn_done"], 1)
                                        else:
                                            nc.vector.tensor_scalar(dst, src, mean_all[:, bass.ds(q, 1)], rstd_all[:, bass.ds(q, 1)], ALU.subtract, ALU.mult).then_inc(S["hn_done"], 1)

                            if front and l == 2:
                                dve.wait_ge(S["lg_mm"], n + 2)
                                nc.vector.tensor_copy(lg[:, :, :], b_lg[:, 0:G * E].rearrange("p (s e) -> p s e", e=E)).then_inc(S["lg_done"], 1)
                                dve.wait_ge(S["lg_done"], n + 2)
                                other = lg[:, :, :].unsqueeze(2).to_broadcast([P, G, E, E])
                                own = lg[:, :, :].unsqueeze(3).to_broadcast([P, G, E, E])
                                step_of = (n + 1) * 9
                                nc.vector.tensor_tensor(cmp[:, :, :, :], other, own, ALU.is_gt).then_inc(S["sel_done"], 1)
                                nc.vector.tensor_tensor(cmp2[:, :, :, :], other, own, ALU.is_equal).then_inc(S["sel_done"], 1)
                                nc.vector.tensor_reduce(tops[:, :], lg[:, :, :], AX.X, ALU.max).then_inc(S["sel_done"], 1)
                                dve.wait_ge(S["sel_done"], step_of + 3)
                                nc.vector.tensor_tensor(cmp2[:, :, :, :], cmp2[:, :, :, :], below[:, :, :].unsqueeze(1).to_broadcast([P, G, E, E]), ALU.mult).then_inc(S["sel_done"], 1)
                                nc.vector.tensor_tensor(lg[:, :, :], lg[:, :, :], tops[:, :].unsqueeze(2).to_broadcast([P, G, E]), ALU.subtract).then_inc(S["route"], 1)
                                dve.wait_ge(S["sel_done"], step_of + 4)
                                nc.vector.tensor_tensor(cmp[:, :, :, :], cmp[:, :, :, :], cmp2[:, :, :, :], ALU.add).then_inc(S["sel_done"], 1)
                                dve.wait_ge(S["sel_done"], step_of + 5)
                                nc.vector.tensor_reduce(sel[:, :, :], cmp[:, :, :, :], AX.X, ALU.add).then_inc(S["sel_done"], 1)
                                dve.wait_ge(S["sel_done"], step_of + 6)
                                dve.wait_ge(S["exp_done"], n + 2)
                                nc.vector.scalar_tensor_tensor(out=wts[:, w, :, :], in0=sel[:, :, :], scalar=1.5, in1=wts[:, w, :, :], op0=ALU.is_lt, op1=ALU.mult).then_inc(S["sel_done"], 1)
                                dve.wait_ge(S["sel_done"], step_of + 7)
                                nc.vector.tensor_reduce(tops[:, :], wts[:, w, :, :], AX.X, ALU.add).then_inc(S["sel_done"], 1)
                                dve.wait_ge(S["sel_done"], step_of + 8)
                                nc.vector.reciprocal(tops[:, :], tops[:, :]).then_inc(S["sel_done"], 1)
                                dve.wait_ge(S["sel_done"], step_of + 9)
                                nc.vector.tensor_tensor(wts[:, w, :, :], wts[:, w, :, :], tops[:, :].unsqueeze(2).to_broadcast([P, G, E]), ALU.mult).then_inc(S["wts_done"], 1)
                            if stats_of_last and l < 2:
                                dve.wait_ge(ones_ready, 1)
                                dve.wait_ge(S["x_new"], n)
                                for s in range(G):
                                    mm = nc.vector.bn_stats(st[:, s, :], x_all[:, (g - 1) * G + s, :])
                                mm.then_inc(S["stat_done"], 1)
                                dve.wait_ge(ones_ready, 1)
                                dve.wait_ge(S["stat_done"], n)
                                for s in range(G):
                                    mm = nc.vector.bn_aggr(ag[:, s, :], st[:, s, :])
                                mm.then_inc(S["aggr_done"], 1)
                                dve.wait_ge(S["aggr_done"], n)
                                for s in range(G):
                                    variance(dve, l == 0, ag[:, s], (g - 1) * G + s, S["var_new"], S.get("ms_done"), (g - 1) * G + s)
                            if products:
                                for e in range(experts - 1):
                                    take(e)
                            if products:
                                take(experts - 1)
                                xs = x_all[:, bass.ds(g * G, G), :]
                                dve.wait_ge(S["upd_done"], (n * experts + experts) * 2)
                                if experts > 1:
                                    nc.vector.tensor_tensor(upd[:, :, :], upd[:, :, :], gate_all[:, 1, bass.ds(g * G, G), :], ALU.mult).then_inc(S["gated"], 1)
                                    dve.wait_ge(S["gated"], n + 1)
                                nc.vector.tensor_tensor(xs, xs, upd[:, :, :], ALU.add).then_inc(S["x_new"], 1)
                        nc.vector.memset(hn_st[:, :, :, :], 0.0).then_inc(S["set"], 1)
                        nc.vector.memset(hid[:, :, MT - 1, :], 1.0).then_inc(S["set"], 1)
                        if l == 2:
                            nc.vector.memset(below[:, :, :], 0.0).then_inc(S["set"], 1)
                            dve.wait_ge(S["set"], 3)
                            for e in range(1, E):
                                nc.vector.memset(below[:, e, 0:e], 1.0).then_inc(S["set"], 1)
                            dve.wait_ge(S["set"], 3 + E - 1)
                        else:
                            dve.wait_ge(S["set"], 2 + 2 * (l == 1))
                        drive(nc.vector, step)
                        if l == 2:
                            dve.wait_ge(S["x_new"], groups)
                        else:
                            dve.wait_ge(S["var_new"], base * G + B)

        mlp(0)
        attention(1)
        mlp(1)
        attention(2)
        mlp(2)


def lay_out(x):
    def wb(w, b):
        return np.concatenate([w, b[None]], 0)

    def fc2(w, b):
        main = w[:4 * P].reshape(4, P, D).transpose(1, 0, 2).reshape(P, 4 * D)
        return main, np.concatenate([w[4 * P:], b[None]], 0)

    def four_times(m, axis):
        out = np.zeros((4, 32) + m.shape[1:] if axis == 0 else m.shape[:1] + (4, 32), np.float32)
        if axis == 0:
            out[:, :m.shape[0]] = m
            return out.reshape((P,) + m.shape[1:])
        out[:, :, :m.shape[1]] = m[:, None]
        return out.reshape(m.shape[0], P)

    a = {"x": x["x"], "cond": x["cond_1152"], "pt": x["L0_cond_P"].T}
    iu, ju = np.triu_indices(R, 1)
    skew = np.zeros((D + 1, R, R), np.float32)
    for i, j in ((iu, ju), (ju, iu)):
        skew[:D, i, j] = x["L0_cond_W"].T
        skew[D, i, j] = x["L0_cond_b"]
    a["skew"] = skew.reshape(D + 1, R * R)
    sign = np.sign(np.arange(R)[None, :] - np.arange(R)[:, None]).astype(np.float32)
    a["sign"] = np.concatenate([sign, sign], 0)
    a["ident"] = np.eye(P, dtype=np.float32)
    ada = a["ada"] = np.stack([wb(x["L1_cond_ada_w"], x["L1_cond_ada_b"]), wb(x["L2_cond_ada_w"].T, x["L2_cond_ada_b"]),
                         wb(x["L3_cond_w_adaln"], x["L3_cond_b_adaln"])])
    a["adat"] = np.zeros((L, 4, D + 1, P), np.float32)
    for l in range(L):
        for w, col in enumerate((0, 1, 3, 4)):
            last = np.zeros((D + 1, DT + 1), np.float32)
            last[:, :DT] = ada[l][:, col * D + P:(col + 1) * D]
            last[D, DT] = 1 - w % 2
            a["adat"][l, w] = four_times(last, 1)
    a["gains"] = np.concatenate([x["L2_cond_g1"], x["L2_cond_g2"], x["L2_cond_qg"], x["L2_cond_kg"]])
    for l, (qkv, proj, fc1, f2) in enumerate((
        (wb(x["L1_cond_qkv_w"], x["L1_cond_qkv_b"]), wb(x["L1_cond_proj_w"], x["L1_cond_proj_b"]),
         [wb(x["L1_cond_fc1_w"], x["L1_cond_fc1_b"])], [fc2(x["L1_cond_fc2_w"], x["L1_cond_fc2_b"])]),
        (wb(x["L2_cond_qkv_w"].T, x["L2_cond_qkv_b"]), wb(x["L2_cond_proj_w"].T, x["L2_cond_proj_b"]),
         [wb(x["L2_cond_fc1_w"].T, x["L2_cond_fc1_b"])], [fc2(x["L2_cond_fc2_w"].T, x["L2_cond_fc2_b"])]),
        (wb(x["L3_cond_w_qkv"], x["L3_cond_b_qkv"]), wb(x["L3_cond_w_proj"], x["L3_cond_b_proj"]),
         [wb(x["L3_cond_w_gate"], np.zeros(E, np.float32))] + [wb(x["L3_cond_w1"][e], x["L3_cond_b1"][e]) for e in range(E)],
         [fc2(x["L3_cond_w2"][e], x["L3_cond_b2"][e]) for e in range(E)]),
    )):
        plain = np.concatenate(([qkv] if l == 0 else []) + [proj] + fc1[:-EXPERTS[l]], 1)
        split = np.concatenate(([] if l == 0 else [qkv]) + fc1[-EXPERTS[l]:], 1)
        a[f"main{l}"] = np.concatenate([plain[:P]] + [m for m, _ in f2], 1)
        a[f"tail{l}"] = plain[P:]
        a[f"split{l}"] = split[:P]
        a[f"stack{l}"] = four_times(split[P:], 0)
        a[f"last{l}"] = np.concatenate([m for _, m in f2], 1)
    return {k: np.ascontiguousarray(v) for k, v in a.items()}


def kernel(**inputs):
    import concourse.bacc as bacc
    from concourse.bass_utils import run_bass_kernel_spmd

    nc = bacc.Bacc("TRN2", target_bir_lowering=False, num_devices=1)
    arrays = lay_out({k: np.asarray(v) for k, v in inputs.items()})
    tensors = {k: nc.dram_tensor("in_" + k, a.shape, mybir.dt.from_np(a.dtype), kind="ExternalInput").ap() for k, a in arrays.items()}
    tensors["out"] = nc.dram_tensor("out", [B, T, D], F32, kind="ExternalOutput").ap()
    program(nc, tensors)
    r = run_bass_kernel_spmd(nc, [{"in_" + k: a for k, a in arrays.items()}], core_ids=[0])
    return r.results[0]["out"]
```
